# Optimizing a Trainium2 kernel written in Bass

```python
import numpy as np
import jax
import jax.numpy as jnp

def _softmax(x, axis=-1):
    return jax.nn.softmax(x, axis=axis)

def _gelu(x):
    return jax.nn.gelu(x, approximate=True)

def _silu(x):
    return jax.nn.silu(x)

def _sigmoid(x):
    return jax.nn.sigmoid(x)

def _layernorm(x, axis=-1, eps=1e-05):
    m = jnp.mean(x, axis=axis, keepdims=True)
    v = jnp.var(x, axis=axis, keepdims=True)
    return (x - m) / jnp.sqrt(v + eps)

def _scatter_add(tgt, idx, src, axis=0):
    return tgt.at[idx].add(src)

def _segment_sum(src, seg, n):
    return jax.ops.segment_sum(src, seg, n)
kernel_name = 'mk_macaron_d2_jaxref_r8_69f16f'

def setup_inputs(seed: int=0):
    np.random.seed(seed)
    _w = jnp.asarray

    def _L0_attn_setup():
        import jax, jax.numpy as jnp
        import numpy as np
        B, T, DIM, H = (2, 256, 128, 16)
        HD = DIM // H

        def _custom_softmax(a):
            a = jnp.clip(a, -100.0, 100.0)
            m = jnp.max(a, axis=-1, keepdims=True)
            e = jnp.exp(a - m)
            p = e / (jnp.sum(e, axis=-1, keepdims=True) + 1e-06)
            p = p + 1e-08
            return p / jnp.sum(p, axis=-1, keepdims=True)
        key = jax.random.key(seed)
        k1, k2, k3 = jax.random.split(key, 3)
        x = jax.random.normal(k1, (B, T, DIM), dtype=jnp.float32)
        w_qkv = jax.random.normal(k2, (3 * DIM, DIM), dtype=jnp.float32) / np.sqrt(DIM)
        w_proj = jax.random.normal(k3, (DIM, DIM), dtype=jnp.float32) / np.sqrt(DIM)
        return {'x': x, 'w_qkv': w_qkv, 'w_proj': w_proj}
    _L0_attn_in = _L0_attn_setup()

    def _L0_ffn_setup():
        import jax, jax.numpy as jnp
        import numpy as np
        DIM = 128

        def _reference_tuple_inner(x, W_r, W_k, W_v, mu_r, mu_k):
            B, T, C = x.shape
            x_prev = jnp.concatenate([jnp.zeros((B, 1, C), x.dtype), x[:, :-1, :]], axis=1)
            xr = mu_r * x + (1.0 - mu_r) * x_prev
            xk = mu_k * x + (1.0 - mu_k) * x_prev
            r = jax.nn.sigmoid(jnp.einsum('btc,dc->btd', xr, W_r))
            k = jnp.einsum('btc,dc->btd', xk, W_k)
            k_act = jnp.square(jax.nn.relu(k))
            out = r * jnp.einsum('btc,dc->btd', k_act, W_v)
            new_state = x[:, -1, :]
            return (out, new_state)
        key = jax.random.key(seed)
        ks = jax.random.split(key, 6)
        B, T, C = (8, 256, DIM)
        x = jax.random.normal(ks[0], (B, T, C), dtype=jnp.float32)
        s = 1.0 / np.sqrt(C)
        W_r = jax.random.uniform(ks[1], (C, C), jnp.float32, -s, s)
        W_k = jax.random.uniform(ks[2], (C, C), jnp.float32, -s, s)
        W_v = jax.random.uniform(ks[3], (C, C), jnp.float32, -s, s)
        mu_r = jax.random.uniform(ks[4], (C,), jnp.float32)
        mu_k = jax.random.uniform(ks[5], (C,), jnp.float32)
        return {'x': x, 'W_r': W_r, 'W_k': W_k, 'W_v': W_v, 'mu_r': mu_r, 'mu_k': mu_k}
    _L0_ffn_in = _L0_ffn_setup()

    def _L1_attn_setup():
        import jax, jax.numpy as jnp
        import numpy as np
        DIMS = 128
        HEAD = 16
        HD = DIMS // HEAD
        MAX_ITER = 3
        MIN_SIZE = 64
        MAX_SIZE = 256
        UP_WIN, DOWN_WIN = (1.1, 0.9)
        UP_DIFF, DOWN_DIFF = (0.05, 0.001)
        B, T = (2, 128)

        def _ln(x, w, eps=1e-05):
            m = jnp.mean(x, axis=-1, keepdims=True)
            v = jnp.var(x, axis=-1, keepdims=True)
            return (x - m) * jax.lax.rsqrt(v + eps) * w

        def _focus(x, Wq, bq, Wk, Wv, bv, Wo, bo, lna_w, lnb_w, lnc_w, lnd_w, lq_w, lq_b, lk_w, lk_b, lv_w, lv_b, threshold, temp_base, factor):
            b, t, d = x.shape
            q = _ln(x, lna_w) @ Wq.T + bq
            kk = _ln(x, lnb_w) @ Wk.T
            v = _ln(x, lnb_w) @ Wv.T + bv
            sc = HD ** (-0.25)

            def _shape(u):
                return u.reshape(b, t, HEAD, HD).transpose(0, 2, 1, 3)
            q_full = _shape(q * sc)
            k_full = _shape(kk * sc)
            v_full = _shape(v)
            thr = jax.lax.stop_gradient(threshold)
            fac = jax.lax.stop_gradient(factor)
            t0 = jax.lax.stop_gradient(temp_base)
            cw0 = jnp.int32(max(min(t, MAX_SIZE), MIN_SIZE))
            inv_sqrt_e = jnp.float32(1.0 / np.sqrt(HD))
            pos = jnp.arange(t)

            def step(carry, i):
                qcur, prev, attn, cw, temp, done = carry
                qp = qcur @ lq_w.T + lq_b
                kp = k_full @ lk_w.T + lk_b
                vp = v_full @ lv_w.T + lv_b
                sq = _ln(qp, lnc_w)
                sk = _ln(kp, lnd_w)
                tscale = jnp.where(temp > 0, jax.lax.rsqrt(temp), jnp.float32(1.0))
                sq = sq * tscale
                scores = jnp.einsum('bhqd,bhkd->bhqk', sq, sk) * inv_sqrt_e
                in_win = pos < cw
                scores = jnp.where(in_win[None, None, None, :], scores, -jnp.inf)
                probs = jax.nn.softmax(scores, axis=-1)
                out = jnp.einsum('bhqk,bhkd->bhqd', probs, vp)
                iter_out = jnp.where(in_win[None, None, :, None], out, 0.0)
                diff = jnp.mean(jnp.abs(iter_out - prev))
                converged = (diff < thr + fac * diff) & (i > 0)
                upd = ~done & ~converged
                new_done = done | converged
                attn_n = jnp.where(done, attn, iter_out)
                prev_n = jnp.where(upd, iter_out, prev)
                qcur_n = jnp.where(upd, qcur + iter_out, qcur)
                up = (cw.astype(jnp.float32) * UP_WIN).astype(jnp.int32)
                down = (cw.astype(jnp.float32) * DOWN_WIN).astype(jnp.int32)
                nw = jnp.where(diff > UP_DIFF, up, jnp.where((diff < DOWN_DIFF) & (cw > MIN_SIZE), down, cw))
                nw = jnp.clip(nw, MIN_SIZE, t)
                cw_n = jnp.where(upd, nw, cw)
                temp_n = jnp.where(upd, temp + jnp.float32(0.005), temp)
                return ((qcur_n, prev_n, attn_n, cw_n, temp_n, new_done), None)
            zeros = jnp.zeros_like(q_full)
            carry0 = (q_full, zeros, zeros, cw0, t0, jnp.array(False))
            (_, _, attn_out, _, _, _), _ = jax.lax.scan(step, carry0, jnp.arange(MAX_ITER))
            output = attn_out.transpose(0, 2, 1, 3).reshape(b, t, d)
            return output @ Wo.T + bo
        key = jax.random.key(seed)
        ks = jax.random.split(key, 12)

        def lin_w(k, o, i):
            return (jax.random.normal(k, (o, i), dtype=jnp.float32) / np.sqrt(i)).astype(jnp.float32)
        return {'x': jax.random.normal(ks[0], (B, T, DIMS), dtype=jnp.float32), 'Wq': lin_w(ks[1], DIMS, DIMS), 'bq': jnp.zeros((DIMS,), jnp.float32), 'Wk': lin_w(ks[2], DIMS, DIMS), 'Wv': lin_w(ks[3], DIMS, DIMS), 'bv': jnp.zeros((DIMS,), jnp.float32), 'Wo': lin_w(ks[4], DIMS, DIMS), 'bo': jnp.zeros((DIMS,), jnp.float32), 'lna_w': jnp.ones((DIMS,), jnp.float32), 'lnb_w': jnp.ones((DIMS,), jnp.float32), 'lnc_w': jnp.ones((HD,), jnp.float32), 'lnd_w': jnp.ones((HD,), jnp.float32), 'lq_w': lin_w(ks[5], HD, HD), 'lq_b': jnp.zeros((HD,), jnp.float32), 'lk_w': lin_w(ks[6], HD, HD), 'lk_b': jnp.zeros((HD,), jnp.float32), 'lv_w': lin_w(ks[7], HD, HD), 'lv_b': jnp.zeros((HD,), jnp.float32), 'threshold': jnp.float32(0.01), 'temp_base': jnp.float32(1.0), 'factor': jnp.float32(0.1)}
    _L1_attn_in = _L1_attn_setup()

    def _L1_ffn_setup():
        import jax, jax.numpy as jnp
        import numpy as np
        HIDDEN = 128
        NUM_EXPERTS = 8
        TOP_K = 2
        B, S = (4, 128)
        key = jax.random.key(seed)
        ks = jax.random.split(key, 8)
        H, E = (HIDDEN, NUM_EXPERTS)
        sc = lambda fan_in: 1.0 / np.sqrt(fan_in)
        x = jax.random.normal(ks[0], (B, S, H), dtype=jnp.float32)
        Wr = jax.random.uniform(ks[1], (H, E), minval=-sc(H), maxval=sc(H), dtype=jnp.float32)
        br = jax.random.uniform(ks[2], (E,), minval=-sc(H), maxval=sc(H), dtype=jnp.float32)
        W1 = jax.random.uniform(ks[3], (E, H, 2 * H), minval=-sc(H), maxval=sc(H), dtype=jnp.float32)
        b1 = jax.random.uniform(ks[4], (E, 2 * H), minval=-sc(H), maxval=sc(H), dtype=jnp.float32)
        W2 = jax.random.uniform(ks[5], (E, 2 * H, H), minval=-sc(2 * H), maxval=sc(2 * H), dtype=jnp.float32)
        b2 = jax.random.uniform(ks[6], (E, H), minval=-sc(2 * H), maxval=sc(2 * H), dtype=jnp.float32)
        return {'x': x, 'Wr': Wr, 'br': br, 'W1': W1, 'b1': b1, 'W2': W2, 'b2': b2}
    _L1_ffn_in = _L1_ffn_setup()
    _d = {'L0_attn_x': _L0_attn_in['x'], 'L0_attn_w_qkv': _L0_attn_in['w_qkv'], 'L0_attn_w_proj': _L0_attn_in['w_proj'], 'L0_ffn_W_r': _L0_ffn_in['W_r'], 'L0_ffn_W_k': _L0_ffn_in['W_k'], 'L0_ffn_W_v': _L0_ffn_in['W_v'], 'L0_ffn_mu_r': _L0_ffn_in['mu_r'], 'L0_ffn_mu_k': _L0_ffn_in['mu_k'], 'L1_attn_Wq': _L1_attn_in['Wq'], 'L1_attn_bq': _L1_attn_in['bq'], 'L1_attn_Wk': _L1_attn_in['Wk'], 'L1_attn_Wv': _L1_attn_in['Wv'], 'L1_attn_bv': _L1_attn_in['bv'], 'L1_attn_Wo': _L1_attn_in['Wo'], 'L1_attn_bo': _L1_attn_in['bo'], 'L1_attn_lna_w': _L1_attn_in['lna_w'], 'L1_attn_lnb_w': _L1_attn_in['lnb_w'], 'L1_attn_lnc_w': _L1_attn_in['lnc_w'], 'L1_attn_lnd_w': _L1_attn_in['lnd_w'], 'L1_attn_lq_w': _L1_attn_in['lq_w'], 'L1_attn_lq_b': _L1_attn_in['lq_b'], 'L1_attn_lk_w': _L1_attn_in['lk_w'], 'L1_attn_lk_b': _L1_attn_in['lk_b'], 'L1_attn_lv_w': _L1_attn_in['lv_w'], 'L1_attn_lv_b': _L1_attn_in['lv_b'], 'L1_attn_threshold': _L1_attn_in['threshold'], 'L1_attn_temp_base': _L1_attn_in['temp_base'], 'L1_attn_factor': _L1_attn_in['factor'], 'L1_ffn_Wr': _L1_ffn_in['Wr'], 'L1_ffn_br': _L1_ffn_in['br'], 'L1_ffn_W1': _L1_ffn_in['W1'], 'L1_ffn_b1': _L1_ffn_in['b1'], 'L1_ffn_W2': _L1_ffn_in['W2'], 'L1_ffn_b2': _L1_ffn_in['b2']}
    _x0 = _d['L0_attn_x']
    _d['L0_attn_x'] = jax.random.normal(jax.random.fold_in(jax.random.key(seed), 1), (16, 256, 128), dtype=_x0.dtype)
    del _x0
    return _d

def reference(L0_attn_x, L0_attn_w_qkv, L0_attn_w_proj, L0_ffn_W_r, L0_ffn_W_k, L0_ffn_W_v, L0_ffn_mu_r, L0_ffn_mu_k, L1_attn_Wq, L1_attn_bq, L1_attn_Wk, L1_attn_Wv, L1_attn_bv, L1_attn_Wo, L1_attn_bo, L1_attn_lna_w, L1_attn_lnb_w, L1_attn_lnc_w, L1_attn_lnd_w, L1_attn_lq_w, L1_attn_lq_b, L1_attn_lk_w, L1_attn_lk_b, L1_attn_lv_w, L1_attn_lv_b, L1_attn_threshold, L1_attn_temp_base, L1_attn_factor, L1_ffn_Wr, L1_ffn_br, L1_ffn_W1, L1_ffn_b1, L1_ffn_W2, L1_ffn_b2):

    def _L0_attn_ref(x, w_qkv, w_proj):
        import jax, jax.numpy as jnp
        import numpy as np
        B, T, DIM, H = (2, 256, 128, 16)
        HD = DIM // H

        def _custom_softmax(a):
            a = jnp.clip(a, -100.0, 100.0)
            m = jnp.max(a, axis=-1, keepdims=True)
            e = jnp.exp(a - m)
            p = e / (jnp.sum(e, axis=-1, keepdims=True) + 1e-06)
            p = p + 1e-08
            return p / jnp.sum(p, axis=-1, keepdims=True)
        b, t, c = x.shape
        scale = HD ** (-0.5)
        qkv = jnp.einsum('btc,oc->bto', x, w_qkv)
        qkv = qkv.reshape(b, t, 3, H, HD)
        q = jnp.transpose(qkv[:, :, 0], (0, 2, 1, 3))
        k = jnp.transpose(qkv[:, :, 1], (0, 2, 1, 3))
        v = jnp.transpose(qkv[:, :, 2], (0, 2, 1, 3))
        attn = jnp.einsum('bhqd,bhkd->bhqk', q, k) * scale
        causal = jnp.tril(jnp.ones((t, t), dtype=bool))
        attn = jnp.where(causal, attn, -jnp.inf)
        attn = _custom_softmax(attn)
        out = jnp.einsum('bhqk,bhkd->bhqd', attn, v)
        out = jnp.transpose(out, (0, 2, 1, 3)).reshape(b, t, c)
        return jnp.einsum('btc,oc->bto', out, w_proj)

    def _L0_ffn_ref(x, W_r, W_k, W_v, mu_r, mu_k):
        import jax, jax.numpy as jnp
        import numpy as np
        DIM = 128

        def _reference_tuple_inner(x, W_r, W_k, W_v, mu_r, mu_k):
            B, T, C = x.shape
            x_prev = jnp.concatenate([jnp.zeros((B, 1, C), x.dtype), x[:, :-1, :]], axis=1)
            xr = mu_r * x + (1.0 - mu_r) * x_prev
            xk = mu_k * x + (1.0 - mu_k) * x_prev
            r = jax.nn.sigmoid(jnp.einsum('btc,dc->btd', xr, W_r))
            k = jnp.einsum('btc,dc->btd', xk, W_k)
            k_act = jnp.square(jax.nn.relu(k))
            out = r * jnp.einsum('btc,dc->btd', k_act, W_v)
            new_state = x[:, -1, :]
            return (out, new_state)
        return _reference_tuple_inner(x, W_r, W_k, W_v, mu_r, mu_k)[0]

    def _L1_attn_ref(x, Wq, bq, Wk, Wv, bv, Wo, bo, lna_w, lnb_w, lnc_w, lnd_w, lq_w, lq_b, lk_w, lk_b, lv_w, lv_b, threshold, temp_base, factor):
        import jax, jax.numpy as jnp
        import numpy as np
        DIMS = 128
        HEAD = 16
        HD = DIMS // HEAD
        MAX_ITER = 3
        MIN_SIZE = 64
        MAX_SIZE = 256
        UP_WIN, DOWN_WIN = (1.1, 0.9)
        UP_DIFF, DOWN_DIFF = (0.05, 0.001)
        B, T = (2, 128)

        def _ln(x, w, eps=1e-05):
            m = jnp.mean(x, axis=-1, keepdims=True)
            v = jnp.var(x, axis=-1, keepdims=True)
            return (x - m) * jax.lax.rsqrt(v + eps) * w

        def _focus(x, Wq, bq, Wk, Wv, bv, Wo, bo, lna_w, lnb_w, lnc_w, lnd_w, lq_w, lq_b, lk_w, lk_b, lv_w, lv_b, threshold, temp_base, factor):
            b, t, d = x.shape
            q = _ln(x, lna_w) @ Wq.T + bq
            kk = _ln(x, lnb_w) @ Wk.T
            v = _ln(x, lnb_w) @ Wv.T + bv
            sc = HD ** (-0.25)

            def _shape(u):
                return u.reshape(b, t, HEAD, HD).transpose(0, 2, 1, 3)
            q_full = _shape(q * sc)
            k_full = _shape(kk * sc)
            v_full = _shape(v)
            thr = jax.lax.stop_gradient(threshold)
            fac = jax.lax.stop_gradient(factor)
            t0 = jax.lax.stop_gradient(temp_base)
            cw0 = jnp.int32(max(min(t, MAX_SIZE), MIN_SIZE))
            inv_sqrt_e = jnp.float32(1.0 / np.sqrt(HD))
            pos = jnp.arange(t)

            def step(carry, i):
                qcur, prev, attn, cw, temp, done = carry
                qp = qcur @ lq_w.T + lq_b
                kp = k_full @ lk_w.T + lk_b
                vp = v_full @ lv_w.T + lv_b
                sq = _ln(qp, lnc_w)
                sk = _ln(kp, lnd_w)
                tscale = jnp.where(temp > 0, jax.lax.rsqrt(temp), jnp.float32(1.0))
                sq = sq * tscale
                scores = jnp.einsum('bhqd,bhkd->bhqk', sq, sk) * inv_sqrt_e
                in_win = pos < cw
                scores = jnp.where(in_win[None, None, None, :], scores, -jnp.inf)
                probs = jax.nn.softmax(scores, axis=-1)
                out = jnp.einsum('bhqk,bhkd->bhqd', probs, vp)
                iter_out = jnp.where(in_win[None, None, :, None], out, 0.0)
                diff = jnp.mean(jnp.abs(iter_out - prev))
                converged = (diff < thr + fac * diff) & (i > 0)
                upd = ~done & ~converged
                new_done = done | converged
                attn_n = jnp.where(done, attn, iter_out)
                prev_n = jnp.where(upd, iter_out, prev)
                qcur_n = jnp.where(upd, qcur + iter_out, qcur)
                up = (cw.astype(jnp.float32) * UP_WIN).astype(jnp.int32)
                down = (cw.astype(jnp.float32) * DOWN_WIN).astype(jnp.int32)
                nw = jnp.where(diff > UP_DIFF, up, jnp.where((diff < DOWN_DIFF) & (cw > MIN_SIZE), down, cw))
                nw = jnp.clip(nw, MIN_SIZE, t)
                cw_n = jnp.where(upd, nw, cw)
                temp_n = jnp.where(upd, temp + jnp.float32(0.005), temp)
                return ((qcur_n, prev_n, attn_n, cw_n, temp_n, new_done), None)
            zeros = jnp.zeros_like(q_full)
            carry0 = (q_full, zeros, zeros, cw0, t0, jnp.array(False))
            (_, _, attn_out, _, _, _), _ = jax.lax.scan(step, carry0, jnp.arange(MAX_ITER))
            output = attn_out.transpose(0, 2, 1, 3).reshape(b, t, d)
            return output @ Wo.T + bo
        return _focus(x, Wq, bq, Wk, Wv, bv, Wo, bo, lna_w, lnb_w, lnc_w, lnd_w, lq_w, lq_b, lk_w, lk_b, lv_w, lv_b, threshold, temp_base, factor)

    def _L1_ffn_ref(x, Wr, br, W1, b1, W2, b2):
        import jax, jax.numpy as jnp
        import numpy as np
        HIDDEN = 128
        NUM_EXPERTS = 8
        TOP_K = 2
        B, S = (4, 128)
        B_, S_, H = x.shape
        xf = x.reshape(-1, H)
        logits = xf @ Wr + br
        topk_w, topk_idx = jax.lax.top_k(logits, TOP_K)
        topk_w = jax.nn.softmax(topk_w, axis=-1)
        gate = jnp.sum(jax.nn.one_hot(topk_idx, NUM_EXPERTS, dtype=xf.dtype) * topk_w[..., None], axis=1)
        h = jax.nn.relu(jnp.einsum('th,ehf->etf', xf, W1) + b1[:, None, :])
        y = jnp.einsum('etf,efh->eth', h, W2) + b2[:, None, :]
        out = jnp.einsum('te,eth->th', gate, y)
        return out.reshape(B_, S_, H)
    x = L0_attn_x
    x = x + 0.5 * _L0_ffn_ref(_layernorm(x, axis=-1), L0_ffn_W_r, L0_ffn_W_k, L0_ffn_W_v, L0_ffn_mu_r, L0_ffn_mu_k)
    x = x + _L0_attn_ref(_layernorm(x, axis=-1), L0_attn_w_qkv, L0_attn_w_proj)
    x = x + 0.5 * _L0_ffn_ref(_layernorm(x, axis=-1), L0_ffn_W_r, L0_ffn_W_k, L0_ffn_W_v, L0_ffn_mu_r, L0_ffn_mu_k)
    x = x + 0.5 * _L1_ffn_ref(_layernorm(x, axis=-1), L1_ffn_Wr, L1_ffn_br, L1_ffn_W1, L1_ffn_b1, L1_ffn_W2, L1_ffn_b2)
    x = x + _L1_attn_ref(_layernorm(x, axis=-1), L1_attn_Wq, L1_attn_bq, L1_attn_Wk, L1_attn_Wv, L1_attn_bv, L1_attn_Wo, L1_attn_bo, L1_attn_lna_w, L1_attn_lnb_w, L1_attn_lnc_w, L1_attn_lnd_w, L1_attn_lq_w, L1_attn_lq_b, L1_attn_lk_w, L1_attn_lk_b, L1_attn_lv_w, L1_attn_lv_b, L1_attn_threshold, L1_attn_temp_base, L1_attn_factor)
    x = x + 0.5 * _L1_ffn_ref(_layernorm(x, axis=-1), L1_ffn_Wr, L1_ffn_br, L1_ffn_W1, L1_ffn_b1, L1_ffn_W2, L1_ffn_b2)
    return x

_drawn_inputs = setup_inputs


def setup_inputs(seed=0):
    import zlib

    import numpy as np

    out = dict(_drawn_inputs(seed))
    spreads = {'L1_attn_bq': (0.0, 0.546),
     'L1_attn_bv': (0.0, 0.1),
     'L1_attn_bo': (0.0, 0.1),
     'L1_attn_lna_w': (1.0, 0.6),
     'L1_attn_lnb_w': (1.0, 0.2),
     'L1_attn_lnc_w': (1.0, 0.6),
     'L1_attn_lnd_w': (1.0, 0.6),
     'L1_attn_lq_b': (0.0, 0.379),
     'L1_attn_lk_b': (0.0, 0.692),
     'L1_attn_lv_b': (0.0, 0.1)}
    factors = {'L0_ffn_mu_r': 4.497, 'L1_ffn_b1': 3.854}
    for name, (base, spread) in spreads.items():
        noise = np.random.default_rng([zlib.crc32(name.encode()), seed]).standard_normal(out[name].shape)
        drawn = base * np.exp(spread * noise) if base else spread * noise
        out[name] = jnp.asarray(drawn.astype(out[name].dtype))
    for name, factor in factors.items():
        out[name] = (out[name] * factor).astype(out[name].dtype)
    return out
```

```python
from contextlib import ExitStack

import numpy as np

import concourse.bass as bass
from concourse import mybir

F32 = mybir.dt.float32
BF16 = mybir.dt.bfloat16
I32 = mybir.dt.int32
ALU = mybir.AluOpType
ACT = mybir.ActivationFunctionType
AX = mybir.AxisListType

P = 128
B, T, C = 16, 256, 128
H, HD = 16, 8
NT = T // P
EXP, HID = 8, 256
NF = HID // P
GB = 2
GT = GB * NT
NG = B // GB
HG = 4
VW = 32
MIN_SIZE, MAX_ITER = 64, 3
UP_WIN, DOWN_WIN, UP_DIFF, DOWN_DIFF = 1.1, 0.9, 0.05, 0.001
EPS = 1e-5
CLIP, DEN_EPS, P_EPS = 100.0, 1e-6, 1e-8
MASKED = -1.0e30
SC = HD ** -0.25
INV_SQRT = HD ** -0.5

ROWS_QK = 9 * HD
ROW_WIN = ROWS_QK
ROW_MAX = ROWS_QK + 1
ROWS_P1 = ROWS_QK + 1
ROWS_P2 = ROW_MAX + 6
PLANE = C * T

W_Q0, W_K0, W_V0, W_P0, W_R, W_K, W_V, W_Q1, W_O1, W_K1, W_V1, W_LQ = range(12)


def macaron_kernel(nc, a, out):
    ctx = ExitStack()
    with ctx:
        def sb(name, shape, dt=F32):
            return ctx.enter_context(nc.sbuf_tensor(name, shape, dt))

        def pb(name, shape, dt=F32):
            return ctx.enter_context(nc.psum_tensor(name, shape, dt))

        made = {}

        def sem(name):
            if name not in made:
                made[name] = ctx.enter_context(nc.semaphore(name))
            return made[name]

        x = sb("x", [P, B, NT * C])
        qcur = sb("qcur", [P, B, NT * C])
        heads_out = sb("heads_out", [P, B, NT * C])
        vp_all = sb("vp_all", [P, B, NT * C])

        w_nat = sb("w_nat", [P, 11, C])
        w_t = sb("w_t", [P, 12, C])
        w1 = sb("w1", [P, EXP, HID])
        w2 = sb("w2", [P, EXP * NF, C])
        wr = sb("wr", [P, EXP])
        b2 = sb("b2", [EXP, C])
        b1_nat = sb("b1_nat", [EXP * NF, P])
        b1_t = sb("b1_t", [P, EXP * NF])
        cols = sb("cols", [P, 8])
        MU_R, MU_K, LNA, LNB, BV, THR, TMP, FAC = range(8)
        rows = sb("rows", [P, 7, C])
        R_BQ, R_BO, R_LQ, R_LK, R_LV, R_LNC, R_LND = range(7)
        v_bias = sb("v_bias", [P, C])
        br_row = sb("br_row", [P, EXP])
        head_w = sb("head_w", [P, 3, HD])
        block_w = sb("block_w", [P, 3, C])
        block_mask = sb("block_mask", [P, H, HD])
        bv_rep = sb("bv_rep", [P, P])

        ident = sb("ident", [P, P])
        ident_b = sb("ident_b", [P, P], BF16)
        ones = sb("ones", [P, P])
        ones_b = sb("ones_b", [P, T], BF16)
        mask_q = sb("mask_q", [P, 2 * P], BF16)
        mask_k = sb("mask_k", [P, 2 * P], BF16)
        sel_l = sb("sel_l", [P, P], BF16)
        k_const = sb("k_const", [P, T], BF16)
        pos_row = sb("pos_row", [P, T])
        pos_col = sb("pos_col", [P, NT])
        tri = sb("tri", [P, EXP, EXP])

        st = sb("st", [P, GT, 6])
        mv = sb("mv", [P, GT, 2])
        lnv = sb("lnv", [P, GT])
        rstd = sb("rstd", [P, GT])
        y = sb("y", [P, GT, C])
        y2 = sb("y2", [P, NT, C])
        y_t = sb("y_t", [P, 1 + T])
        dy = sb("dy", [P, T])
        xr = sb("xr", [P, T])
        xk = sb("xk", [P, T])
        er = sb("er", [P, T])
        rec = sb("rec", [P, T])
        kr = sb("kr", [P, T])
        ka = sb("ka", [P, T])
        gated = sb("gated", [P, T])
        z_t = sb("z_t", [P, T])
        qk32 = sb("qk32", [P, 2, T])
        rest = sb("rest", [P, 2, T])
        parts = sb("parts", [P, 2, 3, T], BF16)
        lin = sb("lin", [P, 2, NT, H, HD])
        cen = sb("cen", [P, 2, NT, H, HD])
        sqr = sb("sqr", [P, 2, NT, H, HD])
        nrm = sb("nrm", [P, 2, NT, HD, H])
        hsum = sb("hsum", [P, 2 * NT * H])
        hvar = sb("hvar", [P, 2 * NT * H])
        hln = sb("hln", [P, 2 * NT * H])
        hrs = sb("hrs", [P, 2 * NT * H])

        q_st = [sb(f"q_st{p}", [P, H, T], BF16) for p in range(2)]
        k_st = [sb(f"k_st{p}", [P, H, T], BF16) for p in range(2)]
        v_st = [sb(f"v_st{p}", [P, NT, H, VW]) for p in range(2)]
        nmax = sb("nmax", [P, NT, H])
        ml = sb("ml", [P, NT, 2, H])
        ml32 = sb("ml32", [2 * H, T])
        ml_rest = sb("ml_rest", [2 * H, T])
        ml_parts = sb("ml_parts", [2 * H, 3, T], BF16)
        e_buf = [sb(f"e_buf{g}", [P, HG, 2 * T]) for g in range(2)]
        o_sb = sb("o_sb", [P, H // HG, T])
        s_sum = sb("s_sum", [P, NT, H])
        s_u = sb("s_u", [P, NT, H])
        s_du = sb("s_du", [P, NT, H])
        s_den = sb("s_den", [P, NT, H])
        s_rec = sb("s_rec", [P, NT, H])
        corr = sb("corr", [P, NT, H, HD])
        corr2 = sb("corr2", [P, H, HD])
        o_tok = sb("o_tok", [P, NT, H, HD])
        o_prev = sb("o_prev", [P, NT * C])
        o_t = sb("o_t", [P, T])

        dsum = sb("dsum", [P, B])
        dtot = sb("dtot", [P, 1])
        ctl = sb("ctl", [P, 24])
        (DIFF, LIM, CONV, DONE, KEEP, CW, UP, DN, GUP, GDN, T0, T1, QSC, NW, TMPC, TPOS, TLN, TRS) = range(18)
        ctl_i = sb("ctl_i", [P, 2], I32)
        in_win = sb("in_win", [P, NT])
        win_row = sb("win_row", [P, T], BF16)

        ym_t = sb("ym_t", [P, GT * P])
        lg = sb("lg", [P, GT, EXP])
        gt_ = sb("gt_", [P, GT, EXP, EXP])
        eq_ = sb("eq_", [P, GT, EXP, EXP])
        rank = sb("rank", [P, GT, EXP])
        lmax = sb("lmax", [P, GT])
        lexp = sb("lexp", [P, GT, EXP])
        gsum = sb("gsum", [P, GT])
        gate = sb("gate", [P, GT, EXP])
        h_sb = [e_buf[i][:, 0:NF, :] for i in range(2)]
        acc = e_buf[0][:, NF, :].rearrange("p (t c) -> p t c", t=GT)
        gate_t = e_buf[1][0:EXP, NF, :]

        ps_q = pb("ps_q", [P, 2, 512])
        ps_k = pb("ps_k", [P, 2, 512])
        ps_o = pb("ps_o", [P, 2, 512])
        ps_m = pb("ps_m", [P, 2, 512])

        scr_q = nc.dram_tensor("scr_q", (2, 3, PLANE), BF16, kind="Internal").ap()
        scr_k = nc.dram_tensor("scr_k", (B, 3, PLANE), BF16, kind="Internal").ap()
        scr_m = nc.dram_tensor("scr_m", (2, 3, 2 * H * T), BF16, kind="Internal").ap()

        def on_all(src, dims):
            return bass.AP(src.tensor, 0, [[0, P]] + dims)

        def col(j):
            return cols[:, j:j + 1]

        def c1(j):
            return ctl[:, j:j + 1]

        SETUP_DMAS = []
        CONSTS = 30
        block = ctx.enter_context(nc.Block())

        @block.sync
        def _(sp):
            loads = sem("loaded")

            def load(dst, src):
                sp.dma_start(dst, src).then_inc(loads, 16)
                SETUP_DMAS.append(1)

            load(w_nat[:, 0:3, :], a["L0_attn_w_qkv"].rearrange("(s o) c -> o s c", s=3))
            for j, name in ((3, "L0_attn_w_proj"), (4, "L0_ffn_W_r"), (5, "L0_ffn_W_k"), (6, "L0_ffn_W_v"),
                            (7, "L1_attn_Wq"), (8, "L1_attn_Wo"), (9, "L1_attn_Wk"), (10, "L1_attn_Wv")):
                load(w_nat[:, j, :], a[name])
            for j, name in ((MU_R, "L0_ffn_mu_r"), (MU_K, "L0_ffn_mu_k"), (LNA, "L1_attn_lna_w"),
                            (LNB, "L1_attn_lnb_w"), (BV, "L1_attn_bv")):
                load(col(j), a[name].rearrange("(p o) -> p o", o=1))
            for j, name in ((THR, "L1_attn_threshold"), (TMP, "L1_attn_temp_base"), (FAC, "L1_attn_factor")):
                load(col(j), on_all(a[name], [[1, 1]]))
            for j, name in ((R_BQ, "L1_attn_bq"), (R_BO, "L1_attn_bo")):
                load(rows[:, j, :], on_all(a[name], [[1, C]]))
            for j, name in ((R_LQ, "L1_attn_lq_b"), (R_LK, "L1_attn_lk_b"), (R_LV, "L1_attn_lv_b"),
                            (R_LNC, "L1_attn_lnc_w"), (R_LND, "L1_attn_lnd_w")):
                load(rows[:, j, :].rearrange("p (h d) -> p h d", h=H), on_all(a[name], [[0, H], [1, HD]]))
            for j, name in enumerate(("L1_attn_lq_w", "L1_attn_lk_w", "L1_attn_lv_w")):
                load(head_w[:, j, :], bass.AP(a[name].tensor, 0, [[0, H], [HD, HD], [1, HD]]))
            load(br_row[:, :], on_all(a["L1_ffn_br"], [[1, EXP]]))
            load(wr[:, :], a["L1_ffn_Wr"])
            load(b1_nat[:, :], a["L1_ffn_b1"].rearrange("e (t p) -> (e t) p", p=P))
            load(b2[:, :], a["L1_ffn_b2"])
            load(x[:, :, :].rearrange("p b (t c) -> p (b t) c", c=C),
                 a["L0_attn_x"].rearrange("b (t p) c -> p (b t) c", p=P))
            load(w1[:, :, :], a["L1_ffn_W1"].rearrange("e h f -> h e f"))
            load(w2[:, :, :], a["L1_ffn_W2"].rearrange("e (t p) h -> p (e t) h", p=P))
            sp.wait_ge(sem("consts"), CONSTS)
            for p in range(2):
                load(k_st[p][ROW_WIN:ROWS_P2, :, :],
                     k_const[ROW_WIN:ROWS_P2, :].unsqueeze(1).broadcast_to([ROWS_P2 - ROW_WIN, H, T]))
                load(q_st[p][ROW_WIN:ROW_WIN + 1, :, :], ones_b[0:1, :].unsqueeze(1).broadcast_to([1, H, T]))

            def operands(n, p, b, with_k):
                sp.wait_ge(sem("parts_ready"), n + 1)
                sp.dma_start(bass.AP(scr_q.tensor, p * 3 * PLANE, [[T, C], [PLANE, 3], [1, T]]),
                             parts[:, 0, :, :]).then_inc(sem("parts_out"), 16)
                if with_k:
                    sp.dma_start(scr_k[b].rearrange("j (c t) -> c j t", t=T),
                                 parts[:, 1, :, :]).then_inc(sem("k_parts_out"), 16)
                    sp.wait_ge(sem("k_parts_out"), n * 16 + 16)
                sp.wait_ge(sem("parts_out"), n * 16 + 16)
                sp.wait_ge(sem("operands_free"), n + 1)
                for j in range(3):
                    sp.dma_start(q_st[p][24 * j:24 * j + 24, :, :].rearrange("r h t -> r (h t)"),
                                 bass.AP(scr_q.tensor, (p * 3 + j) * PLANE, [[0, 3], [H * T, HD], [1, H * T]]))\
                      .then_inc(sem("operands_in"), 16)
                for j in range(3):
                    sp.dma_start(k_st[p][24 * j:24 * j + 24, :, :].rearrange("r h t -> r (h t)"),
                                 scr_k[b].rearrange("j (d n) -> (j d) n", n=H * T))\
                      .then_inc(sem("operands_in"), 16)

            def max_rows(n, p):
                sp.wait_ge(sem("ml_parts_ready"), n + 1)
                sp.dma_start(bass.AP(scr_m.tensor, p * 3 * 2 * H * T, [[T, 2 * H], [2 * H * T, 3], [1, T]]),
                             ml_parts[:, :, :]).then_inc(sem("ml_out"), 16)
                sp.wait_ge(sem("ml_out"), n * 16 + 16)
                sp.dma_start(q_st[p][ROW_MAX:ROWS_P2, :, :].rearrange("r h t -> r (h t)"),
                             bass.AP(scr_m.tensor, p * 3 * 2 * H * T, [[H * T, 6], [1, H * T]]))\
                  .then_inc(sem("ml_in"), 16)

            with sp.Fori(0, B // 2) as i:
                for p in range(2):
                    operands(i * 2 + p, p, i * 2 + p, True)
                    max_rows(i * 2 + p, p)
            for it in range(MAX_ITER):
                if it:
                    sp.wait_ge(sem("window_ready"), it)
                    for p in range(2):
                        sp.dma_start(k_st[p][ROW_WIN:ROW_WIN + 1, :, :],
                                     win_row[0:1, :].unsqueeze(1).broadcast_to([1, H, T]))\
                          .then_inc(sem("window_in"), 16)
                with sp.Fori(0, B // 2) as i:
                    for p in range(2):
                        n = (1 + it) * B + i * 2 + p
                        operands(n, p, i * 2 + p, it == 0)
                        max_rows(n, p)
            with sp.Fori(0, NG) as g:
                sp.wait_ge(sem("M_x"), NG + g + 1)
                sp.dma_start(out.rearrange("b (t p) c -> p (b t) c", p=P)[:, bass.ds(g * GT, GT), :],
                             x[:, bass.ds(g * GB, GB), :].rearrange("p b (t c) -> p (b t) c", c=C))\
                  .then_inc(sem("stored"), 16)
            sp.wait_ge(sem("stored"), NG * 16)

        n_loads = 16 * len(SETUP_DMAS)

        @block.gpsimd
        def _(pool):
            done = [0]

            def const(ins):
                ins.then_inc(sem("consts"), 1)
                done[0] += 1
                pool.wait_ge(sem("consts"), done[0])

            def select(t, op, fill, base, pattern, step):
                const(pool.affine_select(out=t, in_=t, compare_op=op, fill=fill, base=base, pattern=pattern,
                                         channel_multiplier=step))

            for t in (ident, ident_b, mask_q, mask_k, sel_l, k_const):
                const(pool.memset(t[:, :], 0.0))
            for t in (ones, ones_b):
                const(pool.memset(t[:, :], 1.0))
            for t in (block_mask, tri):
                const(pool.memset(t[:, :, :], 1.0))
            for p in range(2):
                const(pool.memset(v_st[p][:, :, :, :], 0.0))
                const(pool.memset(v_st[p][:, :, :, HD:HD + 1], 1.0))
            const(pool.memset(y_t[:, 0:1], 0.0))
            select(ident[:, :], ALU.not_equal, 1.0, 0, [[-1, P]], 1)
            select(ident_b[:, :], ALU.not_equal, 1.0, 0, [[-1, P]], 1)
            select(mask_q[:, :], ALU.is_ge, MASKED, 0, [[0, 2], [-1, P]], 1)
            select(mask_k[:, :], ALU.is_ge, MASKED, 0, [[0, 2], [1, P]], -1)
            for j in range(3):
                select(k_const[:, :], ALU.not_equal, 1.0, -(ROW_MAX + 2 * j), [[0, T]], 1)
                select(sel_l[:, :], ALU.not_equal, 1.0, -(ROW_MAX + 2 * j + 1), [[0, P]], 1)
            select(block_mask[:, :, :], ALU.is_ge, 0.0, 0, [[-HD, H], [0, HD]], 1)
            select(block_mask[:, :, :], ALU.is_ge, 0.0, HD - 1, [[HD, H], [0, HD]], -1)
            select(tri[:, :, :], ALU.is_gt, 0.0, 0, [[1, EXP], [-1, EXP]], 0)
            const(pool.iota(pos_row[:, :], pattern=[[1, T]], base=0, channel_multiplier=0,
                            allow_small_or_imprecise_dtypes=True))
            const(pool.iota(pos_col[:, :], pattern=[[P, NT]], base=0, channel_multiplier=1,
                            allow_small_or_imprecise_dtypes=True))
            assert done[0] == CONSTS

            def ffn(n):
                pool.wait_ge(sem("F_ytc"), n + 1)
                pool.tensor_tensor(dy[:, :], y_t[:, 1:T + 1], y_t[:, 0:T], ALU.subtract).then_inc(sem("F_dy"), 1)
                pool.wait_ge(sem("F_kr"), n + 1)
                pool.tensor_tensor(ka[:, :], kr[:, :], kr[:, :], ALU.mult).then_inc(sem("F_ka"), 1)

            def split(n, s):
                pool.wait_ge(sem("part_hi"), n + 1)
                pool.tensor_tensor(rest[:, 0:s, :], qk32[:, 0:s, :], parts[:, 0:s, 0, :], ALU.subtract)\
                    .then_inc(sem("part_rest"), 1)
                pool.wait_ge(sem("part_mid"), n + 1)
                pool.tensor_tensor(parts[:, 0:s, 2, :], rest[:, 0:s, :], parts[:, 0:s, 1, :], ALU.subtract)\
                    .then_inc(sem("parts_ready"), 1)

            def maxima(n):
                pool.wait_ge(sem("ml_hi"), n + 1)
                pool.tensor_tensor(ml_rest[:, :], ml32[:, :], ml_parts[:, 0, :], ALU.subtract)\
                    .then_inc(sem("ml_rest"), 1)
                pool.wait_ge(sem("ml_mid"), n + 1)
                pool.tensor_tensor(ml_parts[:, 2, :], ml_rest[:, :], ml_parts[:, 1, :], ALU.subtract)\
                    .then_inc(sem("ml_parts_ready"), 1)

            with pool.Fori(0, B // 2) as i:
                for p in range(2):
                    n = i * 2 + p
                    ffn(n * 2)
                    split(n, 2)
                    maxima(n)
                    ffn(n * 2 + 1)
            for it in range(MAX_ITER):
                with pool.Fori(0, B // 2) as i:
                    for p in range(2):
                        n = (1 + it) * B + i * 2 + p
                        split(n, 2 if it == 0 else 1)
                        maxima(n)

        @block.scalar
        def _(act):
            act.preload_act_table_set("natural_log_exp_and_others")
            act.wait_ge(sem("consts"), CONSTS)

            def copy(dst, src, scale=1.0):
                return act.activation(dst, src, ACT.Copy, scale=scale)

            def rsqrt(pre, n, per, var, tmp, res, scale=1.0):
                act.wait_ge(sem(pre + "_mom"), n * per + per)
                act.activation(tmp, var, ACT.Ln, scale=scale, bias=EPS).then_inc(sem(pre + "_ln"), 1)
                act.wait_ge(sem(pre + "_ln"), n + 1)
                act.activation(res, tmp, ACT.Exp, scale=-0.5).then_inc(sem(pre + "_rstd"), 1)

            def ffn(n):
                rsqrt("F", n, NT, mv[:, 0:NT, 1], lnv[:, 0:NT], rstd[:, 0:NT])
                act.wait_ge(sem("F_yt"), n + 1)
                copy(y_t[:, 1:T + 1], ps_m[:, 0, 0:T]).then_inc(sem("F_ytc"), 1)
                act.wait_ge(sem("F_r"), n + 1)
                act.activation(er[:, :], ps_m[:, 1, 0:T], ACT.Exp, scale=-1.0).then_inc(sem("F_er"), 1)
                act.wait_ge(sem("F_k"), n + 1)
                act.activation(kr[:, :], ps_o[:, 0, 0:T], ACT.Relu).then_inc(sem("F_kr"), 1)

            def split(n, s):
                act.wait_ge(sem("qk32"), n * 2 + 2)
                copy(parts[:, 0:s, 0, :], qk32[:, 0:s, :]).then_inc(sem("part_hi"), 1)
                act.wait_ge(sem("part_rest"), n + 1)
                copy(parts[:, 0:s, 1, :], rest[:, 0:s, :]).then_inc(sem("part_mid"), 1)

            def causal_front(n):
                rsqrt("G", n, NT, mv[:, 0:NT, 1], lnv[:, 0:NT], rstd[:, 0:NT])
                act.wait_ge(sem("G_yt"), n + 1)
                copy(z_t[:, :], ps_m[:, 0, 0:T]).then_inc(sem("G_ytc"), 1)
                act.wait_ge(sem("G_qk"), n + 1)
                copy(qk32[:, 0, :], ps_m[:, 1, 0:T], INV_SQRT).then_inc(sem("qk32"), 1)
                copy(qk32[:, 1, :], ps_m[:, 1, T:2 * T]).then_inc(sem("qk32"), 1)
                split(n, 2)

            def focus_front(n, b, first):
                if first:
                    for pre in ("H", "I"):
                        rsqrt(pre, b, NT, mv[:, 0:NT, 1], lnv[:, 0:NT], rstd[:, 0:NT])
                    act.wait_ge(sem("H_yt"), b + 1)
                    copy(z_t[:, :], ps_m[:, 0, 0:T]).then_inc(sem("H_ytc"), 1)
                s = 2 if first else 1
                f = n - B
                act.wait_ge(sem("J_qt"), f + 1)
                copy(o_t[:, :], ps_m[:, 0, 0:T]).then_inc(sem("J_qtc"), 1)
                w = s * NT * H
                rsqrt("J", f, 1, hvar[:, 0:w], hln[:, 0:w], hrs[:, 0:w], 1.0 / HD)
                act.wait_ge(sem("J_nt"), f + 1)
                if first:
                    copy(qk32[:, 1, :], ps_m[:, 0, T:2 * T]).then_inc(sem("qk32"), 1)
                    copy(qk32[:, 0, :], ps_m[:, 0, 0:T]).then_inc(sem("qk32"), 1)
                else:
                    copy(qk32[:, 0, :], ps_m[:, 0, 0:T]).then_inc(sem("qk32"), 2)
                split(n, s)

            def maxima(n, causal):
                if causal:
                    act.wait_ge(sem("ml_m"), n + 1)
                    act.activation(ml[:, :, 1, :], ml[:, :, 0, :], ACT.Exp, bias=-CLIP).then_inc(sem("ml_l"), 1)
                act.wait_ge(sem("ml_t"), n + 1)
                copy(ml32[:, :], ps_m[0:2 * H, 1, 0:T]).then_inc(sem("ml32"), 1)
                act.wait_ge(sem("ml32"), n + 1)
                copy(ml_parts[:, 0, :], ml32[:, :]).then_inc(sem("ml_hi"), 1)
                act.wait_ge(sem("ml_rest"), n + 1)
                copy(ml_parts[:, 1, :], ml_rest[:, :]).then_inc(sem("ml_mid"), 1)

            def exps(n, causal):
                w = 3 * P if causal else 2 * T
                for h in range(H):
                    g = h // HG
                    if h % HG == 0:
                        act.wait_ge(sem("values_done"), n * (H // HG) + g + 1)
                    act.wait_ge(sem("k_scores"), n * H + h + 1)
                    act.activation(e_buf[g % 2][:, h % HG, 0:w], ps_k[:, h % 2, 0:w], ACT.Exp)\
                        .then_inc(sem("exp_done"), 1)
                    if causal and h % HG == HG - 1 and g >= 1:
                        evacuate(n, g - 1)
                if causal:
                    evacuate(n, H // HG - 1)

            def evacuate(n, g):
                act.wait_ge(sem("values_done"), n * (H // HG) + g + 1 + 2)
                copy(o_sb[:, g, :], ps_o[:, g % 2, (g // 2) * T:(g // 2 + 1) * T]).then_inc(sem("o_evac"), 1)

            def project(n, pre):
                act.wait_ge(sem(pre + "_ott"), n + 1)
                copy(o_t[:, :], ps_m[:, 0, 0:T]).then_inc(sem(pre + "_otc"), 1)

            def mixture(m):
                rsqrt("M", m, GT, mv[:, :, 1], lnv[:, :], rstd[:, :])
                act.wait_ge(sem("M_yt"), m + 1)
                copy(ym_t[:, :], ps_m[:, 0, :]).then_inc(sem("M_ytc"), 1)
                act.wait_ge(sem("M_lmax"), m + 1)
                act.activation(lexp[:, :, :], eq_[:, :, 0, :], ACT.Exp).then_inc(sem("M_lexp"), 1)
                act.wait_ge(sem("M_gt"), m + 1)
                copy(gate_t, ps_m[0:EXP, 0, :]).then_inc(sem("M_gtc"), 1)
                for e in range(EXP):
                    act.wait_ge(sem("M_out"), m * EXP + e + 1)
                    for f in range(NF):
                        j = e * NF + f
                        act.wait_ge(sem("M_h"), m * EXP * NF + j + 1)
                        bank = (ps_q, ps_k)[j % 4 // 2][:, j % 2, :]
                        act.activation(h_sb[e % 2][:, f, :], bank, ACT.Relu, bias=b1_t[:, j:j + 1])\
                            .then_inc(sem("M_relu"), 1)

            for k in range(3):
                act.wait_ge(sem("w_trans"), k + 1)
                for j in range(4 * k, min(4 * k + 4, 9)):
                    src = ps_m[:, k % 2, (j % 4) * P:(j % 4 + 1) * P]
                    dst = w_t[:, j, :]
                    if j in (W_Q0, W_K0):
                        src = src.rearrange("p (h d) -> p h d", h=H)
                        dst = dst.rearrange("p (d h) -> p h d", h=H)
                    if j == W_Q1:
                        last = act.activation(dst, src, ACT.Copy, scale=col(LNA))
                    else:
                        last = copy(dst, src)
                last.then_inc(sem("w_copied"), 1)
            act.wait_ge(sem("w_trans"), 4)
            copy(b1_t[:, :], ps_m[:, 1, 256:256 + EXP * NF]).then_inc(sem("w_copied"), 1)
            act.wait_ge(sem("w_block"), 1)
            act.activation(w_t[:, W_K1, :], ps_q[:, 0, 0:P], ACT.Copy, scale=col(LNB))
            act.activation(w_t[:, W_V1, :], ps_q[:, 0, P:2 * P], ACT.Copy, scale=col(LNB)).then_inc(sem("w_copied"), 1)

            act.sem_inc(sem("exp_done"), 2)
            act.sem_inc(sem("M_relu"), 4)
            with act.Fori(0, B // 2) as i:
                for p in range(2):
                    n = i * 2 + p
                    ffn(n * 2)
                    causal_front(n)
                    maxima(n, True)
                    exps(n, True)
                    project(n, "A")
                    ffn(n * 2 + 1)
            with act.Fori(0, NG) as g:
                mixture(g)
            for it in range(MAX_ITER):
                act.wait_ge(sem("t_safe"), it + 1)
                act.activation(c1(TLN), c1(T1), ACT.Ln).then_inc(sem("t_ln"), 1)
                act.wait_ge(sem("t_ln"), it + 1)
                act.activation(c1(TRS), c1(TLN), ACT.Exp, scale=-0.5).then_inc(sem("t_rs"), 1)
                with act.Fori(0, B // 2) as i:
                    for p in range(2):
                        b = i * 2 + p
                        n = (1 + it) * B + b
                        focus_front(n, b, it == 0)
                        maxima(n, False)
                        exps(n, False)
                        if it == MAX_ITER - 1:
                            project(b, "O")
            with act.Fori(0, NG) as g:
                mixture(g + NG)

        @block.tensor
        def _(pe):
            mm = pe.matmul

            def tr(dst, src, k=P):
                return pe.transpose(dst, src, ident[0:k, 0:k])

            def tokens_t(pre, n, src, dst, tiles):
                pe.wait_ge(sem(pre + "_y"), n * tiles + tiles)
                for t in range(tiles):
                    last = tr(dst[:, t * P:(t + 1) * P], src[:, t, :])
                last.then_inc(sem(pre + "_yt"), 1)

            def ffn(n):
                tokens_t("F", n, y, ps_m[:, 0, :], NT)
                pe.wait_ge(sem("F_xr"), n + 1)
                for t in range(NT):
                    last = mm(ps_m[:, 1, t * P:(t + 1) * P], xr[:, t * P:(t + 1) * P], w_t[:, W_R, :],
                              start=True, stop=True)
                last.then_inc(sem("F_r"), 1)
                pe.wait_ge(sem("F_xk"), n + 1)
                mm(ps_o[:, 0, 0:T], w_t[:, W_K, :], xk[:, :], start=True, stop=True).then_inc(sem("F_k"), 1)
                pe.wait_ge(sem("F_ka"), n + 1)
                for t in range(NT):
                    last = mm(ps_m[:, 0, t * P:(t + 1) * P], ka[:, t * P:(t + 1) * P], w_t[:, W_V, :],
                              start=True, stop=True)
                last.then_inc(sem("F_v"), 1)

            def causal_front(n):
                tokens_t("G", n, y, ps_m[:, 0, :], NT)
                pe.wait_ge(sem("G_ytc"), n + 1)
                mm(ps_m[:, 1, 0:T], w_t[:, W_Q0, :], z_t[:, :], start=True, stop=True)
                mm(ps_m[:, 1, T:2 * T], w_t[:, W_K0, :], z_t[:, :], start=True, stop=True).then_inc(sem("G_qk"), 1)
                for t in range(NT):
                    last = mm(ps_o[:, 0, t * P:(t + 1) * P], z_t[:, t * P:(t + 1) * P], w_t[:, W_V0, :],
                              start=True, stop=True)
                last.then_inc(sem("G_v"), 1)

            def focus_front(n, b, first):
                f = n - B
                if first:
                    pe.wait_ge(sem("I_y"), b * NT + NT)
                    for t in range(NT):
                        last = tr(ps_m[:, 0, t * P:(t + 1) * P], y2[:, t, :])
                    last.then_inc(sem("H_yt"), 1)
                    pe.wait_ge(sem("H_ytc"), b + 1)
                    for bank, w in ((ps_m[:, 1, :], W_Q1), (ps_o[:, 0, :], W_K1), (ps_o[:, 1, :], W_V1)):
                        for t in range(NT):
                            last = mm(bank[:, t * P:(t + 1) * P], z_t[:, t * P:(t + 1) * P], w_t[:, w, :],
                                      start=True, stop=True)
                    last.then_inc(sem("H_qkv"), 1)
                pe.wait_ge(sem("J_q"), f + 1)
                for t in range(NT):
                    last = tr(ps_m[:, 0, t * P:(t + 1) * P], o_prev[:, t * P:(t + 1) * P])
                last.then_inc(sem("J_qt"), 1)
                pe.wait_ge(sem("J_qtc"), f + 1)
                for t in range(NT):
                    last = mm(ps_m[:, 1, t * P:(t + 1) * P], o_t[:, t * P:(t + 1) * P], block_w[:, 0, :],
                              start=True, stop=True)
                last.then_inc(sem("J_qp"), 1)
                pe.wait_ge(sem("J_nrm"), f + 1)
                for s in range(2 if first else 1):
                    for t in range(NT):
                        last = tr(ps_m[:, 0, s * T + t * P:s * T + (t + 1) * P],
                                  nrm[:, s, t, :, :].rearrange("p d h -> p (d h)"))
                last.then_inc(sem("J_nt"), 1)

            def maxima_scores(n, p, causal):
                pe.wait_ge(sem("operands_in"), n * 96 + 96)
                q, k = q_st[p], k_st[p]
                for h in range(H):
                    pe.wait_ge(sem("max_done"), n * H + h + 1)
                    o = ps_q[:, h % 2, :]
                    if causal:
                        mm(o[:, P:3 * P], ident_b[:, :], mask_q[:, :], start=True, stop=False, skip_group_check=True)
                        mm(o[:, 0:2 * P], q[0:ROWS_P1, h, P:2 * P], k[0:ROWS_P1, h, :], start=False, stop=False,
                           skip_group_check=True)
                        last = mm(o[:, 2 * P:3 * P], q[0:ROWS_P1, h, 0:P], k[0:ROWS_P1, h, 0:P], start=False,
                                  stop=True, skip_group_check=True)
                    else:
                        for t in range(NT):
                            last = mm(o[:, t * T:(t + 1) * T], q[0:ROWS_P1, h, t * P:(t + 1) * P],
                                      k[0:ROWS_P1, h, :], start=True, stop=True)
                    last.then_inc(sem("q_scores"), 1)

            def maxima_rows(n, causal):
                if causal:
                    pe.wait_ge(sem("ml_l"), n + 1)
                else:
                    pe.wait_ge(sem("max_done"), n * H + H + 2)
                for t in range(NT):
                    last = tr(ps_m[0:2 * H, 1, t * P:(t + 1) * P], ml[:, t, :, :].rearrange("p m h -> p (m h)"))
                last.then_inc(sem("ml_t"), 1)

            def products(n, p, causal):
                q, k, v = q_st[p], k_st[p], v_st[p]

                def value_sums(g):
                    if causal:
                        pe.wait_ge(sem("clamp_done"), n * (H // 2) + 2 * g + 2 + 2)
                    else:
                        pe.wait_ge(sem("exp_done"), n * H + HG * g + HG + 2)
                    pe.wait_ge(sem("o_evac"), n * (H // HG) + g + 1)
                    o = ps_o[:, g % 2, (g // 2) * T:(g // 2 + 1) * T]
                    e = e_buf[g % 2]
                    for kt in range(NT):
                        for j in range(HG):
                            rows_j = slice(VW * j, VW * j + VW)
                            if causal and kt:
                                last = mm(o[rows_j, P:T], v[:, kt, HG * g + j, :], e[:, j, 0:P], start=False,
                                          stop=True, tile_position=(0, VW * j))
                            elif causal:
                                last = mm(o[rows_j, :], v[:, kt, HG * g + j, :], e[:, j, P:3 * P], start=True,
                                          stop=False, tile_position=(0, VW * j))
                            else:
                                last = mm(o[rows_j, :], v[:, kt, HG * g + j, :], e[:, j, kt * T:(kt + 1) * T],
                                          start=kt == 0, stop=kt == NT - 1, tile_position=(0, VW * j))
                    last.then_inc(sem("values_done"), 1)

                pe.wait_ge(sem("ml_in"), n * 16 + 16)
                pe.wait_ge(sem("values_ready"), n + 1)
                for h in range(H):
                    pe.wait_ge(sem("exp_done"), n * H + h + 1)
                    o = ps_k[:, h % 2, :]
                    if causal:
                        mm(o[:, 0:2 * P], ident_b[:, :], mask_k[:, :], start=True, stop=False, skip_group_check=True)
                        mm(o[:, 0:P], k[0:ROWS_P2, h, P:2 * P], q[0:ROWS_P2, h, P:2 * P], start=False, stop=False,
                           skip_group_check=True)
                        last = mm(o[:, P:3 * P], k[0:ROWS_P2, h, 0:P], q[0:ROWS_P2, h, :], start=False, stop=True,
                                  skip_group_check=True)
                    else:
                        for t in range(NT):
                            last = mm(o[:, t * T:(t + 1) * T], k[0:ROWS_P2, h, t * P:(t + 1) * P],
                                      q[0:ROWS_P2, h, :], start=True, stop=True)
                    last.then_inc(sem("k_scores"), 1)
                    if causal and h % 2:
                        pe.wait_ge(sem("clamp_done"), n * (H // 2) + h // 2 + 1)
                        for j in range(2):
                            last = mm(ps_m[:, h // 2 % 2, j * T:(j + 1) * T], sel_l[0:ROWS_P2, :],
                                      q[0:ROWS_P2, h - 1 + j, :], start=True, stop=True)
                        last.then_inc(sem("floor"), 1)
                    if h == H - 1:
                        last = pe.nop()
                        last.then_inc(sem("operands_free"), 1)
                    if h >= HG + 1 and h % HG == 1:
                        value_sums(h // HG - 1)
                value_sums(H // HG - 1)

            def back(n, p, causal):
                pe.wait_ge(sem("o_evac"), n * (H // HG) + H // HG + 2)
                for t in range(NT):
                    for g in range(H // HG):
                        last = tr(ps_m[:, t, g * P:(g + 1) * P], o_sb[:, g, t * P:(t + 1) * P])
                last.then_inc(sem("o_t"), 1)
                if causal:
                    v = v_st[p]
                    mm(ps_o[:, 0, 0:P], ones[:, :], v[:, 1, :, 0:HD], start=True, stop=True)
                    mm(ps_o[:, 0, P:2 * P], ones[:, :], v[:, 0, :, 0:HD], start=True, stop=False)
                    mm(ps_o[:, 0, P:2 * P], ones[:, :], v[:, 1, :, 0:HD], start=False, stop=True)\
                        .then_inc(sem("v_sums"), 1)

            def project(n, pre, w):
                pe.wait_ge(sem(pre + "_o"), n + 1)
                for t in range(NT):
                    last = tr(ps_m[:, 0, t * P:(t + 1) * P], o_tok[:, t, :, :].rearrange("p h d -> p (h d)"))
                last.then_inc(sem(pre + "_ott"), 1)
                pe.wait_ge(sem(pre + "_otc"), n + 1)
                for t in range(NT):
                    last = mm(ps_m[:, 1, t * P:(t + 1) * P], o_t[:, t * P:(t + 1) * P], w_t[:, w, :],
                              start=True, stop=True)
                last.then_inc(sem(pre + "_proj"), 1)

            def mixture(m):
                tokens_t("M", m, y, ps_m[:, 0, :], GT)
                pe.wait_ge(sem("M_ytc"), m + 1)
                for t in range(GT):
                    last = mm(ps_m[:, 1, t * EXP:(t + 1) * EXP], ym_t[:, t * P:(t + 1) * P], wr[:, :],
                              start=True, stop=True)
                last.then_inc(sem("M_lg"), 1)

                def hidden(e):
                    for f in range(NF):
                        j = e * NF + f
                        pe.wait_ge(sem("M_relu"), m * EXP * NF + j + 1)
                        bank = (ps_q, ps_k)[j % 4 // 2][:, j % 2, :]
                        mm(bank, w1[:, e, f * P:(f + 1) * P], ym_t[:, :], start=True, stop=True)\
                            .then_inc(sem("M_h"), 1)

                def outputs(e):
                    pe.wait_ge(sem("M_relu"), m * EXP * NF + e * NF + NF + 4)
                    pe.wait_ge(sem("M_comb"), m * EXP + e + 1)
                    for t in range(GT):
                        for f in range(NF):
                            last = mm(ps_o[:, e % 2, t * P:(t + 1) * P], h_sb[e % 2][:, f, t * P:(t + 1) * P],
                                      w2[:, e * NF + f, :], start=f == 0, stop=f == NF - 1)
                    last.then_inc(sem("M_out"), 1)

                hidden(0)
                hidden(1)
                pe.wait_ge(sem("M_gate"), m + 1)
                for t in range(GT):
                    last = tr(ps_m[0:EXP, 0, t * P:(t + 1) * P], gate[:, t, :])
                last.then_inc(sem("M_gt"), 1)
                pe.wait_ge(sem("M_gtc"), m + 1)
                for t in range(GT):
                    last = mm(ps_m[:, 1, t * P:(t + 1) * P], gate_t[:, t * P:(t + 1) * P], b2[:, :],
                              start=True, stop=True)
                last.then_inc(sem("M_b2"), 1)
                for e in range(EXP):
                    outputs(e)
                    if e + 2 < EXP:
                        hidden(e + 2)

            pe.wait_ge(sem("consts"), CONSTS)
            pe.wait_ge(sem("loaded"), n_loads)
            for k in range(3):
                if k == 2:
                    pe.wait_ge(sem("w_copied"), 1)
                for j in range(4 * k, min(4 * k + 4, 9)):
                    last = tr(ps_m[:, k % 2, (j % 4) * P:(j % 4 + 1) * P], w_nat[:, j, :])
                last.then_inc(sem("w_trans"), 1)
            pe.wait_ge(sem("w_copied"), 2)
            tr(ps_m[:, 1, 256:256 + EXP * NF], b1_nat[:, :], EXP * NF).then_inc(sem("w_trans"), 1)
            pe.wait_ge(sem("block_nat"), 1)
            for j in range(3):
                last = tr(ps_k[:, 0, j * P:(j + 1) * P], e_buf[0][:, j, 0:P])
            last.then_inc(sem("block_t"), 1)
            pe.wait_ge(sem("block_ready"), 1)
            mm(ps_q[:, 0, 0:P], w_nat[:, 9, :], block_w[:, 1, :], start=True, stop=True)
            mm(ps_q[:, 0, P:2 * P], w_nat[:, 10, :], block_w[:, 2, :], start=True, stop=True)\
                .then_inc(sem("w_block"), 1)
            mm(ps_q[:, 1, 0:P], bv_rep[:, :], block_w[:, 2, :], start=True, stop=True).then_inc(sem("v_bias"), 1)
            pe.wait_ge(sem("w_copied"), 5)

            pe.sem_inc(sem("operands_free"), 2)
            pe.sem_inc(sem("values_done"), 2)
            pe.sem_inc(sem("M_out"), 2)
            with pe.Fori(0, B // 2) as i:
                for p in range(2):
                    n = i * 2 + p
                    ffn(n * 2)
                    causal_front(n)
                    maxima_scores(n, p, True)
                    maxima_rows(n, True)
                    products(n, p, True)
                    back(n, p, True)
                    project(n, "A", W_P0)
                    ffn(n * 2 + 1)
            with pe.Fori(0, NG) as g:
                mixture(g)
            for it in range(MAX_ITER):
                if it:
                    pe.wait_ge(sem("window_in"), 32 * it)
                with pe.Fori(0, B // 2) as i:
                    for p in range(2):
                        b = i * 2 + p
                        n = (1 + it) * B + b
                        focus_front(n, b, it == 0)
                        maxima_scores(n, p, False)
                        maxima_rows(n, False)
                        products(n, p, False)
                        back(n, p, False)
                        if it == MAX_ITER - 1:
                            project(b, "O", W_O1)
                if it < MAX_ITER - 1:
                    pe.wait_ge(sem("d_total"), it + 1)
                    mm(ps_m[:, 0, 0:1], ones[:, :], dtot[:, :], start=True, stop=True).then_inc(sem("d_sum"), 1)
            with pe.Fori(0, NG) as g:
                mixture(g + NG)

        @block.vector
        def _(dve):
            tt, ts, stt, red = dve.tensor_tensor, dve.tensor_scalar, dve.scalar_tensor_tensor, dve.tensor_reduce

            class Steps:

                def __init__(self, name, n, per):
                    self.sem, self.base, self.per, self.k = sem(name), n * per, per, 0

                def __call__(self, ins):
                    ins.then_inc(self.sem, 1)
                    self.k += 1

                def wait(self):
                    dve.wait_ge(self.sem, self.base + self.k)

                def end(self):
                    assert self.k == self.per
                    self.wait()

            def hold():
                dve.sem_inc(sem("held"), 1)

            def layernorm(pre, n, src, dst, tiles):
                for t in range(tiles):
                    dve.bn_stats(st[:, t, :], src(t)).then_inc(sem(pre + "_st"), 1)
                dve.wait_ge(sem(pre + "_st"), n * tiles + tiles)
                hold()
                for t in range(tiles):
                    dve.bn_aggr(mv[:, t, :], st[:, t, :]).then_inc(sem(pre + "_mom"), 1)
                dve.wait_ge(sem(pre + "_rstd"), n + 1)
                for t in range(tiles):
                    ts(dst(t), src(t), mv[:, t, 0:1], rstd[:, t:t + 1], ALU.subtract, ALU.mult)\
                        .then_inc(sem(pre + "_y"), 1)

            def of_x(b):
                return lambda t: x[:, b, t * C:(t + 1) * C]

            def of(buf):
                return lambda t: buf[:, t, :]

            def ffn(n, b):
                hold()
                layernorm("F", n, of_x(b), of(y), NT)
                dve.wait_ge(sem("F_dy"), n + 1)
                stt(xr[:, :], dy[:, :], col(MU_R), y_t[:, 0:T], ALU.mult, ALU.add).then_inc(sem("F_xr"), 1)
                stt(xk[:, :], dy[:, :], col(MU_K), y_t[:, 0:T], ALU.mult, ALU.add).then_inc(sem("F_xk"), 1)
                s = Steps("F_step", n, 4)
                dve.wait_ge(sem("F_er"), n + 1)
                s(ts(er[:, :], er[:, :], 1.0, None, ALU.add))
                s.wait()
                s(dve.reciprocal(rec[:, :], er[:, :]))
                s.wait()
                dve.wait_ge(sem("F_v"), n + 1)
                s(stt(gated[:, :], ps_m[:, 0, 0:T], 0.5, rec[:, :], ALU.mult, ALU.mult))
                s.wait()
                s(tt(x[:, b, :], x[:, b, :], gated[:, :], ALU.add))
                s.end()

            def causal_front(n, p, b):
                hold()
                layernorm("G", n, of_x(b), of(y), NT)
                dve.wait_ge(sem("G_v"), n + 1)
                dve.tensor_copy(v_st[p][:, :, :, 0:HD],
                                ps_o[:, 0, 0:T].rearrange("p (t h d) -> p t h d", t=NT, h=H))\
                    .then_inc(sem("values_ready"), 1)

            def maxima(n, causal):
                for h in range(H):
                    dve.wait_ge(sem("q_scores"), n * H + h + 1)
                    o = ps_q[:, h % 2, :]
                    if causal:
                        red(nmax[:, 1, h:h + 1], o[:, 0:2 * P], AX.X, ALU.max, negate=True)
                        last = red(nmax[:, 0, h:h + 1], o[:, 2 * P:3 * P], AX.X, ALU.max, negate=True)
                    else:
                        last = red(ml[:, :, 0, h], o.rearrange("p (t k) -> p t k", t=NT), AX.X, ALU.max, negate=True)
                    last.then_inc(sem("max_done"), 1)
                if causal:
                    dve.wait_ge(sem("max_done"), n * H + H + 2)
                    ts(ml[:, :, 0, :], nmax[:, :, :], -CLIP, CLIP, ALU.max, ALU.min).then_inc(sem("ml_m"), 1)

            def clamps(n):
                for hp in range(H // 2):
                    dve.wait_ge(sem("exp_done"), n * H + 2 * hp + 2 + 2)
                    dve.wait_ge(sem("floor"), n * (H // 2) + hp + 1)
                    j = 2 * hp % HG
                    e = e_buf[hp // 2 % 2][:, j:j + 2, :]
                    lo = ps_m[:, hp % 2, :].rearrange("p (h q) -> p h q", h=2)
                    stt(e[:, :, 0:P], e[:, :, 0:P], 1.0, lo[:, :, P:T], ALU.min, ALU.max)
                    stt(e[:, :, P:3 * P], e[:, :, P:3 * P], 1.0, lo[:, :, :], ALU.min, ALU.max)\
                        .then_inc(sem("clamp_done"), 1)

            def causal_back(n, b):
                dve.wait_ge(sem("o_t"), n + 1)
                dve.wait_ge(sem("v_sums"), n + 1)
                o = ps_m[:, :, :].rearrange("p t (h w) -> p t h w", w=VW)
                v1 = ps_o[:, 0, 0:P].rearrange("p (h d) -> p h d", h=H)
                vs = ps_o[:, 0, P:2 * P].rearrange("p (h d) -> p h d", h=H)
                low = ml[:, 0, 1, :]
                s = Steps("norm_step", n, 12)
                s(dve.tensor_copy(s_sum[:, :, :], o[:, :, :, HD]))
                s.wait()
                s(stt(s_sum[:, 0, :], low, float(P), s_sum[:, 0, :], ALU.mult, ALU.add))
                s.wait()
                s(ts(s_u[:, :, :], s_sum[:, :, :], DEN_EPS, None, ALU.add))
                s.wait()
                s(ts(s_du[:, :, :], s_u[:, :, :], P_EPS, None, ALU.mult))
                s(stt(s_den[:, :, :], s_u[:, :, :], P_EPS * T, s_sum[:, :, :], ALU.mult, ALU.add))
                s.wait()
                s(dve.reciprocal(s_rec[:, :, :], s_den[:, :, :]))
                for t in range(NT):
                    s(tt(corr[:, t, :, :], s_du[:, t, :].unsqueeze(2).broadcast_to([P, H, HD]), vs, ALU.mult))
                s(tt(corr2[:, :, :], low.unsqueeze(2).broadcast_to([P, H, HD]), v1, ALU.mult))
                s.wait()
                s(tt(corr[:, 0, :, :], corr[:, 0, :, :], corr2[:, :, :], ALU.add))
                s.wait()
                s(tt(corr[:, :, :, :], corr[:, :, :, :], o[:, :, :, 0:HD], ALU.add))
                s.wait()
                s(tt(o_tok[:, :, :, :], corr[:, :, :, :], s_rec[:, :, :].unsqueeze(3).broadcast_to([P, NT, H, HD]),
                     ALU.mult))
                s.end()
                dve.nop().then_inc(sem("A_o"), 1)
                dve.wait_ge(sem("A_proj"), n + 1)
                tt(x[:, b, :], x[:, b, :], ps_m[:, 1, 0:T], ALU.add).then_inc(sem("A_x"), 1)
                dve.wait_ge(sem("A_x"), n + 1)

            def mixture(m, g):
                def of_group(t):
                    return x[:, g * GB + t // NT, t % NT * C:(t % NT + 1) * C]

                hold()
                layernorm("M", m, of_group, of(y), GT)
                s = Steps("M_step", m, 12)
                dve.wait_ge(sem("M_lg"), m + 1)
                s(tt(lg[:, :, :], ps_m[:, 1, 0:GT * EXP].rearrange("p (t e) -> p t e", t=GT),
                     br_row[:, :].unsqueeze(1).broadcast_to([P, GT, EXP]), ALU.add))
                s.wait()
                for t in range(GT):
                    mine = lg[:, t, :].unsqueeze(2).broadcast_to([P, EXP, EXP])
                    other = lg[:, t, :].unsqueeze(1).broadcast_to([P, EXP, EXP])
                    tt(gt_[:, t, :, :], other, mine, ALU.is_gt)
                    last = tt(eq_[:, t, :, :], other, mine, ALU.is_equal)
                s(last)
                s(red(lmax[:, :], lg[:, :, :], AX.X, ALU.max))
                s.wait()
                s(tt(eq_[:, :, :, :], eq_[:, :, :, :], tri[:, :, :].unsqueeze(1).broadcast_to([P, GT, EXP, EXP]), ALU.mult))
                s.wait()
                s(tt(gt_[:, :, :, :], gt_[:, :, :, :], eq_[:, :, :, :], ALU.add))
                s.wait()
                s(red(rank[:, :, :], gt_[:, :, :, :], AX.X, ALU.add))
                s.wait()
                s(tt(eq_[:, :, 0, :], lg[:, :, :], lmax[:, :].unsqueeze(2).broadcast_to([P, GT, EXP]), ALU.subtract))
                s.wait()
                dve.nop().then_inc(sem("M_lmax"), 1)
                dve.wait_ge(sem("M_lexp"), m + 1)
                s(ts(rank[:, :, :], rank[:, :, :], float(2), None, ALU.is_lt))
                s.wait()
                s(tt(lexp[:, :, :], lexp[:, :, :], rank[:, :, :], ALU.mult))
                s.wait()
                s(red(gsum[:, :], lexp[:, :, :], AX.X, ALU.add))
                s.wait()
                s(dve.reciprocal(gsum[:, :], gsum[:, :]))
                s.wait()
                s(tt(gate[:, :, :], lexp[:, :, :], gsum[:, :].unsqueeze(2).broadcast_to([P, GT, EXP]), ALU.mult))
                s.end()
                dve.nop().then_inc(sem("M_gate"), 1)
                dve.wait_ge(sem("M_b2"), m + 1)
                dve.tensor_copy(acc[:, :, :], ps_m[:, 1, :].rearrange("p (t c) -> p t c", t=GT))\
                    .then_inc(sem("M_acc"), 1)
                dve.wait_ge(sem("M_acc"), m + 1)
                for e in range(EXP):
                    dve.wait_ge(sem("M_out"), m * EXP + e + 1 + 2)
                    if e:
                        dve.wait_ge(sem("M_comb"), m * EXP + e + 2)
                    for t in range(GT):
                        last = stt(acc[:, t, :], ps_o[:, e % 2, t * P:(t + 1) * P], gate[:, t, e:e + 1], acc[:, t, :],
                                   ALU.mult, ALU.add)
                    last.then_inc(sem("M_comb"), 1)
                dve.wait_ge(sem("M_comb"), m * EXP + EXP + 2)
                xg = x[:, bass.ds(g * GB, GB), :]
                stt(xg, acc[:, :, :].rearrange("p (b t) c -> p b (t c)", b=GB), 0.5, xg, ALU.mult, ALU.add)\
                    .then_inc(sem("M_x"), 1)
                dve.wait_ge(sem("M_x"), m + 1)

            def tiles(ap):
                return ap.rearrange("p (t c) -> p t c", t=NT)

            def row2(j):
                return rows[:, j, :].unsqueeze(1).broadcast_to([P, NT, C])

            def focus_front(n, p, b, first):
                f = n - B
                if first:
                    hold()
                    layernorm("H", b, of_x(b), of(y), NT)
                    dve.wait_ge(sem("H_y"), b * NT + NT)
                    layernorm("I", b, of(y), of(y2), NT)
                    dve.wait_ge(sem("H_qkv"), b + 1)
                    stt(tiles(qcur[:, b, :]), tiles(ps_m[:, 1, 0:T]), SC, row2(R_BQ), ALU.mult, ALU.add)\
                        .then_inc(sem("H_q"), 1)
                    tt(lin[:, 1, :, :, :].rearrange("p t h d -> p t (h d)"), tiles(ps_o[:, 0, 0:T]), row2(R_LK), ALU.add)\
                        .then_inc(sem("H_k"), 1)
                    tt(tiles(vp_all[:, b, :]), tiles(ps_o[:, 1, 0:T]),
                       v_bias[:, :].unsqueeze(1).broadcast_to([P, NT, C]), ALU.add).then_inc(sem("H_v"), 1)
                    dve.wait_ge(sem("H_v"), b + 1)
                    hold()
                dve.tensor_copy(v_st[p][:, :, :, 0:HD],
                                vp_all[:, b, :].rearrange("p (t h d) -> p t h d", t=NT, h=H))\
                    .then_inc(sem("values_ready"), 1)
                dve.tensor_copy(o_prev[:, :], qcur[:, b, :]).then_inc(sem("J_q"), 1)
                sc = 2 if first else 1
                w = sc * NT * H
                s = Steps("J_step", f, 5 if first else 5)

                def heads(buf):
                    return buf[:, 0:sc, :, :, :].rearrange("p s t h d -> p (s t h) d")

                dve.wait_ge(sem("J_qp"), f + 1)
                s(tt(lin[:, 0, :, :, :].rearrange("p t h d -> p t (h d)"), tiles(ps_m[:, 1, 0:T]), row2(R_LQ), ALU.add))
                s.wait()
                s(red(hsum[:, 0:w], heads(lin), AX.X, ALU.add))
                s.wait()
                s(stt(heads(cen), hsum[:, 0:w].unsqueeze(2).broadcast_to([P, w, HD]), -1.0 / HD, heads(lin),
                      ALU.mult, ALU.add))
                s.wait()
                s(tt(heads(sqr), heads(cen), heads(cen), ALU.mult))
                s.wait()
                red(hvar[:, 0:w], heads(sqr), AX.X, ALU.add).then_inc(sem("J_mom"), 1)
                dve.wait_ge(sem("J_rstd"), f + 1)
                s(tt(heads(sqr), heads(cen), hrs[:, 0:w].unsqueeze(2).broadcast_to([P, w, HD]), ALU.mult))
                s.end()
                if first:
                    for t in range(NT):
                        tt(nrm[:, 1, t, :, :].rearrange("p d h -> p h d"), sqr[:, 1, t, :, :],
                           rows[:, R_LND, :].rearrange("p (h d) -> p h d", h=H), ALU.mult)
                for t in range(NT):
                    last = stt(nrm[:, 0, t, :, :].rearrange("p d h -> p h d"), sqr[:, 0, t, :, :], c1(QSC),
                               rows[:, R_LNC, :].rearrange("p (h d) -> p h d", h=H), ALU.mult, ALU.mult)
                last.then_inc(sem("J_nrm"), 1)

            def evacuate(n):
                for g in range(H // HG):
                    dve.wait_ge(sem("values_done"), n * (H // HG) + g + 1 + 2)
                    dve.tensor_copy(o_sb[:, g, :], ps_o[:, g % 2, (g // 2) * T:(g // 2 + 1) * T])\
                        .then_inc(sem("o_evac"), 1)

            def focus_back(n, b, it):
                f = n - B
                ot = o_tok[:, :, :, :].rearrange("p t h d -> p (t h d)")
                dve.wait_ge(sem("o_t"), n + 1)
                o = ps_m[:, :, :].rearrange("p t (h w) -> p t h w", w=VW)
                s = Steps("focus_norm", f, 2)
                s(dve.reciprocal(s_rec[:, :, :], o[:, :, :, HD]))
                s.wait()
                s(tt(o_tok[:, :, :, :], o[:, :, :, 0:HD], s_rec[:, :, :].unsqueeze(3).broadcast_to([P, NT, H, HD]),
                     ALU.mult))
                s.end()
                if it:
                    for t in range(NT):
                        last = ts(o_tok[:, t, :, :], o_tok[:, t, :, :], in_win[:, t:t + 1], None, ALU.mult)
                    last.then_inc(sem("windowed"), 1)
                    dve.wait_ge(sem("windowed"), (it - 1) * B + b + 1)
                if it == 0:
                    hold()
                    red(dsum[:, bass.ds(b, 1)], ot, AX.X, ALU.add, apply_absolute_value=True).then_inc(sem("d_part"), 1)
                    dve.tensor_copy(heads_out[:, b, :], ot).then_inc(sem("d_part"), 1)
                    tt(qcur[:, b, :], qcur[:, b, :], ot, ALU.add).then_inc(sem("d_part"), 1)
                    dve.wait_ge(sem("d_part"), b * 3 + 3)
                elif it == 1:
                    tt(o_prev[:, :], ot, heads_out[:, b, :], ALU.subtract).then_inc(sem("d_diff"), 1)
                    tt(qcur[:, b, :], qcur[:, b, :], ot, ALU.add).then_inc(sem("d_diff"), 1)
                    dve.wait_ge(sem("d_diff"), b * 2 + 2)
                    hold()
                    red(dsum[:, bass.ds(b, 1)], o_prev[:, :], AX.X, ALU.add, apply_absolute_value=True)\
                        .then_inc(sem("d_part"), 2)
                    dve.tensor_copy(heads_out[:, b, :], ot).then_inc(sem("d_part"), 1)
                    dve.wait_ge(sem("d_part"), (B + b) * 3 + 3)
                else:
                    ts(o_prev[:, :], heads_out[:, b, :], c1(DONE), None, ALU.mult).then_inc(sem("O_kept"), 1)
                    dve.wait_ge(sem("O_kept"), b + 1)
                    stt(ot, ot, c1(KEEP), o_prev[:, :], ALU.mult, ALU.add).then_inc(sem("O_o"), 1)
                    dve.wait_ge(sem("O_proj"), b + 1)
                    tt(tiles(x[:, b, :]), tiles(x[:, b, :]), tiles(ps_m[:, 1, 0:T]), ALU.add).then_inc(sem("O_x"), 1)
                    dve.wait_ge(sem("O_x"), b * 2 + 1)
                    tt(tiles(x[:, b, :]), tiles(x[:, b, :]), row2(R_BO), ALU.add).then_inc(sem("O_x"), 1)
                    dve.wait_ge(sem("O_x"), b * 2 + 2)

            step_at = [0]

            def link(ins):
                ins.then_inc(sem("control"), 1)
                step_at[0] += 1
                dve.wait_ge(sem("control"), step_at[0])

            def temperature():
                link(ts(c1(TPOS), c1(TMPC), 0.0, None, ALU.is_gt))
                link(tt(c1(T0), c1(TMPC), c1(TPOS), ALU.mult))
                link(ts(c1(T1), c1(TPOS), -1.0, 1.0, ALU.mult, ALU.add))
                link(tt(c1(T1), c1(T1), c1(T0), ALU.add))
                dve.nop().then_inc(sem("t_safe"), 1)

            def floor(dst, scale):
                link(ts(c1(T0), c1(CW), float(np.float32(scale)), None, ALU.mult))
                link(dve.tensor_copy(ctl_i[:, 0:1], c1(T0)))
                link(dve.tensor_copy(c1(dst), ctl_i[:, 0:1]))
                link(tt(c1(T1), c1(dst), c1(T0), ALU.is_gt))
                link(tt(c1(dst), c1(dst), c1(T1), ALU.subtract))

            def control(it):
                link(red(dtot[:, :], dsum[:, :], AX.X, ALU.add))
                dve.nop().then_inc(sem("d_total"), 1)
                dve.wait_ge(sem("d_sum"), it + 1)
                link(ts(c1(DIFF), ps_m[:, 0, 0:1], 1.0 / (B * T * C), None, ALU.mult))
                if it:
                    link(ts(c1(LIM), c1(DIFF), col(FAC), col(THR), ALU.mult, ALU.add))
                    link(tt(c1(DONE), c1(DIFF), c1(LIM), ALU.is_lt))
                    link(ts(c1(KEEP), c1(DONE), -1.0, 1.0, ALU.mult, ALU.add))
                floor(UP, UP_WIN)
                floor(DN, DOWN_WIN)
                link(ts(c1(GUP), c1(DIFF), UP_DIFF, None, ALU.is_gt))
                link(ts(c1(GDN), c1(DIFF), DOWN_DIFF, None, ALU.is_lt))
                link(ts(c1(T0), c1(CW), float(MIN_SIZE), None, ALU.is_gt))
                link(tt(c1(GDN), c1(GDN), c1(T0), ALU.mult))
                link(tt(c1(DN), c1(DN), c1(CW), ALU.subtract))
                link(tt(c1(DN), c1(DN), c1(GDN), ALU.mult))
                link(tt(c1(NW), c1(DN), c1(CW), ALU.add))
                link(tt(c1(UP), c1(UP), c1(NW), ALU.subtract))
                link(tt(c1(UP), c1(UP), c1(GUP), ALU.mult))
                link(tt(c1(NW), c1(NW), c1(UP), ALU.add))
                link(ts(c1(CW), c1(NW), float(MIN_SIZE), float(T), ALU.max, ALU.min))
                link(ts(win_row[:, :], pos_row[:, :], c1(CW), MASKED, ALU.is_ge, ALU.mult))
                dve.nop().then_inc(sem("window_ready"), 1)
                link(ts(in_win[:, :], pos_col[:, :], c1(CW), None, ALU.is_lt))
                link(ts(c1(TMPC), c1(TMPC), 0.005, None, ALU.add))
                temperature()
                dve.wait_ge(sem("t_rs"), it + 2)
                link(ts(c1(QSC), c1(TRS), INV_SQRT, None, ALU.mult))

            dve.sem_inc(sem("max_done"), 2)
            dve.sem_inc(sem("clamp_done"), 2)
            dve.sem_inc(sem("M_comb"), 2)
            dve.sem_inc(sem("o_evac"), 2)
            dve.wait_ge(sem("consts"), CONSTS)
            dve.wait_ge(sem("loaded"), n_loads)
            for j in range(3):
                link(tt(e_buf[0][:, j, 0:P].rearrange("p (h d) -> p h d", h=H), block_mask[:, :, :],
                        head_w[:, j, :].unsqueeze(1).broadcast_to([P, H, HD]), ALU.mult))
            dve.nop().then_inc(sem("block_nat"), 1)
            dve.wait_ge(sem("block_t"), 1)
            for j in range(3):
                link(ts(block_w[:, j, :], ps_k[:, 0, j * P:(j + 1) * P], SC if j == 1 else 1.0, None, ALU.mult))
            link(ts(rows[:, R_BQ, :], rows[:, R_BQ, :], SC, None, ALU.mult))
            link(ts(bv_rep[:, :], ones[:, :], col(BV), None, ALU.mult))
            dve.nop().then_inc(sem("block_ready"), 1)
            dve.wait_ge(sem("v_bias"), 1)
            link(tt(v_bias[:, :], ps_q[:, 1, 0:P], rows[:, R_LV, :], ALU.add))
            link(dve.memset(c1(CW), float(max(min(T, 256), MIN_SIZE))))
            link(dve.tensor_copy(c1(TMPC), col(TMP)))

            with dve.Fori(0, B // 2) as i:
                for p in range(2):
                    n = i * 2 + p
                    ffn(n * 2, n)
                    causal_front(n, p, n)
                    maxima(n, True)
                    clamps(n)
                    causal_back(n, n)
                    ffn(n * 2 + 1, n)
            with dve.Fori(0, NG) as g:
                mixture(g, g)
            link(dve.memset(ml[:, :, 1, :], 0.0))
            temperature()
            dve.wait_ge(sem("t_rs"), 1)
            link(ts(c1(QSC), c1(TRS), INV_SQRT, None, ALU.mult))
            for it in range(MAX_ITER):
                with dve.Fori(0, B // 2) as i:
                    for p in range(2):
                        b = i * 2 + p
                        n = (1 + it) * B + b
                        focus_front(n, p, b, it == 0)
                        maxima(n, False)
                        evacuate(n)
                        focus_back(n, b, it)
                if it < MAX_ITER - 1:
                    control(it)
            with dve.Fori(0, NG) as g:
                mixture(g + NG, g)



_INS = ['L0_attn_x', 'L0_attn_w_qkv', 'L0_attn_w_proj', 'L0_ffn_W_r', 'L0_ffn_W_k', 'L0_ffn_W_v', 'L0_ffn_mu_r',
        'L0_ffn_mu_k', 'L1_attn_Wq', 'L1_attn_bq', 'L1_attn_Wk', 'L1_attn_Wv', 'L1_attn_bv', 'L1_attn_Wo',
        'L1_attn_bo', 'L1_attn_lna_w', 'L1_attn_lnb_w', 'L1_attn_lnc_w', 'L1_attn_lnd_w', 'L1_attn_lq_w',
        'L1_attn_lq_b', 'L1_attn_lk_w', 'L1_attn_lk_b', 'L1_attn_lv_w', 'L1_attn_lv_b', 'L1_attn_threshold',
        'L1_attn_temp_base', 'L1_attn_factor', 'L1_ffn_Wr', 'L1_ffn_br', 'L1_ffn_W1', 'L1_ffn_b1', 'L1_ffn_W2',
        'L1_ffn_b2']


def kernel(**inputs):
    import concourse.bacc as _bacc
    from concourse.bass_utils import run_bass_kernel_spmd as _run

    nc = _bacc.Bacc("TRN2", target_bir_lowering=False, num_devices=1)
    arrays, args = {}, {}
    for name in _INS:
        v = np.ascontiguousarray(inputs[name])
        arrays[f"in_{name}_dram"] = v
        args[name] = nc.dram_tensor(f"in_{name}_dram", v.shape, mybir.dt.from_np(v.dtype), kind="ExternalInput").ap()
    out = nc.dram_tensor("out_0_dram", (B, T, C), F32, kind="ExternalOutput").ap()
    macaron_kernel(nc, args, out)
    r = _run(nc, [arrays], core_ids=[0])
    return r.results[0]["out_0_dram"]
```

```python
from contextlib import ExitStack

import numpy as np

import concourse.bass as bass
from concourse import mybir

F32 = mybir.dt.float32
BF16 = mybir.dt.bfloat16
I32 = mybir.dt.int32
ALU = mybir.AluOpType
ACT = mybir.ActivationFunctionType
AX = mybir.AxisListType

P = 128
B, T, C = 16, 256, 128
H, HD = 16, 8
NT = T // P
EXP, HID = 8, 256
NF = HID // P
GB = 2
GT = GB * NT
NG = B // GB
HG = 4
VW = 32
MIN_SIZE, MAX_ITER = 64, 3
UP_WIN, DOWN_WIN, UP_DIFF, DOWN_DIFF = 1.1, 0.9, 0.05, 0.001
EPS = 1e-5
CLIP, DEN_EPS, P_EPS = 100.0, 1e-6, 1e-8
MASKED = -1.0e30
SAFE = 60.0
SC = HD ** -0.25
INV_SQRT = HD ** -0.5

ROWS_QK = 9 * HD
ROW_WIN = ROWS_QK
ROW_MAX = ROWS_QK + 1
ROWS_P1 = ROWS_QK + 1
ROWS_P2 = ROW_MAX + 6
HP = H // 2
NGV = H // HG
PLANE = C * T

W_Q0, W_K0, W_V0, W_P0, W_R, W_K, W_V, W_Q1, W_O1, W_K1, W_V1, W_LQ = range(12)


def macaron_kernel(nc, a, out):
    ctx = ExitStack()
    with ctx:
        def sb(name, shape, dt=F32):
            return ctx.enter_context(nc.sbuf_tensor(name, shape, dt))

        def pb(name, shape, dt=F32):
            return ctx.enter_context(nc.psum_tensor(name, shape, dt))

        made = {}

        def sem(name):
            if name not in made:
                made[name] = ctx.enter_context(nc.semaphore(name))
            return made[name]

        x = sb("x", [P, B, NT * C])
        qcur = sb("qcur", [P, B, NT * C])
        heads_out = sb("heads_out", [P, B, NT * C])
        vp_all = sb("vp_all", [P, B, NT * C])

        w_t = sb("w_t", [P, 12, C])
        w1 = sb("w1", [P, EXP, HID])
        w2 = sb("w2", [P, EXP * NF, C])
        wr = sb("wr", [P, EXP])
        b2 = sb("b2", [EXP, C])
        b1_nat = sb("b1_nat", [EXP * NF, P])
        b1_t = sb("b1_t", [P, EXP * NF])
        cols = sb("cols", [P, 8])
        MU_R, MU_K, LNA, LNB, BV, THR, TMP, FAC = range(8)
        rows = sb("rows", [P, 7, C])
        R_BQ, R_BO, R_LQ, R_LK, R_LV, R_LNC, R_LND = range(7)
        v_bias = sb("v_bias", [P, C])
        br_row = sb("br_row", [P, EXP])
        head_w = sb("head_w", [P, 3, HD])
        block_w = sb("block_w", [P, 3, C])
        block_mask = sb("block_mask", [P, H, HD])
        bv_rep = sb("bv_rep", [P, P])

        ident = sb("ident", [P, P])
        ident_b = sb("ident_b", [P, P], BF16)
        ones = sb("ones", [P, P])
        ones_b = sb("ones_b", [P, T], BF16)
        mask_q = sb("mask_q", [P, 2 * P], BF16)
        mask_k = sb("mask_k", [P, 2 * P], BF16)
        sel_l = sb("sel_l", [P, P], BF16)
        k_const = sb("k_const", [P, T], BF16)
        pos_row = sb("pos_row", [P, T])
        pos_col = sb("pos_col", [P, NT])
        tri = sb("tri", [P, EXP, EXP])

        st = sb("st", [P, GT, 6])
        mv = sb("mv", [P, GT, 2])
        lnv = sb("lnv", [P, GT])
        rstd = sb("rstd", [P, GT])
        y = sb("y", [P, GT, C])
        y2 = sb("y2", [P, GT, C])
        y3 = sb("y3", [P, GT, C])
        y_t = sb("y_t", [P, 1 + T])
        dy = sb("dy", [P, T])
        xr = sb("xr", [P, T])
        xk = sb("xk", [P, T])
        er = sb("er", [P, T])
        rec = sb("rec", [P, T])
        kr = sb("kr", [P, T])
        ka = sb("ka", [P, T])
        gated = sb("gated", [P, T])
        z_t = sb("z_t", [P, GT * P])
        st_k = sb("st_k", [P, GT, 6])
        mv_k = sb("mv_k", [P, GT, 2])
        lnv_k = sb("lnv_k", [P, GT])
        rstd_k = sb("rstd_k", [P, GT])
        qk32 = sb("qk32", [P, 2, T])
        rest = sb("rest", [P, 2, T])
        parts = sb("parts", [P, 2, 3, T], BF16)
        cen = sb("cen", [P, GT, H, HD])
        sqr = sb("sqr", [P, GT, H, HD])
        nrm = sb("nrm", [P, GT, HD, H])
        hsum = sb("hsum", [P, GT * H])
        hvar = sb("hvar", [P, GT * H])
        hln = sb("hln", [P, GT * H])
        hrs = sb("hrs", [P, GT * H])

        q_st = [sb(f"q_st{p}", [P, H, T], BF16) for p in range(2)]
        k_st = [sb(f"k_st{p}", [P, H, T], BF16) for p in range(2)]
        v_st = [sb(f"v_st{p}", [P, NT, H, VW]) for p in range(2)]
        nmax = sb("nmax", [P, NT, H])
        ml = sb("ml", [P, NT, 2, H])
        ml32 = sb("ml32", [2 * H, T])
        ml_rest = sb("ml_rest", [2 * H, T])
        ml_parts = sb("ml_parts", [2 * H, 3, T], BF16)
        e_buf = [sb(f"e_buf{g}", [P, HG, 2 * T]) for g in range(2)]
        w_nat = e_buf[1].rearrange("p a (b c) -> p (a b) c", c=C)
        o_sb = sb("o_sb", [P, H // HG, T])
        s_sum = sb("s_sum", [P, NT, H])
        s_u = sb("s_u", [P, NT, H])
        s_du = sb("s_du", [P, NT, H])
        s_den = sb("s_den", [P, NT, H])
        s_rec = sb("s_rec", [P, NT, H])
        corr = sb("corr", [P, NT, H, HD])
        corr2 = sb("corr2", [P, H, HD])
        o_tok = sb("o_tok", [P, NT, H, HD])
        o_prev = sb("o_prev", [P, NT * C])
        q_tok = sb("q_tok", [P, NT * C])
        o_t = sb("o_t", [P, T])

        dsum = sb("dsum", [P, B])
        dtot = sb("dtot", [P, 1])
        ctl = sb("ctl", [P, 24])
        DIFF, LIM, DONE, KEEP, CW, UP, DN, GUP, GDN, T0, T1, NW, BND = range(13)
        temps = sb("temps", [P, 5, MAX_ITER])
        TEMP, T_POS, T_SAFE, T_LN, Q_SC = range(5)
        ctl_i = sb("ctl_i", [P, 2], I32)
        path = sb("path", [P, 1], I32)
        in_win = sb("in_win", [P, NT])
        win_row = sb("win_row", [P, T], BF16)

        ym_t = [sb(f"ym_t{i}", [P, GT * P]) for i in range(2)]
        lg = sb("lg", [P, GT, EXP])
        gt_ = sb("gt_", [P, GT, EXP, EXP])
        eq_ = sb("eq_", [P, GT, EXP, EXP])
        rank = sb("rank", [P, GT, EXP])
        lmax = sb("lmax", [P, GT])
        lexp = sb("lexp", [P, GT, EXP])
        gsum = sb("gsum", [P, GT])
        gate = [sb(f"gate{i}", [P, GT, EXP]) for i in range(2)]
        h_sb = [e_buf[i][:, 0:NF, :] for i in range(2)]
        acc = [e_buf[i][:, NF, :].rearrange("p (t c) -> p t c", t=GT) for i in range(2)]
        gate_t = e_buf[1][0:EXP, NF + 1, :]

        ps_q = pb("ps_q", [P, 2, 512])
        ps_k = pb("ps_k", [P, 2, 512])
        ps_o = pb("ps_o", [P, 2, 512])
        ps_m = pb("ps_m", [P, 2, 512])

        scr_q = nc.dram_tensor("scr_q", (2, 3, PLANE), BF16, kind="Internal").ap()
        scr_k = nc.dram_tensor("scr_k", (B, 3, PLANE), BF16, kind="Internal").ap()
        scr_m = nc.dram_tensor("scr_m", (2, 3, 2 * H * T), BF16, kind="Internal").ap()

        def on_all(src, dims):
            return bass.AP(src.tensor, 0, [[0, P]] + dims)

        def col(j):
            return cols[:, j:j + 1]

        def c1(j):
            return ctl[:, j:j + 1]

        SETUP_DMAS = []
        CONSTS = 30
        LAST = MAX_ITER * B

        def follow(n, j, by):
            if isinstance(j, int):
                return (n + by, (j + by) % B) if n + by < LAST else None
            return n + by, j + by

        def fast_steps(eng, it, body):
            n0 = it * B

            def one(j, p, half):
                body(n0 + j, j, p, half + n0 // 2)

            one(0, 0, 0)
            with eng.Fori(0, (B - 4) // 2) as i:
                one(i * 2 + 1, 1, i)
                one(i * 2 + 2, 0, i + 1)
            for j in range(B - 3, B):
                one(j, j % 2, j // 2)

        def mixture_groups(eng, body):
            body(0, 0)
            with eng.Fori(0, (NG - 2) // 2) as i:
                body(i * 2 + 1, 1)
                body(i * 2 + 2, 0)
            body(NG - 1, (NG - 1) % 2)

        def any_path(eng, fast, general):
            eng.wait_ge(sem("path_ready"), 1)
            with eng.If(eng.value_load(path[0:1, 0:1], min_val=0, max_val=1) > 0):
                fast()
            with eng.Else():
                general()

        block = ctx.enter_context(nc.Block())

        @block.sync
        def _(sp):
            loads = sem("loaded")

            def load(dst, src):
                sp.dma_start(dst, src).then_inc(loads, 16)
                SETUP_DMAS.append(1)

            load(w_nat[:, 0:3, :], a["L0_attn_w_qkv"].rearrange("(s o) c -> o s c", s=3))
            for j, name in ((3, "L0_attn_w_proj"), (4, "L0_ffn_W_r"), (5, "L0_ffn_W_k"), (6, "L0_ffn_W_v"),
                            (7, "L1_attn_Wq"), (8, "L1_attn_Wo"), (9, "L1_attn_Wk"), (10, "L1_attn_Wv")):
                load(w_nat[:, j, :], a[name])
            for j, name in ((MU_R, "L0_ffn_mu_r"), (MU_K, "L0_ffn_mu_k"), (LNA, "L1_attn_lna_w"),
                            (LNB, "L1_attn_lnb_w"), (BV, "L1_attn_bv")):
                load(col(j), a[name].rearrange("(p o) -> p o", o=1))
            for j, name in ((THR, "L1_attn_threshold"), (TMP, "L1_attn_temp_base"), (FAC, "L1_attn_factor")):
                load(col(j), on_all(a[name], [[1, 1]]))
            for j, name in ((R_BQ, "L1_attn_bq"), (R_BO, "L1_attn_bo")):
                load(rows[:, j, :], on_all(a[name], [[1, C]]))
            for j, name in ((R_LQ, "L1_attn_lq_b"), (R_LK, "L1_attn_lk_b"), (R_LV, "L1_attn_lv_b"),
                            (R_LNC, "L1_attn_lnc_w"), (R_LND, "L1_attn_lnd_w")):
                load(rows[:, j, :].rearrange("p (h d) -> p h d", h=H), on_all(a[name], [[0, H], [1, HD]]))
            for j, name in enumerate(("L1_attn_lq_w", "L1_attn_lk_w", "L1_attn_lv_w")):
                load(head_w[:, j, :], bass.AP(a[name].tensor, 0, [[0, H], [HD, HD], [1, HD]]))
            load(br_row[:, :], on_all(a["L1_ffn_br"], [[1, EXP]]))
            load(wr[:, :], a["L1_ffn_Wr"])
            load(b1_nat[:, :], a["L1_ffn_b1"].rearrange("e (t p) -> (e t) p", p=P))
            load(b2[:, :], a["L1_ffn_b2"])
            load(x[:, :, :].rearrange("p b (t c) -> p (b t) c", c=C),
                 a["L0_attn_x"].rearrange("b (t p) c -> p (b t) c", p=P))
            load(w1[:, :, :], a["L1_ffn_W1"].rearrange("e h f -> h e f"))
            load(w2[:, :, :], a["L1_ffn_W2"].rearrange("e (t p) h -> p (e t) h", p=P))
            sp.wait_ge(sem("consts"), CONSTS)
            for p in range(2):
                load(k_st[p][ROW_WIN:ROWS_P2, :, :],
                     k_const[ROW_WIN:ROWS_P2, :].unsqueeze(1).broadcast_to([ROWS_P2 - ROW_WIN, H, T]))
                load(q_st[p][ROW_WIN:ROW_WIN + 1, :, :], ones_b[0:1, :].unsqueeze(1).broadcast_to([1, H, T]))

            def operands(n, p, b, with_k):
                sp.wait_ge(sem("parts_ready"), n + 1)
                sp.dma_start(bass.AP(scr_q.tensor, p * 3 * PLANE, [[T, C], [PLANE, 3], [1, T]]),
                             parts[:, 0, :, :]).then_inc(sem("parts_out"), 16)
                if with_k:
                    sp.dma_start(scr_k[b].rearrange("j (c t) -> c j t", t=T),
                                 parts[:, 1, :, :]).then_inc(sem("k_parts_out"), 16)
                    sp.wait_ge(sem("k_parts_out"), n * 16 + 16)
                sp.wait_ge(sem("parts_out"), n * 16 + 16)
                sp.wait_ge(sem("operands_free"), n + 1)
                for j in range(3):
                    sp.dma_start(q_st[p][24 * j:24 * j + 24, :, :].rearrange("r h t -> r (h t)"),
                                 bass.AP(scr_q.tensor, (p * 3 + j) * PLANE, [[0, 3], [H * T, HD], [1, H * T]]))\
                      .then_inc(sem("operands_in"), 16)
                for j in range(3):
                    sp.dma_start(k_st[p][24 * j:24 * j + 24, :, :].rearrange("r h t -> r (h t)"),
                                 scr_k[b].rearrange("j (d n) -> (j d) n", n=H * T))\
                      .then_inc(sem("operands_in"), 16)

            def max_rows(n, p):
                sp.wait_ge(sem("ml_parts_ready"), n + 1)
                sp.dma_start(bass.AP(scr_m.tensor, p * 3 * 2 * H * T, [[T, 2 * H], [2 * H * T, 3], [1, T]]),
                             ml_parts[:, :, :]).then_inc(sem("ml_out"), 16)
                sp.wait_ge(sem("ml_out"), n * 16 + 16)
                sp.dma_start(q_st[p][ROW_MAX:ROWS_P2, :, :].rearrange("r h t -> r (h t)"),
                             bass.AP(scr_m.tensor, p * 3 * 2 * H * T, [[H * T, 6], [1, H * T]]))\
                  .then_inc(sem("ml_in"), 16)

            def key_parts(g):
                sp.wait_ge(sem("K_parts"), g + 1)
                for u in range(GB):
                    sp.dma_start(scr_k[g * GB + u].rearrange("j (c t) -> c j t", t=T),
                                 parts[:, u, :, :]).then_inc(sem("K_out"), 16)

            def fast_operands(f, b, p, half):
                sp.wait_ge(sem("fast_parts"), f + 1)
                sp.dma_start(bass.AP(scr_q.tensor, p * 3 * PLANE, [[T, C], [PLANE, 3], [1, T]]),
                             parts[:, p, :, :]).then_inc(sem("fast_parts_out"), 16)
                if not isinstance(f, int) or f >= 2:
                    sp.wait_ge(sem("fast_scores"), (f - 1) * HP)
                for j in range(3):
                    sp.dma_start(k_st[p][24 * j:24 * j + 24, :, :].rearrange("r h t -> r (h t)"),
                                 scr_k[b].rearrange("j (d n) -> (j d) n", n=H * T))\
                      .then_inc(sem(f"fast_operands_in_{p}"), 16)
                sp.wait_ge(sem("fast_parts_out"), f * 16 + 16 + 32)
                for j in range(3):
                    sp.dma_start(q_st[p][24 * j:24 * j + 24, :, :].rearrange("r h t -> r (h t)"),
                                 bass.AP(scr_q.tensor, (p * 3 + j) * PLANE, [[0, 3], [H * T, HD], [1, H * T]]))\
                      .then_inc(sem(f"fast_operands_in_{p}"), 16)

            def window_rows(it):
                sp.wait_ge(sem("window_ready"), it)
                for p in range(2):
                    sp.dma_start(k_st[p][ROW_WIN:ROW_WIN + 1, :, :],
                                 win_row[0:1, :].unsqueeze(1).broadcast_to([1, H, T]))\
                      .then_inc(sem("window_in"), 16)

            def fast_focus():
                fast_operands(0, 0, 0, 0)
                fast_operands(1, 1, 1, 0)
                for it in range(MAX_ITER):
                    if it:
                        window_rows(it)

                    def body(n, b, p, half):
                        ahead = follow(n, b, 2)
                        if ahead:
                            fast_operands(*ahead, p, half + 1)

                    fast_steps(sp, it, body)

            def general_focus():
                for it in range(MAX_ITER):
                    if it:
                        window_rows(it)
                    with sp.Fori(0, B // 2) as i:
                        for p in range(2):
                            n = (1 + it) * B + i * 2 + p
                            operands(n, p, i * 2 + p, False)
                            max_rows(n, p)

            sp.sem_inc(sem("fast_parts_out"), 32)
            sp.sem_inc(sem("K_out"), 16 * GB)
            with sp.Fori(0, B // 2) as i:
                for p in range(2):
                    operands(i * 2 + p, p, i * 2 + p, True)
                    max_rows(i * 2 + p, p)
            with sp.Fori(0, NG) as g:
                key_parts(g)
            sp.wait_ge(sem("K_out"), (NG + 1) * 16 * GB)
            any_path(sp, fast_focus, general_focus)
            with sp.Fori(0, NG) as g:
                sp.wait_ge(sem("M_x"), NG + g + 1)
                sp.dma_start(out.rearrange("b (t p) c -> p (b t) c", p=P)[:, bass.ds(g * GT, GT), :],
                             x[:, bass.ds(g * GB, GB), :].rearrange("p b (t c) -> p (b t) c", c=C))\
                  .then_inc(sem("stored"), 16)
            sp.wait_ge(sem("stored"), NG * 16)

        n_loads = 16 * len(SETUP_DMAS)

        @block.gpsimd
        def _(pool):
            done = [0]

            def const(ins):
                ins.then_inc(sem("consts"), 1)
                done[0] += 1
                pool.wait_ge(sem("consts"), done[0])

            def select(t, op, fill, base, pattern, step):
                const(pool.affine_select(out=t, in_=t, compare_op=op, fill=fill, base=base, pattern=pattern,
                                         channel_multiplier=step))

            for t in (ident, ident_b, mask_q, mask_k, sel_l, k_const):
                const(pool.memset(t[:, :], 0.0))
            for t in (ones, ones_b):
                const(pool.memset(t[:, :], 1.0))
            for t in (block_mask, tri):
                const(pool.memset(t[:, :, :], 1.0))
            for p in range(2):
                const(pool.memset(v_st[p][:, :, :, :], 0.0))
                const(pool.memset(v_st[p][:, :, :, HD:HD + 1], 1.0))
            const(pool.memset(y_t[:, 0:1], 0.0))
            select(ident[:, :], ALU.not_equal, 1.0, 0, [[-1, P]], 1)
            select(ident_b[:, :], ALU.not_equal, 1.0, 0, [[-1, P]], 1)
            select(mask_q[:, :], ALU.is_ge, MASKED, 0, [[0, 2], [-1, P]], 1)
            select(mask_k[:, :], ALU.is_ge, MASKED, 0, [[0, 2], [1, P]], -1)
            for j in range(3):
                select(k_const[:, :], ALU.not_equal, 1.0, -(ROW_MAX + 2 * j), [[0, T]], 1)
                select(sel_l[:, :], ALU.not_equal, 1.0, -(ROW_MAX + 2 * j + 1), [[0, P]], 1)
            select(block_mask[:, :, :], ALU.is_ge, 0.0, 0, [[-HD, H], [0, HD]], 1)
            select(block_mask[:, :, :], ALU.is_ge, 0.0, HD - 1, [[HD, H], [0, HD]], -1)
            select(tri[:, :, :], ALU.is_gt, 0.0, 0, [[1, EXP], [-1, EXP]], 0)
            const(pool.iota(pos_row[:, :], pattern=[[1, T]], base=0, channel_multiplier=0,
                            allow_small_or_imprecise_dtypes=True))
            const(pool.iota(pos_col[:, :], pattern=[[P, NT]], base=0, channel_multiplier=1,
                            allow_small_or_imprecise_dtypes=True))
            assert done[0] == CONSTS

            def hold():
                pool.sem_inc(sem("pool_held"), 1)

            def ffn(n, l):
                pool.wait_ge(sem("T_ytc"), l + 1)
                pool.tensor_tensor(dy[:, :], y_t[:, 1:T + 1], y_t[:, 0:T], ALU.subtract).then_inc(sem("F_dy"), 1)
                pool.wait_ge(sem("F_kr"), n + 1)
                pool.tensor_tensor(ka[:, :], kr[:, :], kr[:, :], ALU.mult).then_inc(sem("F_ka"), 1)

            def split(n, s):
                pool.wait_ge(sem("part_hi"), n + 1)
                pool.tensor_tensor(rest[:, 0:s, :], qk32[:, 0:s, :], parts[:, 0:s, 0, :], ALU.subtract)\
                    .then_inc(sem("part_rest"), 1)
                pool.wait_ge(sem("part_mid"), n + 1)
                pool.tensor_tensor(parts[:, 0:s, 2, :], rest[:, 0:s, :], parts[:, 0:s, 1, :], ALU.subtract)\
                    .then_inc(sem("parts_ready"), 1)

            def maxima(n):
                pool.wait_ge(sem("ml_hi"), n + 1)
                pool.tensor_tensor(ml_rest[:, :], ml32[:, :], ml_parts[:, 0, :], ALU.subtract)\
                    .then_inc(sem("ml_rest"), 1)
                pool.wait_ge(sem("ml_mid"), n + 1)
                pool.tensor_tensor(ml_parts[:, 2, :], ml_rest[:, :], ml_parts[:, 1, :], ALU.subtract)\
                    .then_inc(sem("ml_parts_ready"), 1)

            with pool.Fori(0, B // 2) as i:
                for p in range(2):
                    n = i * 2 + p
                    ffn(n * 2, n * 3)
                    split(n, 2)
                    maxima(n)
                    ffn(n * 2 + 1, n * 3 + 2)

            def key_parts(g):
                pool.wait_ge(sem("K_hi"), g + 1 + 1)
                pool.tensor_tensor(rest[:, :, :], qk32[:, :, :], parts[:, :, 0, :], ALU.subtract)\
                    .then_inc(sem("K_rest"), 1)
                pool.wait_ge(sem("K_rest"), g + 1)
                hold()
                pool.tensor_copy(parts[:, :, 1, :], rest[:, :, :]).then_inc(sem("K_mid"), 1)
                pool.wait_ge(sem("K_mid"), g + 1)
                pool.tensor_tensor(parts[:, :, 2, :], rest[:, :, :], parts[:, :, 1, :], ALU.subtract)\
                    .then_inc(sem("K_parts"), 1)

            with pool.Fori(0, NG) as g:
                key_parts(g)

            def queries(f, b):
                pool.wait_ge(sem("query_t"), f + 1)
                pool.wait_ge(sem("fast_q_new"), f + 1)
                hold()
                pool.tensor_copy(q_tok[:, :], qcur[:, b, :]).then_inc(sem("query_tok"), 1)

            def values(n, b, p):
                if not isinstance(n, int) or n >= 2:
                    pool.wait_ge(sem("fast_values"), (n - 1) * NGV + 2)
                hold()
                pool.tensor_copy(v_st[p][:, :, :, 0:HD],
                                 vp_all[:, b, :].rearrange("p (t h d) -> p t h d", t=NT, h=H))\
                    .then_inc(sem("fast_v"), 1)

            def query_parts(f, p):
                pool.wait_ge(sem("fast_hi"), f + 1 + 1)
                pool.tensor_tensor(rest[:, p, :], qk32[:, p, :], parts[:, p, 0, :], ALU.subtract)\
                    .then_inc(sem("fast_rest"), 1)
                pool.wait_ge(sem("fast_rest"), f + 1)
                hold()
                pool.tensor_copy(parts[:, p, 1, :], rest[:, p, :]).then_inc(sem("fast_mid"), 1)
                pool.wait_ge(sem("fast_mid"), f + 1)
                pool.tensor_tensor(parts[:, p, 2, :], rest[:, p, :], parts[:, p, 1, :], ALU.subtract)\
                    .then_inc(sem("fast_parts"), 1)

            def update(n, b, it):
                ot = o_tok[:, :, :, :].rearrange("p t h d -> p (t h d)")
                if it < MAX_ITER - 1:
                    pool.wait_ge(sem("d_part"), n + 1)
                    hold()
                    pool.tensor_copy(heads_out[:, b, :], ot)
                    pool.tensor_tensor(qcur[:, b, :], qcur[:, b, :], ot, ALU.add).then_inc(sem("fast_q_new"), 1)
                else:
                    xb = x[:, b, :].rearrange("p (t c) -> p t c", t=NT)
                    pool.tensor_tensor(xb, xb, rows[:, R_BO, :].unsqueeze(1).broadcast_to([P, NT, C]), ALU.add)\
                        .then_inc(sem("fast_bias"), 1)

            def fast_focus():
                pool.sem_inc(sem("query_t"), 1)
                pool.sem_inc(sem("fast_q_new"), B)
                pool.wait_ge(sem("K_v"), NG)
                queries(0, 0)
                values(0, 0, 0)
                query_parts(0, 0)
                queries(1, 1)
                query_parts(1, 1)
                queries(2, 2)
                for it in range(MAX_ITER):
                    def body(n, b, p, half):
                        after = follow(n, b, 1)
                        if after:
                            values(*after, 1 - p)
                        if not (isinstance(b, int) and b == 0):
                            update(n - 1, b - 1, it)
                        ahead = follow(n, b, 2)
                        if ahead:
                            query_parts(ahead[0], p)
                        ahead = follow(n, b, 3)
                        if ahead:
                            queries(*ahead)

                    fast_steps(pool, it, body)
                    update(it * B + B - 1, B - 1, it)

            def general_focus():
                for it in range(MAX_ITER):
                    with pool.Fori(0, B // 2) as i:
                        for p in range(2):
                            n = (1 + it) * B + i * 2 + p
                            split(n, 1)
                            maxima(n)

            any_path(pool, fast_focus, general_focus)

        @block.scalar
        def _(act):
            act.preload_act_table_set("natural_log_exp_and_others")
            act.wait_ge(sem("consts"), CONSTS)

            def copy(dst, src, scale=1.0):
                return act.activation(dst, src, ACT.Copy, scale=scale)

            def rsqrt(pre, n, per, var, tmp, res, scale=1.0):
                act.wait_ge(sem(pre + "_mom"), n * per + per)
                act.activation(tmp, var, ACT.Ln, scale=scale, bias=EPS).then_inc(sem(pre + "_ln"), 1)
                act.wait_ge(sem(pre + "_ln"), n + 1)
                act.activation(res, tmp, ACT.Exp, scale=-0.5).then_inc(sem(pre + "_rstd"), 1)

            def ffn(n, l):
                rsqrt("T", l, NT, mv[:, 0:NT, 1], lnv[:, 0:NT], rstd[:, 0:NT])
                act.wait_ge(sem("T_yt"), l + 1)
                copy(y_t[:, 1:T + 1], ps_m[:, 0, 0:T]).then_inc(sem("T_ytc"), 1)
                act.wait_ge(sem("F_r"), n + 1)
                act.activation(er[:, :], ps_m[:, 1, 0:T], ACT.Exp, scale=-1.0).then_inc(sem("F_er"), 1)
                act.wait_ge(sem("F_k"), n + 1)
                act.activation(kr[:, :], ps_o[:, 0, 0:T], ACT.Relu).then_inc(sem("F_kr"), 1)

            def split(n, s):
                act.wait_ge(sem("qk32"), n * 2 + 2)
                copy(parts[:, 0:s, 0, :], qk32[:, 0:s, :]).then_inc(sem("part_hi"), 1)
                act.wait_ge(sem("part_rest"), n + 1)
                copy(parts[:, 0:s, 1, :], rest[:, 0:s, :]).then_inc(sem("part_mid"), 1)

            def causal_front(n, l):
                rsqrt("T", l, NT, mv[:, 0:NT, 1], lnv[:, 0:NT], rstd[:, 0:NT])
                act.wait_ge(sem("T_yt"), l + 1)
                copy(z_t[:, 0:T], ps_m[:, 0, 0:T]).then_inc(sem("T_ytc"), 1)
                act.wait_ge(sem("G_qk"), n + 1)
                copy(qk32[:, 0, :], ps_m[:, 1, 0:T], INV_SQRT).then_inc(sem("qk32"), 1)
                copy(qk32[:, 1, :], ps_m[:, 1, T:2 * T]).then_inc(sem("qk32"), 1)
                split(n, 2)

            def focus_front(n):
                f = n - B
                act.wait_ge(sem("query_t"), f + 1)
                copy(o_t[:, :], ps_m[:, 0, 0:T]).then_inc(sem("query_tc"), 1)
                w = NT * H
                rsqrt("query", f, 1, hvar[:, 0:w], hln[:, 0:w], hrs[:, 0:w], 1.0 / HD)
                act.wait_ge(sem("query_nt"), f + 1)
                copy(qk32[:, 0, :], ps_m[:, 0, 0:T]).then_inc(sem("qk32"), 2)
                split(n, 1)

            def maxima(n, causal):
                if causal:
                    act.wait_ge(sem("ml_m"), n + 1)
                    act.activation(ml[:, :, 1, :], ml[:, :, 0, :], ACT.Exp, bias=-CLIP).then_inc(sem("ml_l"), 1)
                act.wait_ge(sem("ml_t"), n + 1)
                copy(ml32[:, :], ps_m[0:2 * H, 1, 0:T]).then_inc(sem("ml32"), 1)
                act.wait_ge(sem("ml32"), n + 1)
                copy(ml_parts[:, 0, :], ml32[:, :]).then_inc(sem("ml_hi"), 1)
                act.wait_ge(sem("ml_rest"), n + 1)
                copy(ml_parts[:, 1, :], ml_rest[:, :]).then_inc(sem("ml_mid"), 1)

            def exps(n, causal):
                w = 3 * P if causal else 2 * T
                for h in range(H):
                    g = h // HG
                    if h % HG == 0:
                        act.wait_ge(sem("values_done"), n * (H // HG) + g + 1)
                    act.wait_ge(sem("k_scores"), n * H + h + 1)
                    act.activation(e_buf[g % 2][:, h % HG, 0:w], ps_k[:, h % 2, 0:w], ACT.Exp)\
                        .then_inc(sem("exp_done"), 1)
                    if causal and h % HG == HG - 1 and g >= 1:
                        evacuate(n, g - 1)
                if causal:
                    evacuate(n, H // HG - 1)

            def evacuate(n, g):
                act.wait_ge(sem("values_done"), n * (H // HG) + g + 1 + 2)
                copy(o_sb[:, g, :], ps_o[:, g % 2, (g // 2) * T:(g // 2 + 1) * T]).then_inc(sem("o_evac"), 1)

            def project(n, pre):
                act.wait_ge(sem(pre + "_ott"), n + 1)
                copy(o_t[:, :], ps_m[:, 0, 0:T]).then_inc(sem(pre + "_otc"), 1)

            def mix_tokens(m, u):
                act.wait_ge(sem("M_yt"), m + 1)
                copy(ym_t[u][:, :], ps_m[:, 0, :]).then_inc(sem("M_ytc"), 1)

            def mix_logits(m):
                act.wait_ge(sem("M_lmax"), m + 1)
                act.activation(lexp[:, :, :], eq_[:, :, 0, :], ACT.Exp).then_inc(sem("M_lexp"), 1)

            def mix_gates(m):
                act.wait_ge(sem("M_gt"), m + 1)
                copy(gate_t, ps_m[0:EXP, 0, :]).then_inc(sem("M_gtc"), 1)

            def mix_norm(m):
                rsqrt("M", m, GT, mv[:, :, 1], lnv[:, :], rstd[:, :])

            def mix_front(m, u):
                mix_norm(m)
                mix_tokens(m, u)
                mix_logits(m)
                mix_gates(m)

            def hidden(m, e):
                act.wait_ge(sem("M_out"), m * EXP + e + 1)
                for f in range(NF):
                    j = e * NF + f
                    act.wait_ge(sem("M_h"), m * EXP * NF + j + 1)
                    bank = (ps_q, ps_k)[j % 4 // 2][:, j % 2, :]
                    act.activation(h_sb[e % 2][:, f, :], bank, ACT.Relu, bias=b1_t[:, j:j + 1])\
                        .then_inc(sem("M_relu"), 1)

            def key_norm(k):
                rsqrt("KN", k, GT, mv_k[:, :, 1], lnv_k[:, :], rstd_k[:, :])

            def key_tokens(g):
                act.wait_ge(sem("K_yt"), g + 1)
                copy(z_t[:, :], ps_m[:, 1, :]).then_inc(sem("K_ytc"), 1)

            def key_heads(g):
                rsqrt("K", g, 1, hvar[:, :], hln[:, :], hrs[:, :], 1.0 / HD)

            def key_parts(g):
                act.wait_ge(sem("K_nt"), g + 1)
                act.wait_ge(sem("K_out"), g * 16 * GB + 16 * GB)
                src = ps_m[:, 1, :].rearrange("p (b t) -> p b t", b=GB)
                copy(qk32[:, :, :], src)
                copy(parts[:, :, 0, :], src).then_inc(sem("K_hi"), 1)

            def mixture(g, u, base, keys):
                m = base + g
                front = not isinstance(g, int) or g < NG - 1
                before = keys and not (isinstance(g, int) and g == 0)
                hidden(m, 0)
                if before:
                    key_norm((g - 1) * 2)
                hidden(m, 1)
                if front:
                    mix_norm(m + 1)
                hidden(m, 2)
                if front:
                    mix_tokens(m + 1, 1 - u)
                if before:
                    key_norm((g - 1) * 2 + 1)
                hidden(m, 3)
                if before:
                    key_tokens(g - 1)
                hidden(m, 4)
                if front:
                    mix_logits(m + 1)
                hidden(m, 5)
                if front:
                    mix_gates(m + 1)
                hidden(m, 6)
                if before:
                    key_heads(g - 1)
                hidden(m, 7)
                if before:
                    key_parts(g - 1)

            def front_heads(f):
                rsqrt("query", f, 1, hvar[:, 0:NT * H], hln[:, 0:NT * H], hrs[:, 0:NT * H], 1.0 / HD)

            def pair_exps(n, hp):
                g = hp * 2 // HG
                if hp * 2 % HG == 0:
                    act.wait_ge(sem("fast_values"), n * NGV + g + 1)
                act.wait_ge(sem("fast_scores"), n * HP + hp + 1)
                act.activation(e_buf[g % 2][:, hp * 2 % HG:hp * 2 % HG + 2, :], (ps_q, ps_k)[hp % 2][:, :, :],
                               ACT.Exp).then_inc(sem("fast_exp"), 1)

            def fast_focus():
                act.sem_inc(sem("fast_exp"), 2)
                front_heads(0)
                front_heads(1)
                for it in range(MAX_ITER):
                    def body(n, b, p, half):
                        ahead = follow(n, b, 2)
                        for hp in range(HP):
                            pair_exps(n, hp)
                            if hp == 3 and ahead:
                                front_heads(ahead[0])

                    fast_steps(act, it, body)

            def general_focus():
                for it in range(MAX_ITER):
                    with act.Fori(0, B // 2) as i:
                        for p in range(2):
                            b = i * 2 + p
                            n = (1 + it) * B + b
                            focus_front(n)
                            maxima(n, False)
                            exps(n, False)
                            if it == MAX_ITER - 1:
                                project(b, "O")

            for k in range(3):
                act.wait_ge(sem("setup_tensor"), k + 1)
                for j in range(4 * k, min(4 * k + 4, 9)):
                    src = ps_m[:, k % 2, (j % 4) * P:(j % 4 + 1) * P]
                    dst = w_t[:, j, :]
                    if j in (W_Q0, W_K0):
                        src = src.rearrange("p (h d) -> p h d", h=H)
                        dst = dst.rearrange("p (d h) -> p h d", h=H)
                    if j == W_Q1:
                        last = act.activation(dst, src, ACT.Copy, scale=col(LNA))
                    else:
                        last = copy(dst, src)
                last.then_inc(sem("setup_scalar"), 1)
            act.wait_ge(sem("setup_tensor"), 4)
            copy(b1_t[:, :], ps_m[:, 1, 256:256 + EXP * NF]).then_inc(sem("setup_scalar"), 1)
            act.wait_ge(sem("setup_tensor"), 6)
            act.activation(w_t[:, W_K1, :], ps_q[:, 0, 0:P], ACT.Copy, scale=col(LNB))
            act.activation(w_t[:, W_V1, :], ps_q[:, 0, P:2 * P], ACT.Copy, scale=col(LNB)).then_inc(sem("setup_scalar"), 1)

            act.wait_ge(sem("setup_vector"), 3)
            act.activation(temps[:, T_LN, :], temps[:, T_SAFE, :], ACT.Ln).then_inc(sem("setup_scalar"), 1)
            act.wait_ge(sem("setup_scalar"), 6)
            act.activation(temps[:, Q_SC, :], temps[:, T_LN, :], ACT.Exp, scale=-0.5).then_inc(sem("setup_scalar"), 1)

            act.sem_inc(sem("exp_done"), 2)
            act.sem_inc(sem("M_relu"), 4)
            with act.Fori(0, B // 2) as i:
                for p in range(2):
                    n = i * 2 + p
                    ffn(n * 2, n * 3)
                    causal_front(n, n * 3 + 1)
                    maxima(n, True)
                    exps(n, True)
                    project(n, "A")
                    ffn(n * 2 + 1, n * 3 + 2)
            mix_front(0, 0)
            mixture_groups(act, lambda g, u: mixture(g, u, 0, True))
            key_norm((NG - 1) * 2)
            key_norm((NG - 1) * 2 + 1)
            key_tokens(NG - 1)
            key_heads(NG - 1)
            key_parts(NG - 1)
            act.wait_ge(sem("K_out"), (NG + 1) * 16 * GB)
            any_path(act, fast_focus, general_focus)
            mix_front(NG, 0)
            mixture_groups(act, lambda g, u: mixture(g, u, NG, False))

        @block.tensor
        def _(pe):
            mm = pe.matmul

            def tr(dst, src, k=P):
                return pe.transpose(dst, src, ident[0:k, 0:k])

            def tokens_t(pre, n, src, dst, tiles):
                pe.wait_ge(sem(pre + "_y"), n * tiles + tiles)
                for t in range(tiles):
                    last = tr(dst[:, t * P:(t + 1) * P], src[:, t, :])
                last.then_inc(sem(pre + "_yt"), 1)

            def ffn(n, l):
                tokens_t("T", l, y, ps_m[:, 0, :], NT)
                pe.wait_ge(sem("F_xr"), n + 1)
                for t in range(NT):
                    last = mm(ps_m[:, 1, t * P:(t + 1) * P], xr[:, t * P:(t + 1) * P], w_t[:, W_R, :],
                              start=True, stop=True)
                last.then_inc(sem("F_r"), 1)
                pe.wait_ge(sem("F_xk"), n + 1)
                mm(ps_o[:, 0, 0:T], w_t[:, W_K, :], xk[:, :], start=True, stop=True).then_inc(sem("F_k"), 1)
                pe.wait_ge(sem("F_ka"), n + 1)
                for t in range(NT):
                    last = mm(ps_m[:, 0, t * P:(t + 1) * P], ka[:, t * P:(t + 1) * P], w_t[:, W_V, :],
                              start=True, stop=True)
                last.then_inc(sem("F_v"), 1)

            def causal_front(n, l):
                tokens_t("T", l, y, ps_m[:, 0, :], NT)
                pe.wait_ge(sem("T_ytc"), l + 1)
                mm(ps_m[:, 1, 0:T], w_t[:, W_Q0, :], z_t[:, 0:T], start=True, stop=True)
                mm(ps_m[:, 1, T:2 * T], w_t[:, W_K0, :], z_t[:, 0:T], start=True, stop=True).then_inc(sem("G_qk"), 1)
                for t in range(NT):
                    last = mm(ps_o[:, 0, t * P:(t + 1) * P], z_t[:, t * P:(t + 1) * P], w_t[:, W_V0, :],
                              start=True, stop=True)
                last.then_inc(sem("G_v"), 1)

            def focus_front(n):
                f = n - B
                pe.wait_ge(sem("query_tok"), f + 1)
                for t in range(NT):
                    last = tr(ps_m[:, 0, t * P:(t + 1) * P], o_prev[:, t * P:(t + 1) * P])
                last.then_inc(sem("query_t"), 1)
                pe.wait_ge(sem("query_tc"), f + 1)
                for t in range(NT):
                    last = mm(ps_m[:, 1, t * P:(t + 1) * P], o_t[:, t * P:(t + 1) * P], block_w[:, 0, :],
                              start=True, stop=True)
                last.then_inc(sem("query_ps"), 1)
                pe.wait_ge(sem("query_nrm"), f + 1)
                for t in range(NT):
                    last = tr(ps_m[:, 0, t * P:(t + 1) * P], nrm[:, t, :, :].rearrange("p d h -> p (d h)"))
                last.then_inc(sem("query_nt"), 1)

            def maxima_scores(n, p, causal):
                pe.wait_ge(sem("operands_in"), n * 96 + 96)
                q, k = q_st[p], k_st[p]
                for h in range(H):
                    pe.wait_ge(sem("max_done"), n * H + h + 1)
                    o = ps_q[:, h % 2, :]
                    if causal:
                        mm(o[:, P:3 * P], ident_b[:, :], mask_q[:, :], start=True, stop=False, skip_group_check=True)
                        mm(o[:, 0:2 * P], q[0:ROWS_P1, h, P:2 * P], k[0:ROWS_P1, h, :], start=False, stop=False,
                           skip_group_check=True)
                        last = mm(o[:, 2 * P:3 * P], q[0:ROWS_P1, h, 0:P], k[0:ROWS_P1, h, 0:P], start=False,
                                  stop=True, skip_group_check=True)
                    else:
                        for t in range(NT):
                            last = mm(o[:, t * T:(t + 1) * T], q[0:ROWS_P1, h, t * P:(t + 1) * P],
                                      k[0:ROWS_P1, h, :], start=True, stop=True)
                    last.then_inc(sem("q_scores"), 1)

            def maxima_rows(n, causal):
                if causal:
                    pe.wait_ge(sem("ml_l"), n + 1)
                else:
                    pe.wait_ge(sem("max_done"), n * H + H + 2)
                for t in range(NT):
                    last = tr(ps_m[0:2 * H, 1, t * P:(t + 1) * P], ml[:, t, :, :].rearrange("p m h -> p (m h)"))
                last.then_inc(sem("ml_t"), 1)

            def products(n, p, causal):
                q, k, v = q_st[p], k_st[p], v_st[p]

                def value_sums(g):
                    if causal:
                        pe.wait_ge(sem("clamp_done"), n * (H // 2) + 2 * g + 2 + 2)
                    else:
                        pe.wait_ge(sem("exp_done"), n * H + HG * g + HG + 2)
                    pe.wait_ge(sem("o_evac"), n * (H // HG) + g + 1)
                    o = ps_o[:, g % 2, (g // 2) * T:(g // 2 + 1) * T]
                    e = e_buf[g % 2]
                    for kt in range(NT):
                        for j in range(HG):
                            rows_j = slice(VW * j, VW * j + VW)
                            if causal and kt:
                                last = mm(o[rows_j, P:T], v[:, kt, HG * g + j, :], e[:, j, 0:P], start=False,
                                          stop=True, tile_position=(0, VW * j))
                            elif causal:
                                last = mm(o[rows_j, :], v[:, kt, HG * g + j, :], e[:, j, P:3 * P], start=True,
                                          stop=False, tile_position=(0, VW * j))
                            else:
                                last = mm(o[rows_j, :], v[:, kt, HG * g + j, :], e[:, j, kt * T:(kt + 1) * T],
                                          start=kt == 0, stop=kt == NT - 1, tile_position=(0, VW * j))
                    last.then_inc(sem("values_done"), 1)

                pe.wait_ge(sem("ml_in"), n * 16 + 16)
                pe.wait_ge(sem("values_ready"), n + 1)
                for h in range(H):
                    pe.wait_ge(sem("exp_done"), n * H + h + 1)
                    o = ps_k[:, h % 2, :]
                    if causal:
                        mm(o[:, 0:2 * P], ident_b[:, :], mask_k[:, :], start=True, stop=False, skip_group_check=True)
                        mm(o[:, 0:P], k[0:ROWS_P2, h, P:2 * P], q[0:ROWS_P2, h, P:2 * P], start=False, stop=False,
                           skip_group_check=True)
                        last = mm(o[:, P:3 * P], k[0:ROWS_P2, h, 0:P], q[0:ROWS_P2, h, :], start=False, stop=True,
                                  skip_group_check=True)
                    else:
                        for t in range(NT):
                            last = mm(o[:, t * T:(t + 1) * T], k[0:ROWS_P2, h, t * P:(t + 1) * P],
                                      q[0:ROWS_P2, h, :], start=True, stop=True)
                    last.then_inc(sem("k_scores"), 1)
                    if causal and h % 2:
                        pe.wait_ge(sem("clamp_done"), n * (H // 2) + h // 2 + 1)
                        for j in range(2):
                            last = mm(ps_m[:, h // 2 % 2, j * T:(j + 1) * T], sel_l[0:ROWS_P2, :],
                                      q[0:ROWS_P2, h - 1 + j, :], start=True, stop=True)
                        last.then_inc(sem("floor"), 1)
                    if h == H - 1:
                        last = pe.nop()
                        last.then_inc(sem("operands_free"), 1)
                    if h >= HG + 1 and h % HG == 1:
                        value_sums(h // HG - 1)
                value_sums(H // HG - 1)

            def back(n, p, causal):
                pe.wait_ge(sem("o_evac"), n * (H // HG) + H // HG + 2)
                for t in range(NT):
                    for g in range(H // HG):
                        last = tr(ps_m[:, t, g * P:(g + 1) * P], o_sb[:, g, t * P:(t + 1) * P])
                last.then_inc(sem("o_t"), 1)
                if causal:
                    v = v_st[p]
                    mm(ps_o[:, 0, 0:P], ones[:, :], v[:, 1, :, 0:HD], start=True, stop=True)
                    mm(ps_o[:, 0, P:2 * P], ones[:, :], v[:, 0, :, 0:HD], start=True, stop=False)
                    mm(ps_o[:, 0, P:2 * P], ones[:, :], v[:, 1, :, 0:HD], start=False, stop=True)\
                        .then_inc(sem("v_sums"), 1)

            def project(n, pre, w):
                pe.wait_ge(sem(pre + "_o"), n + 1)
                for t in range(NT):
                    last = tr(ps_m[:, 0, t * P:(t + 1) * P], o_tok[:, t, :, :].rearrange("p h d -> p (h d)"))
                last.then_inc(sem(pre + "_ott"), 1)
                pe.wait_ge(sem(pre + "_otc"), n + 1)
                for t in range(NT):
                    last = mm(ps_m[:, 1, t * P:(t + 1) * P], o_t[:, t * P:(t + 1) * P], w_t[:, w, :],
                              start=True, stop=True)
                last.then_inc(sem(pre + "_proj"), 1)

            def mix_tokens(m):
                tokens_t("M", m, y, ps_m[:, 0, :], GT)

            def mix_logits(m, u):
                pe.wait_ge(sem("M_ytc"), m + 1)
                for t in range(GT):
                    last = mm(ps_m[:, 0, t * EXP:(t + 1) * EXP], ym_t[u][:, t * P:(t + 1) * P], wr[:, :],
                              start=True, stop=True)
                last.then_inc(sem("M_lg"), 1)

            def mix_gates(m, u):
                pe.wait_ge(sem("M_gate"), m + 1)
                for t in range(GT):
                    last = tr(ps_m[0:EXP, 0, t * P:(t + 1) * P], gate[u][:, t, :])
                last.then_inc(sem("M_gt"), 1)

            def mix_biases(m):
                pe.wait_ge(sem("M_gtc"), m + 1)
                for t in range(GT):
                    last = mm(ps_m[:, 0, t * P:(t + 1) * P], gate_t[:, t * P:(t + 1) * P], b2[:, :],
                              start=True, stop=True)
                last.then_inc(sem("M_b2"), 1)

            def mix_front(m, u):
                mix_tokens(m)
                mix_logits(m, u)
                mix_gates(m, u)
                mix_biases(m)

            def hidden(m, u, e):
                for f in range(NF):
                    j = e * NF + f
                    pe.wait_ge(sem("M_relu"), m * EXP * NF + j + 1)
                    bank = (ps_q, ps_k)[j % 4 // 2][:, j % 2, :]
                    mm(bank, w1[:, e, f * P:(f + 1) * P], ym_t[u][:, :], start=True, stop=True)\
                        .then_inc(sem("M_h"), 1)

            def outputs(m, e):
                pe.wait_ge(sem("M_relu"), m * EXP * NF + e * NF + NF + 4)
                pe.wait_ge(sem("M_comb"), m * EXP + e + 1)
                for t in range(GT):
                    for f in range(NF):
                        last = mm(ps_o[:, e % 2, t * P:(t + 1) * P], h_sb[e % 2][:, f, t * P:(t + 1) * P],
                                  w2[:, e * NF + f, :], start=f == 0, stop=f == NF - 1)
                last.then_inc(sem("M_out"), 1)

            def key_tokens(g):
                pe.wait_ge(sem("KN_y"), g * 2 * GT + 2 * GT)
                pe.wait_ge(sem("K_hi"), g + 1)
                for t in range(GT):
                    last = tr(ps_m[:, 1, t * P:(t + 1) * P], y3[:, t, :])
                last.then_inc(sem("K_yt"), 1)

            def key_product(g, w, free, done):
                pe.wait_ge(sem(free), g + 1)
                for t in range(GT):
                    last = mm(ps_m[:, 1, t * P:(t + 1) * P], z_t[:, t * P:(t + 1) * P], w_t[:, w, :],
                              start=True, stop=True)
                last.then_inc(sem(done), 1)

            def key_queries(g):
                key_product(g, W_Q1, "K_ytc", "K_q_ps")

            def key_keys(g):
                key_product(g, W_K1, "K_q", "K_k_ps")

            def key_values(g):
                key_product(g, W_V1, "K_k", "K_v_ps")

            def key_heads(g):
                pe.wait_ge(sem("K_nrm"), g + 1)
                pe.wait_ge(sem("K_v"), g + 1)
                for t in range(GT):
                    last = tr(ps_m[:, 1, t * P:(t + 1) * P], nrm[:, t, :, :].rearrange("p d h -> p (d h)"))
                last.then_inc(sem("K_nt"), 1)

            def mixture(g, u, base, keys):
                m = base + g
                front = not isinstance(g, int) or g < NG - 1
                before = keys and not (isinstance(g, int) and g == 0)
                hidden(m, u, 0)
                hidden(m, u, 1)
                outputs(m, 0)
                hidden(m, u, 2)
                if front:
                    mix_tokens(m + 1)
                outputs(m, 1)
                hidden(m, u, 3)
                if before:
                    key_tokens(g - 1)
                if front:
                    mix_logits(m + 1, 1 - u)
                outputs(m, 2)
                hidden(m, u, 4)
                if before:
                    key_queries(g - 1)
                outputs(m, 3)
                hidden(m, u, 5)
                if before:
                    key_keys(g - 1)
                if front:
                    mix_gates(m + 1, 1 - u)
                outputs(m, 4)
                hidden(m, u, 6)
                if before:
                    key_values(g - 1)
                if front:
                    mix_biases(m + 1)
                outputs(m, 5)
                hidden(m, u, 7)
                outputs(m, 6)
                if before:
                    key_heads(g - 1)
                outputs(m, 7)

            def front_tokens(f):
                pe.wait_ge(sem("query_tok"), f + 1)
                pe.wait_ge(sem("fast_hi"), f + 1)
                for t in range(NT):
                    last = tr(ps_m[:, 0, t * P:(t + 1) * P], q_tok[:, t * P:(t + 1) * P])
                last.then_inc(sem("query_t"), 1)

            def front_product(f):
                pe.wait_ge(sem("query_tc"), f + 1)
                for t in range(NT):
                    last = mm(ps_m[:, 0, T + t * P:T + (t + 1) * P], z_t[:, t * P:(t + 1) * P], block_w[:, 0, :],
                              start=True, stop=True)
                last.then_inc(sem("query_ps"), 1)

            def front_heads(f):
                pe.wait_ge(sem("query_nrm"), f + 1)
                for t in range(NT):
                    last = tr(ps_m[:, 0, t * P:(t + 1) * P], nrm[:, t, :, :].rearrange("p d h -> p (d h)"))
                last.then_inc(sem("query_nt"), 1)

            def pair_scores(n, p, half, hp):
                pe.wait_ge(sem("fast_exp"), n * HP + hp + 1)
                if hp == 0:
                    pe.wait_ge(sem(f"fast_operands_in_{p}"), half * 96 + 96)
                bank = (ps_q, ps_k)[hp % 2]
                for u in range(2):
                    for t in range(NT):
                        last = mm(bank[:, u, t * T:(t + 1) * T], k_st[p][0:ROWS_P1, hp * 2 + u, t * P:(t + 1) * P],
                                  q_st[p][0:ROWS_P1, hp * 2 + u, :], start=True, stop=True)
                last.then_inc(sem("fast_scores"), 1)

            def fast_values(n, p, g):
                pe.wait_ge(sem("fast_exp"), n * HP + (g + 1) * HG // 2 + 2)
                pe.wait_ge(sem("fast_evac"), n * NGV + g + 1)
                if g == 0:
                    pe.wait_ge(sem("fast_v"), n + 1)
                for kt in range(NT):
                    for j in range(HG):
                        last = mm(ps_o[VW * j:VW * j + VW, g % 2, 0:T], v_st[p][:, kt, HG * g + j, :],
                                  e_buf[g % 2][:, j, kt * T:(kt + 1) * T], start=kt == 0, stop=kt == NT - 1,
                                  tile_position=(0, VW * j))
                last.then_inc(sem("fast_values"), 1)

            def back_tokens(n, b, it, t):
                if t == 0:
                    pe.wait_ge(sem("fast_evac"), n * NGV + NGV + 2)
                    if it == MAX_ITER - 1:
                        pe.wait_ge(sem("O_x"), b + 1)
                pe.wait_ge(sem("fast_o_read"), n * NT + t + 1)
                for g in range(NGV):
                    last = tr(ps_m[:, 1, g * P:(g + 1) * P], o_sb[:, g, t * P:(t + 1) * P])
                last.then_inc(sem("fast_o_t"), 1)

            def back_out(b):
                pe.wait_ge(sem("O_o"), b + 1)
                for t in range(NT):
                    last = tr(ps_m[:, 1, t * P:(t + 1) * P], o_tok[:, t, :, :].rearrange("p h d -> p (h d)"))
                last.then_inc(sem("O_ott"), 1)

            def back_project(b):
                pe.wait_ge(sem("O_otc"), b + 1)
                for t in range(NT):
                    last = mm(ps_m[:, 1, T + t * P:T + (t + 1) * P], o_t[:, t * P:(t + 1) * P], w_t[:, W_O1, :],
                              start=True, stop=True)
                last.then_inc(sem("O_proj"), 1)

            def change_sum(it, bank):
                pe.wait_ge(sem("d_total"), it + 1)
                mm(ps_m[:, bank, 0:1], ones[:, :], dtot[:, :], start=True, stop=True).then_inc(sem("d_sum"), 1)

            def fast_focus():
                pe.sem_inc(sem("fast_values"), 2)
                for f in range(2):
                    front_tokens(f)
                    front_product(f)
                    front_heads(f)
                for it in range(MAX_ITER):
                    final = it == MAX_ITER - 1
                    if it:
                        pe.wait_ge(sem("window_in"), 32 * it)

                    def body(n, b, p, half):
                        first = isinstance(b, int) and b == 0
                        ahead = follow(n, b, 2)
                        for hp in range(HP):
                            pair_scores(n, p, half, hp)
                            if hp == 1:
                                if ahead:
                                    front_tokens(ahead[0])
                                if not first:
                                    fast_values(n - 1, 1 - p, NGV - 1)
                            elif hp == 2 and ahead:
                                front_product(ahead[0])
                            elif hp == 3:
                                if not first:
                                    back_tokens(n - 1, b - 1, it, 0)
                                fast_values(n, p, 0)
                            elif hp == 4 and not first:
                                back_tokens(n - 1, b - 1, it, 1)
                            elif hp == 5:
                                fast_values(n, p, 1)
                                if ahead:
                                    front_heads(ahead[0])
                            elif hp == 6 and not first and final:
                                back_out(b - 1)
                            elif hp == 7:
                                if not first and final:
                                    back_project(b - 1)
                                fast_values(n, p, 2)

                    fast_steps(pe, it, body)
                    n = it * B + B - 1
                    fast_values(n, 1, NGV - 1)
                    for t in range(NT):
                        back_tokens(n, B - 1, it, t)
                    if final:
                        back_out(B - 1)
                        back_project(B - 1)
                    else:
                        change_sum(it, 1)

            def general_focus():
                for it in range(MAX_ITER):
                    if it:
                        pe.wait_ge(sem("window_in"), 32 * it)
                    with pe.Fori(0, B // 2) as i:
                        for p in range(2):
                            b = i * 2 + p
                            n = (1 + it) * B + b
                            focus_front(n)
                            maxima_scores(n, p, False)
                            maxima_rows(n, False)
                            products(n, p, False)
                            back(n, p, False)
                            if it == MAX_ITER - 1:
                                project(b, "O", W_O1)
                    if it < MAX_ITER - 1:
                        change_sum(it, 0)

            pe.wait_ge(sem("consts"), CONSTS)
            pe.wait_ge(sem("loaded"), n_loads)
            for k in range(3):
                if k == 2:
                    pe.wait_ge(sem("setup_scalar"), 1)
                for j in range(4 * k, min(4 * k + 4, 9)):
                    last = tr(ps_m[:, k % 2, (j % 4) * P:(j % 4 + 1) * P], w_nat[:, j, :])
                last.then_inc(sem("setup_tensor"), 1)
            pe.wait_ge(sem("setup_scalar"), 2)
            tr(ps_m[:, 1, 256:256 + EXP * NF], b1_nat[:, :], EXP * NF).then_inc(sem("setup_tensor"), 1)
            pe.wait_ge(sem("setup_vector"), 1)
            for j in range(3):
                last = tr(ps_k[:, 0, j * P:(j + 1) * P], e_buf[0][:, j, 0:P])
            last.then_inc(sem("setup_tensor"), 1)
            pe.wait_ge(sem("setup_vector"), 2)
            mm(ps_q[:, 0, 0:P], w_nat[:, 9, :], block_w[:, 1, :], start=True, stop=True)
            mm(ps_q[:, 0, P:2 * P], w_nat[:, 10, :], block_w[:, 2, :], start=True, stop=True)\
                .then_inc(sem("setup_tensor"), 1)
            mm(ps_q[:, 1, 0:P], bv_rep[:, :], block_w[:, 2, :], start=True, stop=True).then_inc(sem("setup_tensor"), 1)
            pe.wait_ge(sem("setup_scalar"), 5)

            pe.sem_inc(sem("operands_free"), 2)
            pe.sem_inc(sem("values_done"), 2)
            pe.sem_inc(sem("M_out"), 2)
            with pe.Fori(0, B // 2) as i:
                for p in range(2):
                    n = i * 2 + p
                    ffn(n * 2, n * 3)
                    causal_front(n, n * 3 + 1)
                    maxima_scores(n, p, True)
                    maxima_rows(n, True)
                    products(n, p, True)
                    back(n, p, True)
                    project(n, "A", W_P0)
                    ffn(n * 2 + 1, n * 3 + 2)
            mix_front(0, 0)
            mixture_groups(pe, lambda g, u: mixture(g, u, 0, True))
            key_tokens(NG - 1)
            key_queries(NG - 1)
            key_keys(NG - 1)
            key_values(NG - 1)
            key_heads(NG - 1)
            any_path(pe, fast_focus, general_focus)
            mix_front(NG, 0)
            mixture_groups(pe, lambda g, u: mixture(g, u, NG, False))

        @block.vector
        def _(dve):
            tt, ts, stt, red = dve.tensor_tensor, dve.tensor_scalar, dve.scalar_tensor_tensor, dve.tensor_reduce

            class Steps:

                def __init__(self, name, n, per):
                    self.sem, self.base, self.per, self.k = sem(name), n * per, per, 0

                def __call__(self, ins):
                    ins.then_inc(self.sem, 1)
                    self.k += 1

                def wait(self):
                    dve.wait_ge(self.sem, self.base + self.k)

                def end(self):
                    assert self.k == self.per
                    self.wait()

            def hold():
                dve.sem_inc(sem("held"), 1)

            def ln_stats(pre, n, src, tiles, st, mv):
                for t in range(tiles):
                    dve.bn_stats(st[:, t, :], src(t)).then_inc(sem(pre + "_st"), 1)
                dve.wait_ge(sem(pre + "_st"), n * tiles + tiles)
                hold()
                for t in range(tiles):
                    dve.bn_aggr(mv[:, t, :], st[:, t, :]).then_inc(sem(pre + "_mom"), 1)

            def ln_apply(pre, n, src, dst, tiles, mv, rstd):
                dve.wait_ge(sem(pre + "_rstd"), n + 1)
                for t in range(tiles):
                    ts(dst(t), src(t), mv[:, t, 0:1], rstd[:, t:t + 1], ALU.subtract, ALU.mult)\
                        .then_inc(sem(pre + "_y"), 1)

            def layernorm(pre, n, src, dst, tiles):
                ln_stats(pre, n, src, tiles, st, mv)
                ln_apply(pre, n, src, dst, tiles, mv, rstd)

            def of_x(b):
                return lambda t: x[:, b, t * C:(t + 1) * C]

            def of(buf):
                return lambda t: buf[:, t, :]

            def ffn(n, l, b):
                hold()
                layernorm("T", l, of_x(b), of(y), NT)
                dve.wait_ge(sem("F_dy"), n + 1)
                stt(xr[:, :], dy[:, :], col(MU_R), y_t[:, 0:T], ALU.mult, ALU.add).then_inc(sem("F_xr"), 1)
                stt(xk[:, :], dy[:, :], col(MU_K), y_t[:, 0:T], ALU.mult, ALU.add).then_inc(sem("F_xk"), 1)
                s = Steps("F_step", n, 4)
                dve.wait_ge(sem("F_er"), n + 1)
                s(ts(er[:, :], er[:, :], 1.0, None, ALU.add))
                s.wait()
                s(dve.reciprocal(rec[:, :], er[:, :]))
                s.wait()
                dve.wait_ge(sem("F_v"), n + 1)
                s(stt(gated[:, :], ps_m[:, 0, 0:T], 0.5, rec[:, :], ALU.mult, ALU.mult))
                s.wait()
                s(tt(x[:, b, :], x[:, b, :], gated[:, :], ALU.add))
                s.end()

            def causal_front(n, l, p, b):
                hold()
                layernorm("T", l, of_x(b), of(y), NT)
                dve.wait_ge(sem("G_v"), n + 1)
                dve.tensor_copy(v_st[p][:, :, :, 0:HD],
                                ps_o[:, 0, 0:T].rearrange("p (t h d) -> p t h d", t=NT, h=H))\
                    .then_inc(sem("values_ready"), 1)

            def maxima(n, causal):
                for h in range(H):
                    dve.wait_ge(sem("q_scores"), n * H + h + 1)
                    o = ps_q[:, h % 2, :]
                    if causal:
                        red(nmax[:, 1, h:h + 1], o[:, 0:2 * P], AX.X, ALU.max, negate=True)
                        last = red(nmax[:, 0, h:h + 1], o[:, 2 * P:3 * P], AX.X, ALU.max, negate=True)
                    else:
                        last = red(ml[:, :, 0, h], o.rearrange("p (t k) -> p t k", t=NT), AX.X, ALU.max, negate=True)
                    last.then_inc(sem("max_done"), 1)
                if causal:
                    dve.wait_ge(sem("max_done"), n * H + H + 2)
                    ts(ml[:, :, 0, :], nmax[:, :, :], -CLIP, CLIP, ALU.max, ALU.min).then_inc(sem("ml_m"), 1)

            def clamps(n):
                for hp in range(H // 2):
                    dve.wait_ge(sem("exp_done"), n * H + 2 * hp + 2 + 2)
                    dve.wait_ge(sem("floor"), n * (H // 2) + hp + 1)
                    j = 2 * hp % HG
                    e = e_buf[hp // 2 % 2][:, j:j + 2, :]
                    lo = ps_m[:, hp % 2, :].rearrange("p (h q) -> p h q", h=2)
                    stt(e[:, :, 0:P], e[:, :, 0:P], 1.0, lo[:, :, P:T], ALU.min, ALU.max)
                    stt(e[:, :, P:3 * P], e[:, :, P:3 * P], 1.0, lo[:, :, :], ALU.min, ALU.max)\
                        .then_inc(sem("clamp_done"), 1)

            def causal_back(n, b):
                dve.wait_ge(sem("o_t"), n + 1)
                dve.wait_ge(sem("v_sums"), n + 1)
                o = ps_m[:, :, :].rearrange("p t (h w) -> p t h w", w=VW)
                v1 = ps_o[:, 0, 0:P].rearrange("p (h d) -> p h d", h=H)
                vs = ps_o[:, 0, P:2 * P].rearrange("p (h d) -> p h d", h=H)
                low = ml[:, 0, 1, :]
                s = Steps("norm_step", n, 12)
                s(dve.tensor_copy(s_sum[:, :, :], o[:, :, :, HD]))
                s.wait()
                s(stt(s_sum[:, 0, :], low, float(P), s_sum[:, 0, :], ALU.mult, ALU.add))
                s.wait()
                s(ts(s_u[:, :, :], s_sum[:, :, :], DEN_EPS, None, ALU.add))
                s.wait()
                s(ts(s_du[:, :, :], s_u[:, :, :], P_EPS, None, ALU.mult))
                s(stt(s_den[:, :, :], s_u[:, :, :], P_EPS * T, s_sum[:, :, :], ALU.mult, ALU.add))
                s.wait()
                s(dve.reciprocal(s_rec[:, :, :], s_den[:, :, :]))
                for t in range(NT):
                    s(tt(corr[:, t, :, :], s_du[:, t, :].unsqueeze(2).broadcast_to([P, H, HD]), vs, ALU.mult))
                s(tt(corr2[:, :, :], low.unsqueeze(2).broadcast_to([P, H, HD]), v1, ALU.mult))
                s.wait()
                s(tt(corr[:, 0, :, :], corr[:, 0, :, :], corr2[:, :, :], ALU.add))
                s.wait()
                s(tt(corr[:, :, :, :], corr[:, :, :, :], o[:, :, :, 0:HD], ALU.add))
                s.wait()
                s(tt(o_tok[:, :, :, :], corr[:, :, :, :], s_rec[:, :, :].unsqueeze(3).broadcast_to([P, NT, H, HD]),
                     ALU.mult))
                s.end()
                dve.nop().then_inc(sem("A_o"), 1)
                dve.wait_ge(sem("A_proj"), n + 1)
                tt(x[:, b, :], x[:, b, :], ps_m[:, 1, 0:T], ALU.add).then_inc(sem("A_x"), 1)
                dve.wait_ge(sem("A_x"), n + 1)

            def of_group(g):
                return lambda t: x[:, g * GB + t // NT, t % NT * C:(t % NT + 1) * C]

            def group(ap):
                return ap.rearrange("p b (t c) -> p (b t) c", c=C)

            def mix_stats(m, g):
                hold()
                ln_stats("M", m, of_group(g), GT, st, mv)

            def mix_norm(m, g):
                ln_apply("M", m, of_group(g), of(y), GT, mv, rstd)

            def mix_ranks(m):
                s = Steps("M_rank", m, 6)
                dve.wait_ge(sem("M_lg"), m + 1)
                s(tt(lg[:, :, :], ps_m[:, 0, 0:GT * EXP].rearrange("p (t e) -> p t e", t=GT),
                     br_row[:, :].unsqueeze(1).broadcast_to([P, GT, EXP]), ALU.add))
                s.wait()
                for t in range(GT):
                    mine = lg[:, t, :].unsqueeze(2).broadcast_to([P, EXP, EXP])
                    other = lg[:, t, :].unsqueeze(1).broadcast_to([P, EXP, EXP])
                    tt(gt_[:, t, :, :], other, mine, ALU.is_gt)
                    last = tt(eq_[:, t, :, :], other, mine, ALU.is_equal)
                s(last)
                s(red(lmax[:, :], lg[:, :, :], AX.X, ALU.max))
                s.wait()
                s(tt(eq_[:, :, :, :], eq_[:, :, :, :], tri[:, :, :].unsqueeze(1).broadcast_to([P, GT, EXP, EXP]), ALU.mult))
                s.wait()
                s(tt(gt_[:, :, :, :], gt_[:, :, :, :], eq_[:, :, :, :], ALU.add))
                s.wait()
                s(red(rank[:, :, :], gt_[:, :, :, :], AX.X, ALU.add))
                tt(eq_[:, :, 0, :], lg[:, :, :], lmax[:, :].unsqueeze(2).broadcast_to([P, GT, EXP]), ALU.subtract)\
                    .then_inc(sem("M_lmax"), 1)
                s.end()

            def mix_gates(m, u):
                s = Steps("M_gate_step", m, 4)
                s(ts(rank[:, :, :], rank[:, :, :], float(2), None, ALU.is_lt))
                s.wait()
                dve.wait_ge(sem("M_lexp"), m + 1)
                s(tt(lexp[:, :, :], lexp[:, :, :], rank[:, :, :], ALU.mult))
                s.wait()
                s(red(gsum[:, :], lexp[:, :, :], AX.X, ALU.add))
                s.wait()
                s(dve.reciprocal(gsum[:, :], gsum[:, :]))
                s.end()
                tt(gate[u][:, :, :], lexp[:, :, :], gsum[:, :].unsqueeze(2).broadcast_to([P, GT, EXP]), ALU.mult)\
                    .then_inc(sem("M_gate"), 1)

            def mix_biases(m, u):
                dve.wait_ge(sem("M_b2"), m + 1)
                dve.tensor_copy(acc[u][:, :, :], ps_m[:, 0, :].rearrange("p (t c) -> p t c", t=GT))\
                    .then_inc(sem("M_acc"), 1)

            def mix_front(m, g, u):
                mix_stats(m, g)
                mix_norm(m, g)
                mix_ranks(m)
                mix_gates(m, u)
                mix_biases(m, u)

            def combine(m, u, e):
                dve.wait_ge(sem("M_out"), m * EXP + e + 1 + 2)
                if e:
                    dve.wait_ge(sem("M_comb"), m * EXP + e + 2)
                else:
                    dve.wait_ge(sem("M_acc"), m + 1)
                    dve.wait_ge(sem("M_gate"), m + 1)
                for t in range(GT):
                    last = stt(acc[u][:, t, :], ps_o[:, e % 2, t * P:(t + 1) * P], gate[u][:, t, e:e + 1],
                               acc[u][:, t, :], ALU.mult, ALU.add)
                last.then_inc(sem("M_comb"), 1)

            def key_stats1(g):
                dve.wait_ge(sem("M_x"), g + 1)
                hold()
                ln_stats("KN", g * 2, of_group(g), GT, st_k, mv_k)

            def key_norm1(g):
                ln_apply("KN", g * 2, of_group(g), of(y2), GT, mv_k, rstd_k)

            def key_stats2(g):
                dve.wait_ge(sem("KN_y"), g * 2 * GT + GT)
                hold()
                ln_stats("KN", g * 2 + 1, of(y2), GT, st_k, mv_k)

            def key_norm2(g):
                ln_apply("KN", g * 2 + 1, of(y2), of(y3), GT, mv_k, rstd_k)

            def rows_g(r):
                return r.unsqueeze(1).broadcast_to([P, GT, C])

            def from_bank(bank):
                return bank.rearrange("p (t c) -> p t c", c=C)

            def key_queries(g):
                dve.wait_ge(sem("K_q_ps"), g + 1)
                stt(group(qcur[:, bass.ds(g * GB, GB), :]), from_bank(ps_m[:, 1, :]), SC, rows_g(rows[:, R_BQ, :]),
                    ALU.mult, ALU.add).then_inc(sem("K_q"), 1)

            def key_keys(g):
                dve.wait_ge(sem("K_k_ps"), g + 1)
                tt(cen[:, :, :, :].rearrange("p t h d -> p t (h d)"), from_bank(ps_m[:, 1, :]), rows_g(rows[:, R_LK, :]),
                   ALU.add).then_inc(sem("K_k"), 1)
                dve.wait_ge(sem("K_k"), g + 1)
                tt(sqr[:, :, :, :], cen[:, :, :, :], cen[:, :, :, :], ALU.mult).then_inc(sem("K_sqr"), 1)
                dve.wait_ge(sem("K_sqr"), g + 1)
                hold()
                red(hvar[:, :], heads(sqr, GT), AX.X, ALU.add).then_inc(sem("K_mom"), 1)

            def key_values(g):
                dve.wait_ge(sem("K_v_ps"), g + 1)
                tt(group(vp_all[:, bass.ds(g * GB, GB), :]), from_bank(ps_m[:, 1, :]), rows_g(v_bias[:, :]), ALU.add)\
                    .then_inc(sem("K_v"), 1)

            def heads(buf, tiles_):
                return buf[:, 0:tiles_, :, :].rearrange("p t h d -> p (t h) d")

            def normalise_heads(done, scaled, g, tiles_, weights, scale=None):
                dve.wait_ge(sem(done), g + 1)
                w = tiles_ * H
                tt(heads(sqr, tiles_), heads(cen, tiles_), hrs[:, 0:w].unsqueeze(2).broadcast_to([P, w, HD]), ALU.mult)\
                    .then_inc(sem(scaled), 1)
                dve.wait_ge(sem(scaled), g + 1)
                per = weights.rearrange("p (h d) -> p h d", h=H)
                for t in range(tiles_):
                    dst = nrm[:, t, :, :].rearrange("p d h -> p h d")
                    if scale is None:
                        last = tt(dst, sqr[:, t, :, :], per, ALU.mult)
                    else:
                        last = stt(dst, sqr[:, t, :, :], scale, per, ALU.mult, ALU.mult)
                return last

            def key_heads(g):
                normalise_heads("K_rstd", "K_scaled", g, GT, rows[:, R_LND, :]).then_inc(sem("K_nrm"), 1)

            def mixture(g, u, base, keys):
                m = base + g
                front = not isinstance(g, int) or g < NG - 1
                before = keys and not (isinstance(g, int) and g == 0)
                if before:
                    key_stats1(g - 1)
                if front:
                    mix_stats(m + 1, g + 1)
                if before:
                    key_norm1(g - 1)
                if front:
                    mix_norm(m + 1, g + 1)
                if before:
                    key_stats2(g - 1)
                combine(m, u, 0)
                if before:
                    key_norm2(g - 1)
                combine(m, u, 1)
                if front:
                    mix_ranks(m + 1)
                combine(m, u, 2)
                if before:
                    key_queries(g - 1)
                if front:
                    mix_gates(m + 1, 1 - u)
                combine(m, u, 3)
                if before:
                    key_keys(g - 1)
                combine(m, u, 4)
                if before:
                    key_values(g - 1)
                if front:
                    mix_biases(m + 1, 1 - u)
                combine(m, u, 5)
                combine(m, u, 6)
                if before:
                    key_heads(g - 1)
                combine(m, u, 7)
                dve.wait_ge(sem("M_comb"), m * EXP + EXP + 2)
                xg = x[:, bass.ds(g * GB, GB), :]
                stt(xg, acc[u][:, :, :].rearrange("p (b t) c -> p b (t c)", b=GB), 0.5, xg, ALU.mult, ALU.add)\
                    .then_inc(sem("M_x"), 1)

            def tiles(ap):
                return ap.rearrange("p (t c) -> p t c", t=NT)

            def row2(j):
                return rows[:, j, :].unsqueeze(1).broadcast_to([P, NT, C])

            def query_deviations(f, src):
                tt(cen[:, 0:NT, :, :].rearrange("p t h d -> p t (h d)"), tiles(src), row2(R_LQ), ALU.add)\
                    .then_inc(sem("query_cen"), 1)
                dve.wait_ge(sem("query_cen"), f + 1)
                tt(sqr[:, 0:NT, :, :], cen[:, 0:NT, :, :], cen[:, 0:NT, :, :], ALU.mult).then_inc(sem("query_sqr"), 1)
                dve.wait_ge(sem("query_sqr"), f + 1)
                hold()
                red(hvar[:, 0:NT * H], heads(sqr, NT), AX.X, ALU.add).then_inc(sem("query_mom"), 1)

            def focus_front(n, p, b, it):
                f = n - B
                hold()
                dve.tensor_copy(v_st[p][:, :, :, 0:HD],
                                vp_all[:, b, :].rearrange("p (t h d) -> p t h d", t=NT, h=H))\
                    .then_inc(sem("values_ready"), 1)
                dve.tensor_copy(o_prev[:, :], qcur[:, b, :]).then_inc(sem("query_tok"), 1)
                dve.wait_ge(sem("query_ps"), f + 1)
                query_deviations(f, ps_m[:, 1, 0:T])
                normalise_heads("query_rstd", "query_scaled", f, NT, rows[:, R_LNC, :], temps[:, Q_SC, it:it + 1])\
                    .then_inc(sem("query_nrm"), 1)

            def evacuate(n):
                for g in range(H // HG):
                    dve.wait_ge(sem("values_done"), n * (H // HG) + g + 1 + 2)
                    dve.tensor_copy(o_sb[:, g, :], ps_o[:, g % 2, (g // 2) * T:(g // 2 + 1) * T])\
                        .then_inc(sem("o_evac"), 1)

            def focus_back(n, b, it):
                f = n - B
                ot = o_tok[:, :, :, :].rearrange("p t h d -> p (t h d)")
                dve.wait_ge(sem("o_t"), n + 1)
                o = ps_m[:, :, :].rearrange("p t (h w) -> p t h w", w=VW)
                s = Steps("focus_norm", f, 2)
                s(dve.reciprocal(s_rec[:, :, :], o[:, :, :, HD]))
                s.wait()
                s(tt(o_tok[:, :, :, :], o[:, :, :, 0:HD], s_rec[:, :, :].unsqueeze(3).broadcast_to([P, NT, H, HD]),
                     ALU.mult))
                s.end()
                if it:
                    for t in range(NT):
                        last = ts(o_tok[:, t, :, :], o_tok[:, t, :, :], in_win[:, t:t + 1], None, ALU.mult)
                    last.then_inc(sem("windowed"), 1)
                    dve.wait_ge(sem("windowed"), (it - 1) * B + b + 1)
                if it == 0:
                    hold()
                    red(dsum[:, bass.ds(b, 1)], ot, AX.X, ALU.add, apply_absolute_value=True).then_inc(sem("d_part"), 1)
                    dve.tensor_copy(heads_out[:, b, :], ot).then_inc(sem("d_part"), 1)
                    tt(qcur[:, b, :], qcur[:, b, :], ot, ALU.add).then_inc(sem("d_part"), 1)
                    dve.wait_ge(sem("d_part"), b * 3 + 3)
                elif it == 1:
                    tt(o_prev[:, :], ot, heads_out[:, b, :], ALU.subtract).then_inc(sem("d_diff"), 1)
                    tt(qcur[:, b, :], qcur[:, b, :], ot, ALU.add).then_inc(sem("d_diff"), 1)
                    dve.wait_ge(sem("d_diff"), b * 2 + 2)
                    hold()
                    red(dsum[:, bass.ds(b, 1)], o_prev[:, :], AX.X, ALU.add, apply_absolute_value=True)\
                        .then_inc(sem("d_part"), 2)
                    dve.tensor_copy(heads_out[:, b, :], ot).then_inc(sem("d_part"), 1)
                    dve.wait_ge(sem("d_part"), (B + b) * 3 + 3)
                else:
                    ts(o_prev[:, :], heads_out[:, b, :], c1(DONE), None, ALU.mult).then_inc(sem("O_kept"), 1)
                    dve.wait_ge(sem("O_kept"), b + 1)
                    stt(ot, ot, c1(KEEP), o_prev[:, :], ALU.mult, ALU.add).then_inc(sem("O_o"), 1)
                    dve.wait_ge(sem("O_proj"), b + 1)
                    tt(tiles(x[:, b, :]), tiles(x[:, b, :]), tiles(ps_m[:, 1, 0:T]), ALU.add).then_inc(sem("O_x"), 1)
                    dve.wait_ge(sem("O_x"), b * 2 + 1)
                    tt(tiles(x[:, b, :]), tiles(x[:, b, :]), row2(R_BO), ALU.add).then_inc(sem("O_x"), 1)
                    dve.wait_ge(sem("O_x"), b * 2 + 2)

            def front_tokens(f):
                dve.wait_ge(sem("query_t"), f + 1 + 1)
                dve.tensor_copy(z_t[:, 0:T], ps_m[:, 0, 0:T]).then_inc(sem("query_tc"), 1)

            def front_deviations(f):
                dve.wait_ge(sem("query_ps"), f + 1)
                query_deviations(f, ps_m[:, 0, T:2 * T])

            def front_heads(f, it):
                normalise_heads("query_rstd", "query_scaled", f, NT, rows[:, R_LNC, :], temps[:, Q_SC, it:it + 1])\
                    .then_inc(sem("query_nrm"), 1)

            def front_parts(f, p):
                dve.wait_ge(sem("query_nt"), f + 1)
                dve.wait_ge(sem("fast_parts_out"), f * 16 + 16)
                hold()
                dve.tensor_copy(qk32[:, p, :], ps_m[:, 0, 0:T])
                dve.tensor_copy(parts[:, p, 0, :], ps_m[:, 0, 0:T]).then_inc(sem("fast_hi"), 1)

            def evacuate_group(n, g):
                dve.wait_ge(sem("fast_values"), n * NGV + g + 1 + 2)
                if g == 0:
                    dve.wait_ge(sem("fast_o_t"), n * NT + 2)
                hold()
                dve.tensor_copy(o_sb[:, g, :], ps_o[:, g % 2, 0:T]).then_inc(sem("fast_evac"), 1)

            def normalise(n, it, t):
                if t == 0:
                    dve.wait_ge(sem("fast_q_new"), n + B if it < MAX_ITER - 1 else (MAX_ITER - 1) * B + B)
                dve.wait_ge(sem("fast_o_t"), n * NT + t + 1 + 2)
                o = ps_m[:, 1, :].rearrange("p (h w) -> p h w", w=VW)
                hold()
                dve.reciprocal(s_rec[:, t, :], o[:, :, HD]).then_inc(sem("focus_norm"), 1)
                dve.wait_ge(sem("focus_norm"), n * NT + t + 1)
                if it:
                    ts(s_rec[:, t, :], s_rec[:, t, :], in_win[:, t:t + 1], None, ALU.mult)\
                        .then_inc(sem("windowed"), 1)
                    dve.wait_ge(sem("windowed"), (n - B) * NT + t + 1)
                tt(o_tok[:, t, :, :], o[:, :, 0:HD], s_rec[:, t, :].unsqueeze(2).broadcast_to([P, H, HD]), ALU.mult)\
                    .then_inc(sem("fast_o_read"), 1)

            def change(n, b, it):
                ot = o_tok[:, :, :, :].rearrange("p t h d -> p (t h d)")
                dve.wait_ge(sem("fast_o_read"), n * NT + NT + 1)
                hold()
                if it == 0:
                    red(dsum[:, bass.ds(b, 1)], ot, AX.X, ALU.add, apply_absolute_value=True)\
                        .then_inc(sem("d_part"), 1)
                elif it == 1:
                    tt(o_prev[:, :], ot, heads_out[:, b, :], ALU.subtract).then_inc(sem("d_diff"), 1)
                    dve.wait_ge(sem("d_diff"), b + 1)
                    hold()
                    red(dsum[:, bass.ds(b, 1)], o_prev[:, :], AX.X, ALU.add, apply_absolute_value=True)\
                        .then_inc(sem("d_part"), 1)
                else:
                    ts(o_prev[:, :], heads_out[:, b, :], c1(DONE), None, ALU.mult).then_inc(sem("O_kept"), 1)
                    dve.wait_ge(sem("O_kept"), b + 1)
                    stt(ot, ot, c1(KEEP), o_prev[:, :], ALU.mult, ALU.add).then_inc(sem("O_o"), 1)

            def back_out(b):
                dve.wait_ge(sem("O_ott"), b + 1)
                dve.tensor_copy(o_t[:, :], ps_m[:, 1, 0:T]).then_inc(sem("O_otc"), 1)

            def back_project(b):
                dve.wait_ge(sem("O_proj"), b + 1)
                dve.wait_ge(sem("fast_bias"), b + 1)
                tt(tiles(x[:, b, :]), tiles(x[:, b, :]), tiles(ps_m[:, 1, T:2 * T]), ALU.add).then_inc(sem("O_x"), 1)

            def fast_focus():
                dve.sem_inc(sem("fast_hi"), 1)
                dve.sem_inc(sem("fast_evac"), 2)
                dve.sem_inc(sem("fast_o_t"), 2)
                dve.sem_inc(sem("fast_o_read"), 1)
                dve.sem_inc(sem("O_x"), 1)
                for f in range(2):
                    front_tokens(f)
                    front_deviations(f)
                    front_heads(f, 0)
                    front_parts(f, f)
                for it in range(MAX_ITER):
                    final = it == MAX_ITER - 1

                    def body(n, b, p, half):
                        first = isinstance(b, int) and b == 0
                        ahead = follow(n, b, 2)
                        if ahead:
                            front_tokens(ahead[0])
                        if not first:
                            evacuate_group(n - 1, NGV - 1)
                        if ahead:
                            front_deviations(ahead[0])
                        if not first:
                            normalise(n - 1, it, 0)
                        evacuate_group(n, 0)
                        if not first:
                            normalise(n - 1, it, 1)
                            change(n - 1, b - 1, it)
                        if ahead:
                            later = isinstance(b, int) and b + 2 >= B
                            front_heads(ahead[0], it + 1 if later else it)
                        evacuate_group(n, 1)
                        if not first and final:
                            back_out(b - 1)
                        if ahead:
                            front_parts(ahead[0], p)
                        if not first and final:
                            back_project(b - 1)
                        evacuate_group(n, 2)

                    fast_steps(dve, it, body)
                    n = it * B + B - 1
                    evacuate_group(n, NGV - 1)
                    for t in range(NT):
                        normalise(n, it, t)
                    change(n, B - 1, it)
                    if final:
                        back_out(B - 1)
                        back_project(B - 1)
                        dve.wait_ge(sem("O_x"), B + 1)
                    else:
                        dve.wait_ge(sem("d_part"), n + 1)
                        control(it, 1)

            def general_focus():
                link(dve.memset(ml[:, :, 1, :], 0.0))
                for it in range(MAX_ITER):
                    with dve.Fori(0, B // 2) as i:
                        for p in range(2):
                            b = i * 2 + p
                            n = (1 + it) * B + b
                            focus_front(n, p, b, it)
                            maxima(n, False)
                            evacuate(n)
                            focus_back(n, b, it)
                    if it < MAX_ITER - 1:
                        control(it, 0)

            step_at = [0]

            def link(ins):
                ins.then_inc(sem("control"), 1)
                step_at[0] += 1
                dve.wait_ge(sem("control"), step_at[0])

            def temperatures():
                link(dve.tensor_copy(temps[:, TEMP, 0:1], col(TMP)))
                for j in range(1, MAX_ITER):
                    link(ts(temps[:, TEMP, j:j + 1], temps[:, TEMP, j - 1:j], 0.005, None, ALU.add))
                link(ts(temps[:, T_POS, :], temps[:, TEMP, :], 0.0, None, ALU.is_gt))
                link(tt(temps[:, T_SAFE, :], temps[:, TEMP, :], temps[:, T_POS, :], ALU.mult))
                link(ts(temps[:, T_POS, :], temps[:, T_POS, :], -1.0, 1.0, ALU.mult, ALU.add))
                link(tt(temps[:, T_SAFE, :], temps[:, T_SAFE, :], temps[:, T_POS, :], ALU.add))
                dve.nop().then_inc(sem("setup_vector"), 1)
                dve.wait_ge(sem("setup_scalar"), 7)
                link(ts(temps[:, Q_SC, :], temps[:, Q_SC, :], INV_SQRT, None, ALU.mult))
                link(red(c1(T0), temps[:, Q_SC, :], AX.X, ALU.max))
                link(tt(o_prev[:, 0:C], rows[:, R_LNC, :], rows[:, R_LND, :], ALU.mult))
                link(red(c1(T1), o_prev[:, 0:C], AX.X, ALU.max, apply_absolute_value=True))
                link(ts(c1(BND), c1(T0), c1(T1), float(HD), ALU.mult, ALU.mult))
                link(ts(c1(BND), c1(BND), SAFE, None, ALU.is_le))
                link(dve.tensor_copy(path[:, :], c1(BND)))
                dve.nop().then_inc(sem("path_ready"), 1)

            def floor(dst, scale):
                link(ts(c1(T0), c1(CW), float(np.float32(scale)), None, ALU.mult))
                link(dve.tensor_copy(ctl_i[:, 0:1], c1(T0)))
                link(dve.tensor_copy(c1(dst), ctl_i[:, 0:1]))
                link(tt(c1(T1), c1(dst), c1(T0), ALU.is_gt))
                link(tt(c1(dst), c1(dst), c1(T1), ALU.subtract))

            def control(it, bank):
                link(red(dtot[:, :], dsum[:, :], AX.X, ALU.add))
                dve.nop().then_inc(sem("d_total"), 1)
                dve.wait_ge(sem("d_sum"), it + 1)
                link(ts(c1(DIFF), ps_m[:, bank, 0:1], 1.0 / (B * T * C), None, ALU.mult))
                if it:
                    link(ts(c1(LIM), c1(DIFF), col(FAC), col(THR), ALU.mult, ALU.add))
                    link(tt(c1(DONE), c1(DIFF), c1(LIM), ALU.is_lt))
                    link(ts(c1(KEEP), c1(DONE), -1.0, 1.0, ALU.mult, ALU.add))
                floor(UP, UP_WIN)
                floor(DN, DOWN_WIN)
                link(ts(c1(GUP), c1(DIFF), UP_DIFF, None, ALU.is_gt))
                link(ts(c1(GDN), c1(DIFF), DOWN_DIFF, None, ALU.is_lt))
                link(ts(c1(T0), c1(CW), float(MIN_SIZE), None, ALU.is_gt))
                link(tt(c1(GDN), c1(GDN), c1(T0), ALU.mult))
                link(tt(c1(DN), c1(DN), c1(CW), ALU.subtract))
                link(tt(c1(DN), c1(DN), c1(GDN), ALU.mult))
                link(tt(c1(NW), c1(DN), c1(CW), ALU.add))
                link(tt(c1(UP), c1(UP), c1(NW), ALU.subtract))
                link(tt(c1(UP), c1(UP), c1(GUP), ALU.mult))
                link(tt(c1(NW), c1(NW), c1(UP), ALU.add))
                link(ts(c1(CW), c1(NW), float(MIN_SIZE), float(T), ALU.max, ALU.min))
                link(ts(win_row[:, :], pos_row[:, :], c1(CW), MASKED, ALU.is_ge, ALU.mult))
                dve.nop().then_inc(sem("window_ready"), 1)
                link(ts(in_win[:, :], pos_col[:, :], c1(CW), None, ALU.is_lt))

            dve.sem_inc(sem("max_done"), 2)
            dve.sem_inc(sem("clamp_done"), 2)
            dve.sem_inc(sem("K_hi"), 1)
            dve.sem_inc(sem("M_comb"), 2)
            dve.sem_inc(sem("o_evac"), 2)
            dve.wait_ge(sem("consts"), CONSTS)
            dve.wait_ge(sem("loaded"), n_loads)
            for j in range(3):
                link(tt(e_buf[0][:, j, 0:P].rearrange("p (h d) -> p h d", h=H), block_mask[:, :, :],
                        head_w[:, j, :].unsqueeze(1).broadcast_to([P, H, HD]), ALU.mult))
            dve.nop().then_inc(sem("setup_vector"), 1)
            dve.wait_ge(sem("setup_tensor"), 5)
            for j in range(3):
                link(ts(block_w[:, j, :], ps_k[:, 0, j * P:(j + 1) * P], SC if j == 1 else 1.0, None, ALU.mult))
            for row in (block_w[:, 0, :], block_w[:, 1, :], rows[:, R_LQ, :], rows[:, R_LK, :]):
                per = row.rearrange("p (h d) -> p h d", h=H)
                link(red(hvar[:, 0:H], per, AX.X, ALU.add))
                link(stt(per, hvar[:, 0:H].unsqueeze(2).broadcast_to([P, H, HD]), -1.0 / HD, per, ALU.mult, ALU.add))
            link(ts(rows[:, R_BQ, :], rows[:, R_BQ, :], SC, None, ALU.mult))
            link(ts(bv_rep[:, :], ones[:, :], col(BV), None, ALU.mult))
            dve.nop().then_inc(sem("setup_vector"), 1)
            dve.wait_ge(sem("setup_tensor"), 7)
            link(tt(v_bias[:, :], ps_q[:, 1, 0:P], rows[:, R_LV, :], ALU.add))
            link(dve.memset(c1(CW), float(max(min(T, 256), MIN_SIZE))))
            temperatures()

            with dve.Fori(0, B // 2) as i:
                for p in range(2):
                    n = i * 2 + p
                    ffn(n * 2, n * 3, n)
                    causal_front(n, n * 3 + 1, p, n)
                    maxima(n, True)
                    clamps(n)
                    causal_back(n, n)
                    ffn(n * 2 + 1, n * 3 + 2, n)
            mix_front(0, 0, 0)
            mixture_groups(dve, lambda g, u: mixture(g, u, 0, True))
            key_stats1(NG - 1)
            key_norm1(NG - 1)
            key_stats2(NG - 1)
            key_norm2(NG - 1)
            key_queries(NG - 1)
            key_keys(NG - 1)
            key_values(NG - 1)
            key_heads(NG - 1)
            dve.wait_ge(sem("K_out"), (NG + 1) * 16 * GB)
            links = step_at[0]

            def fast():
                step_at[0] = links
                fast_focus()

            def general():
                step_at[0] = links
                general_focus()

            any_path(dve, fast, general)
            mix_front(NG, 0, 0)
            mixture_groups(dve, lambda g, u: mixture(g, u, NG, False))



_INS = ['L0_attn_x', 'L0_attn_w_qkv', 'L0_attn_w_proj', 'L0_ffn_W_r', 'L0_ffn_W_k', 'L0_ffn_W_v', 'L0_ffn_mu_r',
        'L0_ffn_mu_k', 'L1_attn_Wq', 'L1_attn_bq', 'L1_attn_Wk', 'L1_attn_Wv', 'L1_attn_bv', 'L1_attn_Wo',
        'L1_attn_bo', 'L1_attn_lna_w', 'L1_attn_lnb_w', 'L1_attn_lnc_w', 'L1_attn_lnd_w', 'L1_attn_lq_w',
        'L1_attn_lq_b', 'L1_attn_lk_w', 'L1_attn_lk_b', 'L1_attn_lv_w', 'L1_attn_lv_b', 'L1_attn_threshold',
        'L1_attn_temp_base', 'L1_attn_factor', 'L1_ffn_Wr', 'L1_ffn_br', 'L1_ffn_W1', 'L1_ffn_b1', 'L1_ffn_W2',
        'L1_ffn_b2']


def kernel(**inputs):
    import concourse.bacc as _bacc
    from concourse.bass_utils import run_bass_kernel_spmd as _run

    nc = _bacc.Bacc("TRN2", target_bir_lowering=False, num_devices=1)
    arrays, args = {}, {}
    for name in _INS:
        v = np.ascontiguousarray(inputs[name])
        arrays[f"in_{name}_dram"] = v
        args[name] = nc.dram_tensor(f"in_{name}_dram", v.shape, mybir.dt.from_np(v.dtype), kind="ExternalInput").ap()
    out = nc.dram_tensor("out_0_dram", (B, T, C), F32, kind="ExternalOutput").ap()
    macaron_kernel(nc, args, out)
    r = _run(nc, [arrays], core_ids=[0])
    return r.results[0]["out_0_dram"]
```

```python
from contextlib import ExitStack

import numpy as np

import concourse.bass as bass
from concourse import mybir

F32 = mybir.dt.float32
BF16 = mybir.dt.bfloat16
I32 = mybir.dt.int32
ALU = mybir.AluOpType
ACT = mybir.ActivationFunctionType
AX = mybir.AxisListType

P = 128
B, T, C = 16, 256, 128
H, HD = 16, 8
NT = T // P
EXP, HID = 8, 256
NF = HID // P
GB = 2
GT = GB * NT
NG = B // GB
HG = 4
VW = 32
MIN_SIZE, MAX_ITER = 64, 3
UP_WIN, DOWN_WIN, UP_DIFF, DOWN_DIFF = 1.1, 0.9, 0.05, 0.001
EPS = 1e-5
CLIP, DEN_EPS, P_EPS = 100.0, 1e-6, 1e-8
MASKED = -1.0e30
MAX_SAFE, CLIP_SAFE, V_SAFE = 55.0, 80.0, 60.0
SHIFT = 18.0
LOW = float(np.exp(np.float64(SHIFT - CLIP)))
SAFE = 60.0
SC = HD ** -0.25
INV_SQRT = HD ** -0.5

ROWS_QK = 9 * HD
ROW_WIN = ROWS_QK
ROW_MAX = ROWS_QK + 1
ROWS_P1 = ROWS_QK + 1
ROWS_P2 = ROW_MAX + 6
HP = H // 2
NGV = H // HG
PLANE = C * T

W_Q0, W_K0, W_V0, W_P0, W_R, W_K, W_V, W_Q1, W_O1, W_K1, W_V1 = range(11)


def macaron_kernel(nc, a, out):
    ctx = ExitStack()
    with ctx:
        def sb(name, shape, dt=F32):
            return ctx.enter_context(nc.sbuf_tensor(name, shape, dt))

        def pb(name, shape, dt=F32):
            return ctx.enter_context(nc.psum_tensor(name, shape, dt))

        made = {}

        def sem(name):
            if name not in made:
                made[name] = ctx.enter_context(nc.semaphore(name))
            return made[name]

        x = sb("x", [P, B, NT * C])
        qcur = sb("qcur", [P, B, NT * C])
        heads_out = sb("heads_out", [P, B, NT * C])
        vp_all = sb("vp_all", [P, B, NT * C])

        w_t = sb("w_t", [P, 11, C])
        w1 = sb("w1", [P, EXP, HID])
        w2 = sb("w2", [P, EXP * NF, C])
        wr = sb("wr", [P, EXP])
        b2 = sb("b2", [EXP, C])
        b1_nat = sb("b1_nat", [EXP * NF, P])
        b1_t = sb("b1_t", [P, EXP * NF])
        cols = sb("cols", [P, 8])
        MU_R, MU_K, LNA, LNB, BV, THR, TMP, FAC = range(8)
        rows = sb("rows", [P, 7, C])
        R_BQ, R_BO, R_LQ, R_LK, R_LV, R_LNC, R_LND = range(7)
        v_bias = sb("v_bias", [P, C])
        br_row = sb("br_row", [P, EXP])
        head_w = sb("head_w", [P, 3, HD])
        block_w = sb("block_w", [P, 3, C])
        block_mask = sb("block_mask", [P, H, HD])
        bv_rep = sb("bv_rep", [P, P])

        ident = sb("ident", [P, P])
        ident_b = sb("ident_b", [P, P], BF16)
        ones = sb("ones", [P, P])
        ones_b = sb("ones_b", [P, T], BF16)
        mask_q = sb("mask_q", [P, 2 * P], BF16)
        mask_k = sb("mask_k", [P, 2 * P], BF16)
        sel_l = sb("sel_l", [P, P], BF16)
        k_const = sb("k_const", [P, T], BF16)
        pos_row = sb("pos_row", [P, T])
        pos_col = sb("pos_col", [P, NT])
        tri = sb("tri", [P, EXP, EXP])

        st = sb("st", [P, GT, 6])
        mv = sb("mv", [P, GT, 2])
        lnv = sb("lnv", [P, GT])
        rstd = sb("rstd", [P, GT])
        y = sb("y", [P, GT, C])
        y_b = y[:, NT:2 * NT, :]
        y2 = sb("y2", [P, GT, C])
        y3 = sb("y3", [P, GT, C])
        y_t = sb("y_t", [P, 1 + T])
        mix = sb("mix", [P, 8, T])
        dy, xr, xk, er, rec, kr, ka, gated = [mix[:, i, :] for i in range(8)]
        z_t = sb("z_t", [P, GT * P])
        v_tok = sb("v_tok", [P, NT, H, HD])
        vs = sb("vs", [P, 3, H, HD])
        mx = sb("mx", [P, H, 3])
        rmax = sb("rmax", [P, NT, H])
        emax = sb("emax", [P, NT, H])
        low_behind = sb("low_behind", [P, NT])
        qk_max = sb("qk_max", [H, B, 2])
        qk_bound = sb("qk_bound", [H, B])
        top = sb("top", [P, B])
        safe = sb("safe", [P, 4])
        redo = sb("redo", [P, 1], I32)
        behind = sb("behind", [P, P])
        head_sum = sb("head_sum", [P, H])
        st_k = sb("st_k", [P, GT, 6])
        mv_k = sb("mv_k", [P, GT, 2])
        lnv_k = sb("lnv_k", [P, GT])
        rstd_k = sb("rstd_k", [P, GT])
        qk32 = sb("qk32", [P, 2, T])
        rest = sb("rest", [P, 2, T])
        parts = sb("parts", [P, 2, 3, T], BF16)
        cen = sb("cen", [P, GT, H, HD])
        squares = cen.rearrange("p t h d -> p (t h d)")
        sqr = sb("sqr", [P, GT, H, HD])
        nrm = sb("nrm", [P, GT, HD, H])
        hvar = sb("hvar", [P, GT * H])
        hln = sb("hln", [P, GT * H])
        hrs = sb("hrs", [P, GT * H])

        q_st = [sb(f"q_st{p}", [P, H, T], BF16) for p in range(2)]
        k_st = [sb(f"k_st{p}", [P, H, T], BF16) for p in range(2)]
        v_st = [sb(f"v_st{p}", [P, NT, H, VW]) for p in range(2)]
        nmax = sb("nmax", [P, NT, H])
        ml = sb("ml", [P, NT, 2, H])
        ml32 = sb("ml32", [2 * H, T])
        ml_rest = sb("ml_rest", [2 * H, T])
        ml_parts = sb("ml_parts", [2 * H, 3, T], BF16)
        e_buf = [sb(f"e_buf{g}", [P, HG, 2 * T]) for g in range(2)]
        w_nat = e_buf[1].rearrange("p a (b c) -> p (a b) c", c=C)
        o_sb = sb("o_sb", [P, H // HG, T])
        s_sum = sb("s_sum", [P, NT, H])
        s_u = sb("s_u", [P, NT, H])
        s_du = sb("s_du", [P, NT, H])
        s_den = sb("s_den", [P, NT, H])
        s_rec = sb("s_rec", [P, NT, H])
        corr = sb("corr", [P, NT, H, HD])
        corr2 = sb("corr2", [P, H, HD])
        o_tok = sb("o_tok", [P, NT, H, HD])
        o_prev = sb("o_prev", [P, NT * C])
        q_tok = sb("q_tok", [P, NT * C])
        o_t = sb("o_t", [P, T])

        dsum = sb("dsum", [P, B])
        dtot = sb("dtot", [P, 1])
        ctl = sb("ctl", [P, 24])
        DIFF, LIM, DONE, KEEP, CW, UP, DN, GUP, GDN, T0, T1, NW, BND = range(13)
        temps = sb("temps", [P, 5, MAX_ITER])
        TEMP, T_POS, T_SAFE, T_LN, Q_SC = range(5)
        ctl_i = sb("ctl_i", [P, 2], I32)
        path = sb("path", [P, 1], I32)
        in_win = sb("in_win", [P, NT])
        win_row = sb("win_row", [P, T], BF16)

        ym_t = [mix[:, 2 * i:2 * i + 2, :].rearrange("p a t -> p (a t)") for i in range(2)]
        lg = sb("lg", [P, GT, EXP])
        gt_ = sb("gt_", [P, GT, EXP, EXP])
        eq_ = sb("eq_", [P, GT, EXP, EXP])
        rank = sb("rank", [P, GT, EXP])
        lmax = sb("lmax", [P, GT])
        lexp = sb("lexp", [P, GT, EXP])
        gsum = sb("gsum", [P, GT])
        gate = [sb(f"gate{i}", [P, GT, EXP]) for i in range(2)]
        h_sb = [e_buf[i][:, 0:NF, :] for i in range(2)]
        acc = [e_buf[i][:, NF, :].rearrange("p (t c) -> p t c", t=GT) for i in range(2)]
        gate_t = e_buf[1][0:EXP, NF + 1, :]

        q_chan = y_t[:, 1:1 + T]
        q_nrm = y[:, 0:NT, :].rearrange("p t (d h) -> p t d h", d=HD)

        ps_q = pb("ps_q", [P, 2, 512])
        ps_k = pb("ps_k", [P, 2, 512])
        ps_o = pb("ps_o", [P, 2, 512])
        ps_m = pb("ps_m", [P, 2, 512])
        MIX_BANK = [ps_m[:, 0, :], ps_o[:, 1, :], ps_k[:, 1, :]]
        SQUARES = [ps_m[:, 1, :], ps_k[:, 1, :], ps_o[:, 0, :]]

        BACK_BANK = [ps_m[:, 1, :], ps_k[:, 1, :]]

        scr_q = nc.dram_tensor("scr_q", (2, 3, PLANE), BF16, kind="Internal").ap()
        scr_k = nc.dram_tensor("scr_k", (B, 3, PLANE), BF16, kind="Internal").ap()
        scr_m = nc.dram_tensor("scr_m", (2, 3, 2 * H * T), BF16, kind="Internal").ap()

        def on_all(src, dims):
            return bass.AP(src.tensor, 0, [[0, P]] + dims)

        def col(j):
            return cols[:, j:j + 1]

        def c1(j):
            return ctl[:, j:j + 1]

        SETUP_DMAS, lots = [], []
        CONSTS = 41
        FIRST_CONSTS = 3
        LAST = MAX_ITER * B

        def follow(n, j, by):
            if isinstance(j, int):
                return (n + by, (j + by) % B) if n + by < LAST else None
            return n + by, j + by

        def fast_steps(eng, it, body):
            n0 = it * B

            def one(j, p, half):
                body(n0 + j, j, p, half + (n0 + B) // 2)

            one(0, 0, 0)
            with eng.Fori(0, (B - 4) // 2) as i:
                one(i * 2 + 1, 1, i)
                one(i * 2 + 2, 0, i + 1)
            for j in range(B - 3, B):
                one(j, j % 2, j // 2)

        def causal_steps(eng, body):
            body(0, 0, 0)
            body(1, 1, 0)
            with eng.Fori(0, (B - 6) // 2) as i:
                body(i * 2 + 2, 0, i + 1)
                body(i * 2 + 3, 1, i + 1)
            for n in range(B - 4, B):
                body(n, n % 2, n // 2)

        def within(n, low, high):
            return not isinstance(n, int) or low <= n <= high

        mix_order, norm_order = [(1, 0), (1, 1), (1, 2)], [(1, 0), (1, 1), (2, 0), (1, 2), (2, 1), (1, 3)]
        for n in range(B + 2):
            mix_order += [(k, b) for k, b in ((1, n + 3), (2, n - 2)) if 0 <= b < B]
            norm_order += [(k, b) for k, b in ((3, n - 2), (2, n + 2), (1, n + 4)) if 0 <= b < B]

        def place(order, kind, b, line):
            if isinstance(b, int):
                return order.index((kind, b))
            return b * line[0] + line[1]

        def mix1(f):
            return place(mix_order, 1, f, (2, -5))

        def mix2(b):
            return place(mix_order, 2, b, (2, 6))

        def norm1(f):
            return place(norm_order, 1, f, (3, -6))

        def norm2(f):
            return place(norm_order, 2, f, (3, -1))

        def norm3(b):
            return place(norm_order, 3, b, (3, 10))

        MIXES, NORMS = 2 * B, 3 * B

        def redo_causal(eng, general):
            eng.wait_ge(sem("setup_vector"), 5)
            with eng.If(eng.value_load(redo[0:1, 0:1], min_val=0, max_val=1) > 0):
                general()

        def general_base(eng):
            return eng.value_load(redo[0:1, 0:1], min_val=0, max_val=1) * B

        def mixture_groups(eng, body):
            body(0, 0)
            with eng.Fori(0, (NG - 2) // 2) as i:
                body(i * 2 + 1, 1)
                body(i * 2 + 2, 0)
            body(NG - 1, (NG - 1) % 2)

        def any_path(eng, fast, general):
            eng.wait_ge(sem("path_ready"), 1)
            with eng.If(eng.value_load(path[0:1, 0:1], min_val=0, max_val=1) > 0):
                fast()
            with eng.Else():
                general()

        block = ctx.enter_context(nc.Block())

        @block.sync
        def _(sp):
            loads = sem("loaded")

            def load(dst, src):
                sp.dma_start(dst, src).then_inc(loads, 16)
                SETUP_DMAS.append(1)

            load(w_nat[:, 0:3, :], a["L0_attn_w_qkv"].rearrange("(s o) c -> o s c", s=3))
            for j, name in ((3, "L0_attn_w_proj"), (4, "L0_ffn_W_r"), (5, "L0_ffn_W_k"), (6, "L0_ffn_W_v"),
                            (7, "L1_attn_Wq"), (8, "L1_attn_Wo")):
                load(w_nat[:, j, :], a[name])
            load(x[:, :, :].rearrange("p b (t c) -> p (b t) c", c=C),
                 a["L0_attn_x"].rearrange("b (t p) c -> p (b t) c", p=P))
            for j, name in ((MU_R, "L0_ffn_mu_r"), (MU_K, "L0_ffn_mu_k"), (LNA, "L1_attn_lna_w")):
                load(col(j), a[name].rearrange("(p o) -> p o", o=1))
            lots.append(16 * len(SETUP_DMAS))
            sp.wait_ge(loads, lots[0])
            for j, name in ((9, "L1_attn_Wk"), (10, "L1_attn_Wv")):
                load(w_nat[:, j, :], a[name])
            for j, name in enumerate(("L1_attn_lq_w", "L1_attn_lk_w", "L1_attn_lv_w")):
                load(head_w[:, j, :], bass.AP(a[name].tensor, 0, [[0, H], [HD, HD], [1, HD]]))
            load(b1_nat[:, :], a["L1_ffn_b1"].rearrange("e (t p) -> (e t) p", p=P))
            for j, name in ((LNB, "L1_attn_lnb_w"), (BV, "L1_attn_bv")):
                load(col(j), a[name].rearrange("(p o) -> p o", o=1))
            for j, name in ((THR, "L1_attn_threshold"), (TMP, "L1_attn_temp_base"), (FAC, "L1_attn_factor")):
                load(col(j), on_all(a[name], [[1, 1]]))
            for j, name in ((R_BQ, "L1_attn_bq"), (R_BO, "L1_attn_bo")):
                load(rows[:, j, :], on_all(a[name], [[1, C]]))
            for j, name in ((R_LQ, "L1_attn_lq_b"), (R_LK, "L1_attn_lk_b"), (R_LV, "L1_attn_lv_b"),
                            (R_LNC, "L1_attn_lnc_w"), (R_LND, "L1_attn_lnd_w")):
                load(rows[:, j, :].rearrange("p (h d) -> p h d", h=H), on_all(a[name], [[0, H], [1, HD]]))
            load(br_row[:, :], on_all(a["L1_ffn_br"], [[1, EXP]]))
            load(wr[:, :], a["L1_ffn_Wr"])
            load(b2[:, :], a["L1_ffn_b2"])
            lots.append(16 * len(SETUP_DMAS))
            sp.wait_ge(loads, lots[1])
            load(w1[:, :, :], a["L1_ffn_W1"].rearrange("e h f -> h e f"))
            load(w2[:, :, :], a["L1_ffn_W2"].rearrange("e (t p) h -> p (e t) h", p=P))
            sp.wait_ge(sem("consts"), CONSTS)
            for p in range(2):
                load(k_st[p][ROW_WIN:ROWS_P2, :, :],
                     k_const[ROW_WIN:ROWS_P2, :].unsqueeze(1).broadcast_to([ROWS_P2 - ROW_WIN, H, T]))
                load(q_st[p][ROW_WIN:ROW_WIN + 1, :, :], ones_b[0:1, :].unsqueeze(1).broadcast_to([1, H, T]))

            def hold():
                sp.sem_inc(sem("held"), 1)

            def operands(n, p, b, with_k):
                sp.wait_ge(sem("parts_ready"), n + B + 1)
                hold()
                sp.dma_start(bass.AP(scr_q.tensor, p * 3 * PLANE, [[T, C], [PLANE, 3], [1, T]]),
                             parts[:, 0, :, :]).then_inc(sem("parts_out"), 16)
                if with_k:
                    sp.dma_start(scr_k[b].rearrange("j (c t) -> c j t", t=T),
                                 parts[:, 1, :, :]).then_inc(sem("k_parts_out"), 16)
                    sp.wait_ge(sem("k_parts_out"), (n + B) * 16 + 32)
                    hold()
                sp.wait_ge(sem("parts_out"), (n + B) * 16 + 32)
                hold()
                sp.wait_ge(sem("operands_free"), n + 1)
                hold()
                for j in range(3):
                    sp.dma_start(q_st[p][24 * j:24 * j + 24, :, :].rearrange("r h t -> r (h t)"),
                                 bass.AP(scr_q.tensor, (p * 3 + j) * PLANE, [[0, 3], [H * T, HD], [1, H * T]]))\
                      .then_inc(sem("operands_in"), 16)
                for j in range(3):
                    sp.dma_start(k_st[p][24 * j:24 * j + 24, :, :].rearrange("r h t -> r (h t)"),
                                 scr_k[b].rearrange("j (d n) -> (j d) n", n=H * T))\
                      .then_inc(sem("operands_in"), 16)

            def max_rows(n, p):
                sp.wait_ge(sem("ml_parts_ready"), n + 1)
                hold()
                sp.dma_start(bass.AP(scr_m.tensor, p * 3 * 2 * H * T, [[T, 2 * H], [2 * H * T, 3], [1, T]]),
                             ml_parts[:, :, :]).then_inc(sem("ml_out"), 16)
                sp.wait_ge(sem("ml_out"), n * 16 + 16)
                hold()
                sp.dma_start(q_st[p][ROW_MAX:ROWS_P2, :, :].rearrange("r h t -> r (h t)"),
                             bass.AP(scr_m.tensor, p * 3 * 2 * H * T, [[H * T, 6], [1, H * T]]))\
                  .then_inc(sem("ml_in"), 16)

            def key_parts(g):
                sp.wait_ge(sem("K_parts"), g + 1)
                for u in range(GB):
                    sp.dma_start(scr_k[g * GB + u].rearrange("j (c t) -> c j t", t=T),
                                 parts[:, u, :, :]).then_inc(sem("K_out"), 16)

            def fast_operands(f, b, p, half):
                sp.wait_ge(sem("fast_parts"), f + 1)
                hold()
                sp.dma_start(bass.AP(scr_q.tensor, p * 3 * PLANE, [[T, C], [PLANE, 3], [1, T]]),
                             parts[:, p, :, :]).then_inc(sem("fast_parts_out"), 16)
                sp.wait_ge(sem("fast_scores"), (f + B - 1) * HP)
                hold()
                for j in range(3):
                    sp.dma_start(k_st[p][24 * j:24 * j + 24, :, :].rearrange("r h t -> r (h t)"),
                                 scr_k[b].rearrange("j (d n) -> (j d) n", n=H * T))\
                      .then_inc(sem(f"fast_operands_in_{p}"), 16)
                sp.wait_ge(sem("fast_parts_out"), f * 16 + 16 + 32)
                hold()
                for j in range(3):
                    sp.dma_start(q_st[p][24 * j:24 * j + 24, :, :].rearrange("r h t -> r (h t)"),
                                 bass.AP(scr_q.tensor, (p * 3 + j) * PLANE, [[0, 3], [H * T, HD], [1, H * T]]))\
                      .then_inc(sem(f"fast_operands_in_{p}"), 16)

            def window_rows(it):
                sp.wait_ge(sem("window_ready"), it)
                for p in range(2):
                    sp.dma_start(k_st[p][ROW_WIN:ROW_WIN + 1, :, :],
                                 win_row[0:1, :].unsqueeze(1).broadcast_to([1, H, T]))\
                      .then_inc(sem("window_in"), 16)

            def fast_focus():
                sp.wait_ge(sem("K_out"), NG * 16 * GB)
                fast_operands(0, 0, 0, B // 2)
                fast_operands(1, 1, 1, B // 2)
                key_parts(NG - 1)
                sp.wait_ge(sem("K_out"), (NG + 1) * 16 * GB)
                for it in range(MAX_ITER):
                    if it:
                        window_rows(it)

                    def body(n, b, p, half):
                        ahead = follow(n, b, 2)
                        if ahead:
                            fast_operands(*ahead, p, half + 1)

                    fast_steps(sp, it, body)

            def general_focus():
                key_parts(NG - 1)
                sp.wait_ge(sem("K_out"), (NG + 1) * 16 * GB)
                base = general_base(sp)
                for it in range(MAX_ITER):
                    if it:
                        window_rows(it)
                    with sp.Fori(0, B // 2) as i:
                        for p in range(2):
                            n = base + it * B + i * 2 + p
                            operands(n, p, i * 2 + p, False)
                            max_rows(n, p)

            sp.sem_inc(sem("fast_parts_out"), 32)
            sp.sem_inc(sem("K_out"), 16 * GB)
            sp.sem_inc(sem("parts_out"), 16)
            sp.sem_inc(sem("k_parts_out"), 16)

            def causal_operands(f, p, half):
                sp.wait_ge(sem("parts_ready"), f + 1)
                hold()
                sp.dma_start(bass.AP(scr_q.tensor, p * 3 * PLANE, [[T, C], [PLANE, 3], [1, T]]),
                             parts[:, 0, :, :]).then_inc(sem("parts_out"), 16)
                sp.dma_start(scr_k[f].rearrange("j (c t) -> c j t", t=T),
                             parts[:, 1, :, :]).then_inc(sem("k_parts_out"), 16)
                if not isinstance(f, int) or f >= 2:
                    sp.wait_ge(sem("fast_scores"), (f - 1) * HP)
                    hold()
                sp.wait_ge(sem("parts_out"), f * 16 + 32)
                hold()
                for j in range(3):
                    sp.dma_start(q_st[p][24 * j:24 * j + 24, :, :].rearrange("r h t -> r (h t)"),
                                 bass.AP(scr_q.tensor, (p * 3 + j) * PLANE, [[0, 3], [H * T, HD], [1, H * T]]))\
                      .then_inc(sem(f"fast_operands_in_{p}"), 16)
                sp.wait_ge(sem("k_parts_out"), f * 16 + 32)
                hold()
                for j in range(3):
                    sp.dma_start(k_st[p][24 * j:24 * j + 24, :, :].rearrange("r h t -> r (h t)"),
                                 scr_k[f].rearrange("j (d n) -> (j d) n", n=H * T))\
                      .then_inc(sem(f"fast_operands_in_{p}"), 16)

            def causal_round(n, p, half):
                if isinstance(n, int) and n in (0, B - 1):
                    return
                causal_operands(n + 1, 1 - p, half)

            sp.wait_ge(loads, 16 * len(SETUP_DMAS))
            causal_operands(0, 0, 0)
            causal_operands(1, 1, 0)
            causal_steps(sp, causal_round)

            def general_causal():
                sp.wait_ge(sem("F_x"), MIXES + 1)
                load(x[:, :, :].rearrange("p b (t c) -> p (b t) c", c=C),
                     a["L0_attn_x"].rearrange("b (t p) c -> p (b t) c", p=P))
                SETUP_DMAS.pop()
                with sp.Fori(0, B // 2) as i:
                    for p in range(2):
                        operands(i * 2 + p, p, i * 2 + p, True)
                        max_rows(i * 2 + p, p)

            redo_causal(sp, general_causal)
            with sp.Fori(0, NG - 1) as g:
                key_parts(g)
            any_path(sp, fast_focus, general_focus)
            with sp.Fori(0, NG) as g:
                sp.wait_ge(sem("M_x"), NG + g + 1)
                sp.dma_start(out.rearrange("b (t p) c -> p (b t) c", p=P)[:, bass.ds(g * GT, GT), :],
                             x[:, bass.ds(g * GB, GB), :].rearrange("p b (t c) -> p (b t) c", c=C))\
                  .then_inc(sem("stored"), 16)
            sp.wait_ge(sem("stored"), NG * 16)

        n_loads = 16 * len(SETUP_DMAS)

        @block.gpsimd
        def _(pool):
            done = [0]

            def const(ins):
                ins.then_inc(sem("consts"), 1)
                done[0] += 1
                pool.wait_ge(sem("consts"), done[0])

            def select(t, op, fill, base, pattern, step):
                const(pool.affine_select(out=t, in_=t, compare_op=op, fill=fill, base=base, pattern=pattern,
                                         channel_multiplier=step))

            const(pool.memset(ident[:, :], 0.0))
            select(ident[:, :], ALU.not_equal, 1.0, 0, [[-1, P]], 1)
            const(pool.memset(y_t[:, 0:1], 0.0))
            assert done[0] == FIRST_CONSTS
            for t in (ident_b, mask_q, mask_k, sel_l, k_const, head_sum):
                const(pool.memset(t[:, :], 0.0))
            for t in (ones, ones_b, behind):
                const(pool.memset(t[:, :], 1.0))
            for t in (block_mask, tri):
                const(pool.memset(t[:, :, :], 1.0))
            for p in range(2):
                const(pool.memset(v_st[p][:, :, :, :], 0.0))
                const(pool.memset(v_st[p][:, :, :, HD:HD + 1], 1.0))
            select(ident_b[:, :], ALU.not_equal, 1.0, 0, [[-1, P]], 1)
            select(mask_q[:, :], ALU.is_ge, MASKED, 0, [[0, 2], [-1, P]], 1)
            select(mask_k[:, :], ALU.is_ge, MASKED, 0, [[0, 2], [1, P]], -1)
            for j in range(3):
                select(k_const[:, :], ALU.not_equal, 1.0, -(ROW_MAX + 2 * j), [[0, T]], 1)
                select(sel_l[:, :], ALU.not_equal, 1.0, -(ROW_MAX + 2 * j + 1), [[0, P]], 1)
            select(behind[:, :], ALU.is_gt, 0.0, 0, [[-1, P]], 1)
            for d in range(HD):
                select(head_sum[:, :], ALU.not_equal, 1.0, -d * H, [[-1, H]], 1)
            select(block_mask[:, :, :], ALU.is_ge, 0.0, 0, [[-HD, H], [0, HD]], 1)
            select(block_mask[:, :, :], ALU.is_ge, 0.0, HD - 1, [[HD, H], [0, HD]], -1)
            select(tri[:, :, :], ALU.is_gt, 0.0, 0, [[1, EXP], [-1, EXP]], 0)
            const(pool.iota(pos_row[:, :], pattern=[[1, T]], base=0, channel_multiplier=0,
                            allow_small_or_imprecise_dtypes=True))
            const(pool.iota(pos_col[:, :], pattern=[[P, NT]], base=0, channel_multiplier=1,
                            allow_small_or_imprecise_dtypes=True))
            assert done[0] == CONSTS

            def hold():
                pool.sem_inc(sem("held"), 1)

            def mix_step(i, l):
                pool.wait_ge(sem("T_ytc"), l + 1)
                pool.tensor_tensor(dy[:, :], y_t[:, 1:T + 1], y_t[:, 0:T], ALU.subtract).then_inc(sem("F_dy"), 1)

            def mix_square(i):
                pool.wait_ge(sem("F_kr"), i + 1)
                pool.tensor_tensor(ka[:, :], kr[:, :], kr[:, :], ALU.mult).then_inc(sem("F_ka"), 1)

            def mix_gate(i):
                pool.wait_ge(sem("F_ln"), i * 2 + 2)
                pool.tensor_tensor(er[:, :], er[:, :], rec[:, :], ALU.add).then_inc(sem("F_sum"), 1)

            def mix_add(i, b):
                pool.wait_ge(sem("F_gated"), i + 1)
                hold()
                pool.tensor_tensor(x[:, b, :], x[:, b, :], gated[:, :], ALU.add).then_inc(sem("F_x"), 1)

            def ffn(i, l, b):
                mix_step(i, l)
                mix_square(i)
                mix_gate(i)
                mix_add(i, b)

            def split(n, s):
                pool.wait_ge(sem("part_hi"), n + B + 1)
                pool.tensor_tensor(rest[:, 0:s, :], qk32[:, 0:s, :], parts[:, 0:s, 0, :], ALU.subtract)\
                    .then_inc(sem("part_rest"), 1)
                pool.wait_ge(sem("part_mid"), n + B + 1)
                pool.tensor_tensor(parts[:, 0:s, 2, :], rest[:, 0:s, :], parts[:, 0:s, 1, :], ALU.subtract)\
                    .then_inc(sem("parts_ready"), 1)

            def maxima(n):
                pool.wait_ge(sem("ml_hi"), n + 1)
                pool.tensor_tensor(ml_rest[:, :], ml32[:, :], ml_parts[:, 0, :], ALU.subtract)\
                    .then_inc(sem("ml_rest"), 1)
                pool.wait_ge(sem("ml_mid"), n + 1)
                pool.tensor_tensor(ml_parts[:, 2, :], ml_rest[:, :], ml_parts[:, 1, :], ALU.subtract)\
                    .then_inc(sem("ml_parts_ready"), 1)

            def causal_parts(f):
                pool.wait_ge(sem("part_hi"), f + 1)
                pool.tensor_tensor(rest[:, :, :], qk32[:, :, :], parts[:, :, 0, :], ALU.subtract)\
                    .then_inc(sem("part_rest"), 1)
                pool.wait_ge(sem("part_rest"), f + 1)
                hold()
                pool.tensor_copy(parts[:, :, 1, :], rest[:, :, :]).then_inc(sem("part_mid"), 1)

            def causal_last_parts(f):
                pool.wait_ge(sem("part_mid"), f + 1)
                pool.tensor_tensor(parts[:, :, 2, :], rest[:, :, :], parts[:, :, 1, :], ALU.subtract)\
                    .then_inc(sem("parts_ready"), 1)

            def causal_values(n, p):
                if not isinstance(n, int) or n >= 2:
                    pool.wait_ge(sem("fast_values"), (n - 1) * NGV + 2)
                pool.wait_ge(sem("G_vc"), n + 1 + 1)
                hold()
                pool.tensor_copy(v_st[p][:, :, :, 0:HD], v_tok[:, :, :, :]).then_inc(sem("fast_v"), 1)

            def causal_round(n, p, half):
                first, second, after = within(n, 0, B - 4), within(n, 2, B), within(n, 0, B - 2)
                if first:
                    mix_step(mix1(n + 3), norm1(n + 3))
                if within(n, 1, B - 2):
                    causal_parts(n + 1)
                if first:
                    mix_square(mix1(n + 3))
                    mix_gate(mix1(n + 3))
                if second:
                    mix_step(mix2(n - 2), norm3(n - 2))
                if within(n, 1, B - 2):
                    causal_last_parts(n + 1)
                if first:
                    mix_add(mix1(n + 3), n + 3)
                if second:
                    mix_square(mix2(n - 2))
                    mix_gate(mix2(n - 2))
                if after:
                    causal_values(n + 1, 1 - p)
                if second:
                    mix_add(mix2(n - 2), n - 2)

            pool.sem_inc(sem("F_x"), 1)
            ffn(mix1(0), norm1(0), 0)
            for f in range(2):
                mix_step(mix1(f + 1), norm1(f + 1))
                if f:
                    causal_last_parts(0)
                    causal_values(0, 0)
                mix_square(mix1(f + 1))
                mix_gate(mix1(f + 1))
                mix_add(mix1(f + 1), f + 1)
                causal_parts(f)
            causal_last_parts(1)
            causal_steps(pool, causal_round)
            ffn(mix2(B - 2), norm3(B - 2), B - 2)
            ffn(mix2(B - 1), norm3(B - 1), B - 1)

            def general_causal():
                with pool.Fori(0, B // 2) as i:
                    for p in range(2):
                        n = i * 2 + p
                        ffn(n * 2 + MIXES, n * 3 + NORMS, n)
                        split(n, 2)
                        maxima(n)
                        ffn(n * 2 + 1 + MIXES, n * 3 + 2 + NORMS, n)

            redo_causal(pool, general_causal)

            def key_parts(g):
                pool.wait_ge(sem("K_hi"), g + 1 + 1)
                pool.tensor_tensor(rest[:, :, :], qk32[:, :, :], parts[:, :, 0, :], ALU.subtract)\
                    .then_inc(sem("K_split"), 1)
                pool.wait_ge(sem("K_split"), g * 2 + 1)
                hold()
                pool.tensor_copy(parts[:, :, 1, :], rest[:, :, :]).then_inc(sem("K_split"), 1)
                pool.wait_ge(sem("K_split"), g * 2 + 2)
                pool.tensor_tensor(parts[:, :, 2, :], rest[:, :, :], parts[:, :, 1, :], ALU.subtract)\
                    .then_inc(sem("K_parts"), 1)

            with pool.Fori(0, NG - 1) as g:
                key_parts(g)

            def queries(f, b):
                pool.wait_ge(sem("query_t"), f + 1)
                pool.wait_ge(sem("fast_q_new"), f + 1)
                hold()
                pool.tensor_copy(q_tok[:, :], qcur[:, b, :]).then_inc(sem("query_tok"), 1)

            def values(n, b, p):
                pool.wait_ge(sem("fast_values"), (n + B - 1) * NGV + 2)
                hold()
                pool.tensor_copy(v_st[p][:, :, :, 0:HD],
                                 vp_all[:, b, :].rearrange("p (t h d) -> p t h d", t=NT, h=H))\
                    .then_inc(sem("fast_v"), 1)

            def query_parts(f, p):
                pool.wait_ge(sem("fast_hi"), f + 1 + 1)
                pool.tensor_tensor(rest[:, p, :], qk32[:, p, :], parts[:, p, 0, :], ALU.subtract)\
                    .then_inc(sem("fast_split"), 1)
                pool.wait_ge(sem("fast_split"), f * 2 + 1)
                hold()
                pool.tensor_copy(parts[:, p, 1, :], rest[:, p, :]).then_inc(sem("fast_split"), 1)
                pool.wait_ge(sem("fast_split"), f * 2 + 2)
                pool.tensor_tensor(parts[:, p, 2, :], rest[:, p, :], parts[:, p, 1, :], ALU.subtract)\
                    .then_inc(sem("fast_parts"), 1)

            def update(n, b, it):
                ot = o_tok[:, :, :, :].rearrange("p t h d -> p (t h d)")
                if it < MAX_ITER - 1:
                    pool.wait_ge(sem("d_part"), n + 1)
                    hold()
                    pool.tensor_copy(heads_out[:, b, :], ot)
                    pool.tensor_tensor(qcur[:, b, :], qcur[:, b, :], ot, ALU.add).then_inc(sem("fast_q_new"), 1)
                else:
                    xb = x[:, b, :].rearrange("p (t c) -> p t c", t=NT)
                    pool.tensor_tensor(xb, xb, rows[:, R_BO, :].unsqueeze(1).broadcast_to([P, NT, C]), ALU.add)\
                        .then_inc(sem("fast_bias"), 1)

            def fast_focus():
                pool.sem_inc(sem("query_t"), 1)
                pool.sem_inc(sem("fast_q_new"), B)
                pool.wait_ge(sem("K_read"), (NG - 1) * 3)
                queries(0, 0)
                values(0, 0, 0)
                queries(1, 1)
                query_parts(0, 0)
                queries(2, 2)
                query_parts(1, 1)
                key_parts(NG - 1)
                for it in range(MAX_ITER):
                    def body(n, b, p, half):
                        after = follow(n, b, 1)
                        if after:
                            values(*after, 1 - p)
                        ahead = follow(n, b, 3)
                        if ahead:
                            queries(*ahead)
                        if not (isinstance(b, int) and b == 0):
                            update(n - 1, b - 1, it)
                        ahead = follow(n, b, 2)
                        if ahead:
                            query_parts(ahead[0], p)

                    fast_steps(pool, it, body)
                    update(it * B + B - 1, B - 1, it)

            def general_focus():
                key_parts(NG - 1)
                base = general_base(pool)
                for it in range(MAX_ITER):
                    with pool.Fori(0, B // 2) as i:
                        for p in range(2):
                            n = base + it * B + i * 2 + p
                            split(n, 1)
                            maxima(n)

            any_path(pool, fast_focus, general_focus)

        @block.scalar
        def _(act):
            act.preload_act_table_set("natural_log_exp_and_others")
            act.wait_ge(sem("consts"), FIRST_CONSTS)

            def copy(dst, src, scale=1.0):
                return act.activation(dst, src, ACT.Copy, scale=scale)

            def rsqrt(pre, n, per, var, tmp, res, scale=1.0):
                act.wait_ge(sem(pre + "_mom"), n * per + per)
                act.activation(tmp, var, ACT.Ln, scale=scale, bias=EPS).then_inc(sem(pre + "_ln"), 1)
                act.wait_ge(sem(pre + "_ln"), n + 1)
                act.activation(res, tmp, ACT.Exp, scale=-0.5).then_inc(sem(pre + "_rstd"), 1)

            def token_norm(l, mv, lnv, rstd):
                rsqrt("T", l, NT, mv[:, 0:NT, 1], lnv[:, 0:NT], rstd[:, 0:NT])

            def ffn_tokens(i, l, bank):
                act.wait_ge(sem("T_yt"), l + 1)
                if not isinstance(i, int) or i:
                    act.wait_ge(sem("F_mix"), i * 2)
                copy(y_t[:, 1:T + 1], MIX_BANK[bank][:, 0:T]).then_inc(sem("T_ytc"), 1)

            def ffn_hidden(i, bank):
                act.wait_ge(sem("F_rk"), i + 1)
                if not isinstance(i, int) or i:
                    act.wait_ge(sem("F_gated"), i)
                k, r = MIX_BANK[bank][:, 0:T], MIX_BANK[bank][:, T:2 * T]
                act.activation(kr[:, :], k, ACT.Relu).then_inc(sem("F_kr"), 1)
                act.activation(er[:, :], r, ACT.Abs)
                act.activation(rec[:, :], r, ACT.Relu, scale=-1.0).then_inc(sem("F_er"), 1)
                act.wait_ge(sem("F_er"), i + 1)
                act.activation(er[:, :], er[:, :], ACT.Exp, scale=-1.0).then_inc(sem("F_ln"), 1)
                act.wait_ge(sem("F_ln"), i * 2 + 1)
                act.activation(er[:, :], er[:, :], ACT.Ln, bias=1.0).then_inc(sem("F_ln"), 1)

            def ffn_sigmoid(i):
                act.wait_ge(sem("F_sum"), i + 1)
                act.activation(rec[:, :], er[:, :], ACT.Exp, scale=-1.0).then_inc(sem("F_rec"), 1)

            def ffn(i, l):
                token_norm(l, mv, lnv, rstd)
                ffn_tokens(i, l, 0)
                ffn_hidden(i, 0)
                ffn_sigmoid(i)

            def split(n, s):
                act.wait_ge(sem("qk32"), (n + B) * 2 + 2)
                copy(parts[:, 0:s, 0, :], qk32[:, 0:s, :]).then_inc(sem("part_hi"), 1)
                act.wait_ge(sem("part_rest"), n + B + 1)
                copy(parts[:, 0:s, 1, :], rest[:, 0:s, :]).then_inc(sem("part_mid"), 1)

            def causal_front(n, l):
                token_norm(l, mv, lnv, rstd)
                act.wait_ge(sem("T_yt"), l + 1)
                copy(z_t[:, 0:T], ps_m[:, 0, 0:T]).then_inc(sem("T_ytc"), 1)
                act.wait_ge(sem("G_qk"), n + B + 1)
                copy(qk32[:, 0, :], ps_m[:, 1, 0:T], INV_SQRT).then_inc(sem("qk32"), 1)
                copy(qk32[:, 1, :], ps_m[:, 1, T:2 * T]).then_inc(sem("qk32"), 1)
                split(n, 2)

            def focus_front(n, f):
                act.wait_ge(sem("query_t"), f + 1)
                copy(o_t[:, :], ps_m[:, 0, 0:T]).then_inc(sem("query_tc"), 1)
                w = NT * H
                rsqrt("query", f, 1, hvar[:, 0:w], hln[:, 0:w], hrs[:, 0:w], 1.0 / HD)
                act.wait_ge(sem("query_nt"), f + 1)
                copy(qk32[:, 0, :], ps_m[:, 0, 0:T]).then_inc(sem("qk32"), 2)
                split(n, 1)

            def maxima(n, causal):
                if causal:
                    act.wait_ge(sem("ml_m"), n + 1)
                    act.activation(ml[:, :, 1, :], ml[:, :, 0, :], ACT.Exp, bias=-CLIP).then_inc(sem("ml_l"), 1)
                act.wait_ge(sem("ml_t"), n + 1)
                copy(ml32[:, :], ps_m[0:2 * H, 1, 0:T]).then_inc(sem("ml32"), 1)
                act.wait_ge(sem("ml32"), n + 1)
                copy(ml_parts[:, 0, :], ml32[:, :]).then_inc(sem("ml_hi"), 1)
                act.wait_ge(sem("ml_rest"), n + 1)
                copy(ml_parts[:, 1, :], ml_rest[:, :]).then_inc(sem("ml_mid"), 1)

            def exps(n, causal):
                w = 3 * P if causal else 2 * T
                for h in range(H):
                    g = h // HG
                    if h % HG == 0:
                        act.wait_ge(sem("values_done"), n * (H // HG) + g + 1)
                    act.wait_ge(sem("k_scores"), n * H + h + 1)
                    act.activation(e_buf[g % 2][:, h % HG, 0:w], ps_k[:, h % 2, 0:w], ACT.Exp)\
                        .then_inc(sem("exp_done"), 1)
                    if causal and h % HG == HG - 1 and g >= 1:
                        evacuate(n, g - 1)
                if causal:
                    evacuate(n, H // HG - 1)

            def evacuate(n, g):
                act.wait_ge(sem("values_done"), n * (H // HG) + g + 1 + 2)
                copy(o_sb[:, g, :], ps_o[:, g % 2, (g // 2) * T:(g // 2 + 1) * T]).then_inc(sem("o_evac"), 1)

            def normed_tokens(f):
                act.wait_ge(sem("T_yt"), norm2(f) + 1)
                copy(z_t[:, 0:T], ps_m[:, 0, 0:T]).then_inc(sem("T_ytc"), 1)

            def causal_parts(f):
                act.wait_ge(sem("G_qk"), f + 1)
                copy(qk32[:, 0, :], ps_m[:, 0, 0:T], INV_SQRT).then_inc(sem("qk32"), 1)
                copy(qk32[:, 1, :], ps_m[:, 0, T:2 * T]).then_inc(sem("qk32"), 1)
                act.wait_ge(sem("qk32"), f * 2 + 2)
                act.wait_ge(sem("parts_out"), f * 16 + 16)
                act.wait_ge(sem("k_parts_out"), f * 16 + 16)
                copy(parts[:, :, 0, :], qk32[:, :, :]).then_inc(sem("part_hi"), 1)
                act.activation(squares, qk32[:, :, :].rearrange("p s t -> p (s t)"), ACT.Square)\
                    .then_inc(sem("qk_squares"), 1)

            def causal_values(f):
                act.wait_ge(sem("G_v"), f + 1)
                if not isinstance(f, int) or f >= 1:
                    act.wait_ge(sem("fast_v"), f)
                copy(v_tok[:, :, :, :].rearrange("p t h d -> p (t h d)"), ps_m[:, 0, 0:T]).then_inc(sem("G_vc"), 1)

            def causal_exps(n, hp):
                g = hp * 2 // HG
                if hp * 2 % HG == 0:
                    act.wait_ge(sem("fast_values"), n * NGV + g + 1)
                act.wait_ge(sem("fast_scores"), n * HP + hp + 1)
                act.activation(e_buf[g % 2][:, hp * 2 % HG:hp * 2 % HG + 2, 0:3 * P], ps_k[:, :, 0:3 * P],
                               ACT.Exp, bias=SHIFT).then_inc(sem("fast_exp"), 1)

            def evacuate_group(n, g):
                act.wait_ge(sem("fast_values"), n * NGV + g + 1 + 2)
                if g == 0:
                    act.wait_ge(sem("fast_o_t"), n * NT + 2)
                copy(o_sb[:, g, :], ps_o[:, 0, 0:T]).then_inc(sem("fast_evac"), 1)

            def max_exps(n):
                act.wait_ge(sem("row_maxima"), n + 1)
                act.activation(emax[:, :, :], rmax[:, :, :], ACT.Exp, bias=SHIFT).then_inc(sem("max_exps"), 1)

            def value_sums(n):
                act.wait_ge(sem("v_sums"), n + 1)
                copy(vs[:, :, :, :].rearrange("p s h d -> p (s h d)"), ps_m[:, 1, 0:3 * P]).then_inc(sem("v_sums_c"), 1)

            def causal_out(b):
                act.wait_ge(sem("A_ott"), b + 1)
                copy(o_t[:, :], ps_m[:, 1, 0:T]).then_inc(sem("A_otc"), 1)

            def causal_round(n, p, half):
                before, first, second, ahead = within(n, 1, B), within(n, 0, B - 4), within(n, 2, B), within(n, 0, B - 3)
                causal_exps(n, 0)
                if before:
                    evacuate_group(n - 1, NGV - 1)
                if first:
                    ffn_tokens(mix1(n + 3), norm1(n + 3), 0)
                if before:
                    max_exps(n - 1)
                causal_exps(n, 1)
                causal_exps(n, 2)
                if first:
                    ffn_hidden(mix1(n + 3), 0)
                evacuate_group(n, 0)
                causal_exps(n, 3)
                if second:
                    ffn_tokens(mix2(n - 2), norm3(n - 2), 1)
                if first:
                    ffn_sigmoid(mix1(n + 3))
                if ahead:
                    token_norm(norm2(n + 2), mv, lnv, rstd)
                causal_exps(n, 4)
                if before:
                    causal_out(n - 1)
                evacuate_group(n, 1)
                causal_exps(n, 5)
                if ahead:
                    normed_tokens(n + 2)
                if second:
                    ffn_hidden(mix2(n - 2), 1)
                causal_exps(n, 6)
                if ahead:
                    causal_parts(n + 2)
                evacuate_group(n, 2)
                if second:
                    ffn_sigmoid(mix2(n - 2))
                causal_exps(n, 7)
                if ahead:
                    causal_values(n + 2)
                value_sums(n)
                if within(n, 0, B - 5):
                    token_norm(norm1(n + 4), mv, lnv, rstd)
                if before:
                    token_norm(norm3(n - 1), mv_k, lnv_k, rstd_k)

            def project(n, pre):
                act.wait_ge(sem(pre + "_ott"), n + 1)
                copy(o_t[:, :], ps_m[:, 0, 0:T]).then_inc(sem(pre + "_otc"), 1)

            def mix_tokens(m, u):
                act.wait_ge(sem("M_yt"), m + 1)
                copy(ym_t[u][:, :], ps_m[:, 0, :]).then_inc(sem("M_ytc"), 1)

            def mix_logits(m):
                act.wait_ge(sem("M_lmax"), m + 1)
                act.activation(lexp[:, :, :], eq_[:, :, 0, :], ACT.Exp).then_inc(sem("M_lexp"), 1)

            def mix_gates(m):
                act.wait_ge(sem("M_gt"), m + 1)
                copy(gate_t, ps_m[0:EXP, 0, :]).then_inc(sem("M_gtc"), 1)

            def mix_norm(m):
                rsqrt("M", m, GT, mv[:, :, 1], lnv[:, :], rstd[:, :])

            def mix_front(m, u):
                mix_norm(m)
                mix_tokens(m, u)
                mix_logits(m)
                mix_gates(m)

            def hidden(m, e):
                act.wait_ge(sem("M_out"), m * EXP + e + 1)
                for f in range(NF):
                    j = e * NF + f
                    act.wait_ge(sem("M_h"), m * EXP * NF + j + 1)
                    bank = (ps_q, ps_k)[j % 4 // 2][:, j % 2, :]
                    act.activation(h_sb[e % 2][:, f, :], bank, ACT.Relu, bias=b1_t[:, j:j + 1])\
                        .then_inc(sem("M_relu"), 1)

            def key_norm(k):
                rsqrt("KN", k, GT, mv_k[:, :, 1], lnv_k[:, :], rstd_k[:, :])

            def key_tokens(g):
                act.wait_ge(sem("K_yt"), g + 1)
                copy(z_t[:, :], ps_m[:, 1, :]).then_inc(sem("K_ytc"), 1)

            def key_heads(g):
                rsqrt("K", g, 1, hvar[:, :], hln[:, :], hrs[:, :], 1.0 / HD)

            def key_parts(g):
                act.wait_ge(sem("K_nt"), g + 1)
                act.wait_ge(sem("K_out"), g * 16 * GB + 16 * GB)
                src = ps_m[:, 1, :].rearrange("p (b t) -> p b t", b=GB)
                copy(qk32[:, :, :], src)
                copy(parts[:, :, 0, :], src).then_inc(sem("K_hi"), 1)

            def mixture(g, u, base, keys):
                m = base + g
                front = not isinstance(g, int) or g < NG - 1
                before = keys and not (isinstance(g, int) and g == 0)
                hidden(m, 0)
                if before:
                    key_norm((g - 1) * 2)
                hidden(m, 1)
                if front:
                    mix_norm(m + 1)
                hidden(m, 2)
                if front:
                    mix_tokens(m + 1, 1 - u)
                if before:
                    key_norm((g - 1) * 2 + 1)
                hidden(m, 3)
                if before:
                    key_tokens(g - 1)
                hidden(m, 4)
                if front:
                    mix_logits(m + 1)
                hidden(m, 5)
                if front:
                    mix_gates(m + 1)
                hidden(m, 6)
                if before:
                    key_heads(g - 1)
                hidden(m, 7)
                if before:
                    key_parts(g - 1)

            def front_heads(f):
                rsqrt("query", f, 1, hvar[:, 0:NT * H], hln[:, 0:NT * H], hrs[:, 0:NT * H], 1.0 / HD)

            def pair_exps(n, hp):
                g = hp * 2 // HG
                if hp * 2 % HG == 0:
                    act.wait_ge(sem("fast_values"), (n + B) * NGV + g + 1)
                act.wait_ge(sem("fast_scores"), (n + B) * HP + hp + 1)
                act.activation(e_buf[g % 2][:, hp * 2 % HG:hp * 2 % HG + 2, :], (ps_q, ps_k)[hp % 2][:, :, :],
                               ACT.Exp).then_inc(sem("fast_exp"), 1)

            def fast_focus():
                key_norm((NG - 1) * 2)
                front_heads(0)
                key_norm((NG - 1) * 2 + 1)
                front_heads(1)
                key_tokens(NG - 1)
                key_heads(NG - 1)
                act.wait_ge(sem("fast_parts_out"), 32 + 32)
                key_parts(NG - 1)
                for it in range(MAX_ITER):
                    def body(n, b, p, half):
                        ahead = follow(n, b, 2)
                        for hp in range(HP):
                            pair_exps(n, hp)
                            if hp == 2 and ahead:
                                front_heads(ahead[0])

                    fast_steps(act, it, body)

            def general_focus():
                key_norm((NG - 1) * 2)
                key_norm((NG - 1) * 2 + 1)
                key_tokens(NG - 1)
                key_heads(NG - 1)
                key_parts(NG - 1)
                act.wait_ge(sem("K_out"), (NG + 1) * 16 * GB)
                base = general_base(act)
                for it in range(MAX_ITER):
                    with act.Fori(0, B // 2) as i:
                        for p in range(2):
                            b = i * 2 + p
                            n = base + it * B + b
                            focus_front(n, it * B + b)
                            maxima(n, False)
                            exps(n, False)
                            if it == MAX_ITER - 1:
                                project(b, "O")

            for k in range(3):
                act.wait_ge(sem("setup_tensor"), k + 1)
                for j in range(4 * k, min(4 * k + 4, 9)):
                    src = SQUARES[k][:, (j % 4) * P:(j % 4 + 1) * P]
                    dst = w_t[:, j, :]
                    if j in (W_Q0, W_K0):
                        src = src.rearrange("p (h d) -> p h d", h=H)
                        dst = dst.rearrange("p (d h) -> p h d", h=H)
                    if j == W_Q1:
                        last = act.activation(dst, src, ACT.Copy, scale=col(LNA))
                    else:
                        last = copy(dst, src)
                last.then_inc(sem("setup_scalar"), 1)
            act.sem_inc(sem("exp_done"), 2)
            act.sem_inc(sem("M_relu"), 4)
            act.sem_inc(sem("fast_exp"), 2)
            act.sem_inc(sem("fast_evac"), 2)
            act.sem_inc(sem("G_vc"), 1)
            token_norm(norm1(0), mv, lnv, rstd)
            ffn_tokens(mix1(0), norm1(0), 2)
            token_norm(norm1(1), mv, lnv, rstd)
            ffn_hidden(mix1(0), 2)
            ffn_sigmoid(mix1(0))
            act.wait_ge(sem("setup_tensor"), 4)
            copy(b1_t[:, :], ps_m[:, 1, 256:256 + EXP * NF]).then_inc(sem("setup_scalar"), 1)
            for f in range(2):
                ffn_tokens(mix1(f + 1), norm1(f + 1), 2)
                token_norm(norm2(f), mv, lnv, rstd)
                ffn_hidden(mix1(f + 1), 2)
                normed_tokens(f)
                token_norm(norm1(f + 2), mv, lnv, rstd)
                ffn_sigmoid(mix1(f + 1))
                causal_parts(f)
                causal_values(f)
                if f == 0:
                    act.wait_ge(sem("setup_tensor"), 6)
                    act.activation(w_t[:, W_K1, :], ps_q[:, 0, 0:P], ACT.Copy, scale=col(LNB))
                    act.activation(w_t[:, W_V1, :], ps_q[:, 0, P:2 * P], ACT.Copy, scale=col(LNB))\
                        .then_inc(sem("setup_scalar"), 1)
                    act.wait_ge(sem("setup_vector"), 3)
                    act.activation(temps[:, T_LN, :], temps[:, T_SAFE, :], ACT.Ln).then_inc(sem("setup_scalar"), 1)
                    act.wait_ge(sem("setup_scalar"), 6)
                    act.activation(temps[:, Q_SC, :], temps[:, T_LN, :], ACT.Exp, scale=-0.5).then_inc(sem("setup_scalar"), 1)
            causal_steps(act, causal_round)
            max_exps(B - 1)
            evacuate_group(B - 1, NGV - 1)
            ffn_tokens(mix2(B - 2), norm3(B - 2), 1)
            ffn_hidden(mix2(B - 2), 1)
            ffn_sigmoid(mix2(B - 2))
            causal_out(B - 1)
            token_norm(norm3(B - 1), mv_k, lnv_k, rstd_k)
            ffn_tokens(mix2(B - 1), norm3(B - 1), 1)
            ffn_hidden(mix2(B - 1), 1)
            ffn_sigmoid(mix2(B - 1))

            def general_causal():
                with act.Fori(0, B // 2) as i:
                    for p in range(2):
                        n = i * 2 + p
                        ffn(n * 2 + MIXES, n * 3 + NORMS)
                        causal_front(n, n * 3 + 1 + NORMS)
                        maxima(n, True)
                        exps(n, True)
                        project(n + B, "A")
                        ffn(n * 2 + 1 + MIXES, n * 3 + 2 + NORMS)

            redo_causal(act, general_causal)
            mix_front(0, 0)
            mixture_groups(act, lambda g, u: mixture(g, u, 0, True))
            any_path(act, fast_focus, general_focus)
            mix_front(NG, 0)
            mixture_groups(act, lambda g, u: mixture(g, u, NG, False))

        @block.tensor
        def _(pe):
            mm = pe.matmul

            def tr(dst, src, k=P):
                return pe.transpose(dst, src, ident[0:k, 0:k])

            def tokens_t(pre, n, src, dst, tiles):
                pe.wait_ge(sem(pre + "_y"), n * tiles + tiles)
                for t in range(tiles):
                    last = tr(dst[:, t * P:(t + 1) * P], src[:, t, :])
                last.then_inc(sem(pre + "_yt"), 1)

            def ffn_hidden(i, bank):
                pe.wait_ge(sem("F_mix"), i * 2 + 2)
                bank = MIX_BANK[bank]
                for t in range(NT):
                    mm(bank[:, T + t * P:T + (t + 1) * P], xr[:, t * P:(t + 1) * P], w_t[:, W_R, :],
                       start=True, stop=True)
                mm(bank[:, 0:T], w_t[:, W_K, :], xk[:, :], start=True, stop=True).then_inc(sem("F_rk"), 1)

            def ffn_out(i, bank):
                pe.wait_ge(sem("F_ka"), i + 1)
                pe.wait_ge(sem("F_er"), i + 1)
                for t in range(NT):
                    last = mm(MIX_BANK[bank][:, t * P:(t + 1) * P], ka[:, t * P:(t + 1) * P], w_t[:, W_V, :],
                              start=True, stop=True)
                last.then_inc(sem("F_v"), 1)

            def ffn(i, l):
                tokens_t("T", l, y, ps_m[:, 0, :], NT)
                ffn_hidden(i, 0)
                ffn_out(i, 0)

            def causal_front(n, l):
                tokens_t("T", l, y, ps_m[:, 0, :], NT)
                pe.wait_ge(sem("T_ytc"), l + 1)
                mm(ps_m[:, 1, 0:T], w_t[:, W_Q0, :], z_t[:, 0:T], start=True, stop=True)
                mm(ps_m[:, 1, T:2 * T], w_t[:, W_K0, :], z_t[:, 0:T], start=True, stop=True).then_inc(sem("G_qk"), 1)
                for t in range(NT):
                    last = mm(ps_o[:, 0, t * P:(t + 1) * P], z_t[:, t * P:(t + 1) * P], w_t[:, W_V0, :],
                              start=True, stop=True)
                last.then_inc(sem("G_v"), 1)

            def queries_keys(f):
                pe.wait_ge(sem("T_ytc"), norm2(f) + 1)
                mm(ps_m[:, 0, 0:T], w_t[:, W_Q0, :], z_t[:, 0:T], start=True, stop=True)
                mm(ps_m[:, 0, T:2 * T], w_t[:, W_K0, :], z_t[:, 0:T], start=True, stop=True).then_inc(sem("G_qk"), 1)

            def values_front(f):
                pe.wait_ge(sem("qk32"), f * 2 + 2)
                for t in range(NT):
                    last = mm(ps_m[:, 0, t * P:(t + 1) * P], z_t[:, t * P:(t + 1) * P], w_t[:, W_V0, :],
                              start=True, stop=True)
                last.then_inc(sem("G_v"), 1)

            def squared_lengths(f):
                pe.wait_ge(sem("qk_squares"), f + 1)
                if isinstance(f, int) and f in (1, 2):
                    pe.wait_ge(sem("qk_longest"), f)
                elif not isinstance(f, int) or f >= 4:
                    pe.wait_ge(sem("F_gated"), mix2(f - 4) + 1)
                elif f == 3:
                    pe.wait_ge(sem("qk_longest"), f)
                mm(ps_o[0:H, 1, :], head_sum[:, :], squares, start=True, stop=True).then_inc(sem("qk_lengths"), 1)

            def row_scores(n, p, half, hp):
                if hp == 0:
                    pe.wait_ge(sem(f"fast_operands_in_{p}"), half * 96 + 96)
                pe.wait_ge(sem("row_max"), n * HP + hp + 1)
                q, k = q_st[p], k_st[p]
                for u in range(2):
                    h, o = hp * 2 + u, ps_q[:, u, :]
                    mm(o[:, P:3 * P], ident_b[:, :], mask_q[:, :], start=True, stop=False, skip_group_check=True)
                    mm(o[:, 0:2 * P], q[0:ROWS_P1, h, P:2 * P], k[0:ROWS_P1, h, :], start=False, stop=False,
                       skip_group_check=True)
                    last = mm(o[:, 2 * P:3 * P], q[0:ROWS_P1, h, 0:P], k[0:ROWS_P1, h, 0:P], start=False,
                              stop=True, skip_group_check=True)
                last.then_inc(sem("row_scores"), 1)

            def causal_scores(n, p, hp):
                pe.wait_ge(sem("fast_exp"), n * HP + hp + 2)
                q, k = q_st[p], k_st[p]
                for u in range(2):
                    h, o = hp * 2 + u, ps_k[:, u, :]
                    mm(o[:, 0:2 * P], ident_b[:, :], mask_k[:, :], start=True, stop=False, skip_group_check=True)
                    mm(o[:, 0:P], k[0:ROWS_P1, h, P:2 * P], q[0:ROWS_P1, h, P:2 * P], start=False, stop=False,
                       skip_group_check=True)
                    last = mm(o[:, P:3 * P], k[0:ROWS_P1, h, 0:P], q[0:ROWS_P1, h, :], start=False, stop=True,
                              skip_group_check=True)
                last.then_inc(sem("fast_scores"), 1)

            def causal_values(n, p, g):
                pe.wait_ge(sem("fast_exp"), n * HP + (g + 1) * HG // 2 + 2)
                pe.wait_ge(sem("fast_evac"), n * NGV + g + 2)
                if g == 0:
                    pe.wait_ge(sem("fast_v"), n + 1)
                for kt in range(NT):
                    for j in range(HG):
                        rows_j = slice(VW * j, VW * j + VW)
                        if kt:
                            last = mm(ps_o[rows_j, 0, P:T], v_st[p][:, kt, HG * g + j, :], e_buf[g % 2][:, j, 0:P],
                                      start=False, stop=True, tile_position=(0, VW * j))
                        else:
                            last = mm(ps_o[rows_j, 0, 0:T], v_st[p][:, kt, HG * g + j, :],
                                      e_buf[g % 2][:, j, P:3 * P], start=True, stop=False, tile_position=(0, VW * j))
                last.then_inc(sem("fast_values"), 1)

            def sums_t(n, t, bank):
                for g in range(NGV):
                    last = tr(bank[:, g * P:(g + 1) * P], o_sb[:, g, t * P:(t + 1) * P])
                last.then_inc(sem("fast_o_t"), 1)

            def causal_back(b, t):
                if t == 0:
                    pe.wait_ge(sem("fast_evac"), b * NGV + NGV + 2)
                    if not isinstance(b, int) or b >= 1:
                        pe.wait_ge(sem("v_sums_c"), b + 1)
                pe.wait_ge(sem("fast_o_read"), b * NT + t + 1)
                sums_t(b, t, BACK_BANK[0])

            def causal_out(b):
                pe.wait_ge(sem("A_o"), b + 1)
                for t in range(NT):
                    last = tr(ps_m[:, 1, t * P:(t + 1) * P], o_tok[:, t, :, :].rearrange("p h d -> p (h d)"))
                last.then_inc(sem("A_ott"), 1)

            def causal_project(b):
                pe.wait_ge(sem("A_otc"), b + 1)
                for t in range(NT):
                    last = mm(ps_m[:, 1, T + t * P:T + (t + 1) * P], o_t[:, t * P:(t + 1) * P], w_t[:, W_P0, :],
                              start=True, stop=True)
                last.then_inc(sem("A_proj"), 1)

            def value_sums(n, p):
                if not isinstance(n, int) or n >= 1:
                    pe.wait_ge(sem("A_x"), n)
                v0, v1 = v_st[p][:, 0, :, 0:HD], v_st[p][:, 1, :, 0:HD]
                mm(ps_m[:, 1, 0:P], behind[:, :], v0, start=True, stop=False)
                mm(ps_m[:, 1, 0:P], ones[:, :], v1, start=False, stop=True)
                mm(ps_m[:, 1, P:2 * P], behind[:, :], v1, start=True, stop=True)
                mm(ps_m[:, 1, 2 * P:3 * P], ones[:, :], v0, start=True, stop=False)
                mm(ps_m[:, 1, 2 * P:3 * P], ones[:, :], v1, start=False, stop=True).then_inc(sem("v_sums"), 1)

            def causal_round(n, p, half):
                before, first, second, ahead = within(n, 1, B), within(n, 0, B - 4), within(n, 2, B), within(n, 0, B - 3)
                b = n - 1
                for hp in range(HP):
                    row_scores(n, p, half, hp)
                    causal_scores(n, p, hp)
                    if hp == 0:
                        if before:
                            causal_values(b, 1 - p, NGV - 1)
                        if within(n, 1, B - 2):
                            squared_lengths(n + 1)
                        if first:
                            pe.wait_ge(sem("G_vc"), n + 2 + 1 if ahead else B)
                            tokens_t("T", norm1(n + 3), y, ps_m[:, 0, :], NT)
                    elif hp == 1:
                        if before:
                            causal_back(b, 0)
                    elif hp == 2:
                        if before:
                            causal_back(b, 1)
                        if first:
                            ffn_hidden(mix1(n + 3), 0)
                        causal_values(n, p, 0)
                    elif hp == 3:
                        if second:
                            if within(n, 0, B - 2):
                                pe.wait_ge(sem("qk_longest"), n + 2)
                            else:
                                pe.wait_ge(sem("F_gated"), mix2(n - 3) + 1)
                            tokens_t("T", norm3(n - 2), y_b, MIX_BANK[1], NT)
                        if first:
                            ffn_out(mix1(n + 3), 0)
                    elif hp == 4:
                        if before:
                            causal_out(b)
                        causal_values(n, p, 1)
                    elif hp == 5:
                        if before:
                            causal_project(b)
                        if ahead:
                            if first:
                                pe.wait_ge(sem("F_gated"), mix1(n + 3) + 1)
                            else:
                                pe.wait_ge(sem("G_vc"), n + 2 + 1)
                            tokens_t("T", norm2(n + 2), y, ps_m[:, 0, :], NT)
                        if second:
                            ffn_hidden(mix2(n - 2), 1)
                    elif hp == 6:
                        if ahead:
                            queries_keys(n + 2)
                        if second:
                            ffn_out(mix2(n - 2), 1)
                        causal_values(n, p, 2)
                    elif hp == 7:
                        if ahead:
                            values_front(n + 2)
                        value_sums(n, p)

            def focus_front(f):
                pe.wait_ge(sem("query_tok"), f + 1)
                for t in range(NT):
                    last = tr(ps_m[:, 0, t * P:(t + 1) * P], o_prev[:, t * P:(t + 1) * P])
                last.then_inc(sem("query_t"), 1)
                pe.wait_ge(sem("query_tc"), f + 1)
                for t in range(NT):
                    last = mm(ps_m[:, 1, t * P:(t + 1) * P], o_t[:, t * P:(t + 1) * P], block_w[:, 0, :],
                              start=True, stop=True)
                last.then_inc(sem("query_ps"), 1)
                pe.wait_ge(sem("query_nrm"), f + 1)
                for t in range(NT):
                    last = tr(ps_m[:, 0, t * P:(t + 1) * P], nrm[:, t, :, :].rearrange("p d h -> p (d h)"))
                last.then_inc(sem("query_nt"), 1)

            def maxima_scores(n, p, causal):
                pe.wait_ge(sem("operands_in"), n * 96 + 96)
                q, k = q_st[p], k_st[p]
                for h in range(H):
                    pe.wait_ge(sem("max_done"), n * H + h + 1)
                    o = ps_q[:, h % 2, :]
                    if causal:
                        mm(o[:, P:3 * P], ident_b[:, :], mask_q[:, :], start=True, stop=False, skip_group_check=True)
                        mm(o[:, 0:2 * P], q[0:ROWS_P1, h, P:2 * P], k[0:ROWS_P1, h, :], start=False, stop=False,
                           skip_group_check=True)
                        last = mm(o[:, 2 * P:3 * P], q[0:ROWS_P1, h, 0:P], k[0:ROWS_P1, h, 0:P], start=False,
                                  stop=True, skip_group_check=True)
                    else:
                        for t in range(NT):
                            last = mm(o[:, t * T:(t + 1) * T], q[0:ROWS_P1, h, t * P:(t + 1) * P],
                                      k[0:ROWS_P1, h, :], start=True, stop=True)
                    last.then_inc(sem("q_scores"), 1)

            def maxima_rows(n, causal):
                if causal:
                    pe.wait_ge(sem("ml_l"), n + 1)
                else:
                    pe.wait_ge(sem("max_done"), n * H + H + 2)
                for t in range(NT):
                    last = tr(ps_m[0:2 * H, 1, t * P:(t + 1) * P], ml[:, t, :, :].rearrange("p m h -> p (m h)"))
                last.then_inc(sem("ml_t"), 1)

            def products(n, p, causal):
                q, k, v = q_st[p], k_st[p], v_st[p]

                def value_sums(g):
                    if causal:
                        pe.wait_ge(sem("clamp_done"), n * (H // 2) + 2 * g + 2 + 2)
                    else:
                        pe.wait_ge(sem("exp_done"), n * H + HG * g + HG + 2)
                    pe.wait_ge(sem("o_evac"), n * (H // HG) + g + 1)
                    o = ps_o[:, g % 2, (g // 2) * T:(g // 2 + 1) * T]
                    e = e_buf[g % 2]
                    for kt in range(NT):
                        for j in range(HG):
                            rows_j = slice(VW * j, VW * j + VW)
                            if causal and kt:
                                last = mm(o[rows_j, P:T], v[:, kt, HG * g + j, :], e[:, j, 0:P], start=False,
                                          stop=True, tile_position=(0, VW * j))
                            elif causal:
                                last = mm(o[rows_j, :], v[:, kt, HG * g + j, :], e[:, j, P:3 * P], start=True,
                                          stop=False, tile_position=(0, VW * j))
                            else:
                                last = mm(o[rows_j, :], v[:, kt, HG * g + j, :], e[:, j, kt * T:(kt + 1) * T],
                                          start=kt == 0, stop=kt == NT - 1, tile_position=(0, VW * j))
                    last.then_inc(sem("values_done"), 1)

                pe.wait_ge(sem("ml_in"), n * 16 + 16)
                pe.wait_ge(sem("values_ready"), n + 1)
                for h in range(H):
                    pe.wait_ge(sem("exp_done"), n * H + h + 1)
                    o = ps_k[:, h % 2, :]
                    if causal:
                        mm(o[:, 0:2 * P], ident_b[:, :], mask_k[:, :], start=True, stop=False, skip_group_check=True)
                        mm(o[:, 0:P], k[0:ROWS_P2, h, P:2 * P], q[0:ROWS_P2, h, P:2 * P], start=False, stop=False,
                           skip_group_check=True)
                        last = mm(o[:, P:3 * P], k[0:ROWS_P2, h, 0:P], q[0:ROWS_P2, h, :], start=False, stop=True,
                                  skip_group_check=True)
                    else:
                        for t in range(NT):
                            last = mm(o[:, t * T:(t + 1) * T], k[0:ROWS_P2, h, t * P:(t + 1) * P],
                                      q[0:ROWS_P2, h, :], start=True, stop=True)
                    last.then_inc(sem("k_scores"), 1)
                    if causal and h % 2:
                        pe.wait_ge(sem("clamp_done"), n * (H // 2) + h // 2 + 1)
                        for j in range(2):
                            last = mm(ps_m[:, h // 2 % 2, j * T:(j + 1) * T], sel_l[0:ROWS_P2, :],
                                      q[0:ROWS_P2, h - 1 + j, :], start=True, stop=True)
                        last.then_inc(sem("floor"), 1)
                    if h == H - 1:
                        last = pe.nop()
                        last.then_inc(sem("operands_free"), 1)
                    if h >= HG + 1 and h % HG == 1:
                        value_sums(h // HG - 1)
                value_sums(H // HG - 1)

            def back(n, p, causal):
                pe.wait_ge(sem("o_evac"), n * (H // HG) + H // HG + 2)
                for t in range(NT):
                    for g in range(H // HG):
                        last = tr(ps_m[:, t, g * P:(g + 1) * P], o_sb[:, g, t * P:(t + 1) * P])
                last.then_inc(sem("o_t"), 1)
                if causal:
                    v = v_st[p]
                    mm(ps_o[:, 0, 0:P], ones[:, :], v[:, 1, :, 0:HD], start=True, stop=True)
                    mm(ps_o[:, 0, P:2 * P], ones[:, :], v[:, 0, :, 0:HD], start=True, stop=False)
                    mm(ps_o[:, 0, P:2 * P], ones[:, :], v[:, 1, :, 0:HD], start=False, stop=True)\
                        .then_inc(sem("v_sums"), 1)

            def project(n, pre, w, o):
                pe.wait_ge(sem(pre + "_o"), o)
                for t in range(NT):
                    last = tr(ps_m[:, 0, t * P:(t + 1) * P], o_tok[:, t, :, :].rearrange("p h d -> p (h d)"))
                last.then_inc(sem(pre + "_ott"), 1)
                pe.wait_ge(sem(pre + "_otc"), n + 1)
                for t in range(NT):
                    last = mm(ps_m[:, 1, t * P:(t + 1) * P], o_t[:, t * P:(t + 1) * P], w_t[:, w, :],
                              start=True, stop=True)
                last.then_inc(sem(pre + "_proj"), 1)

            def mix_tokens(m):
                tokens_t("M", m, y, ps_m[:, 0, :], GT)

            def mix_logits(m, u):
                pe.wait_ge(sem("M_ytc"), m + 1)
                for t in range(GT):
                    last = mm(ps_m[:, 0, t * EXP:(t + 1) * EXP], ym_t[u][:, t * P:(t + 1) * P], wr[:, :],
                              start=True, stop=True)
                last.then_inc(sem("M_lg"), 1)

            def mix_gates(m, u):
                pe.wait_ge(sem("M_gate"), m + 1)
                for t in range(GT):
                    last = tr(ps_m[0:EXP, 0, t * P:(t + 1) * P], gate[u][:, t, :])
                last.then_inc(sem("M_gt"), 1)

            def mix_biases(m):
                pe.wait_ge(sem("M_gtc"), m + 1)
                for t in range(GT):
                    last = mm(ps_m[:, 0, t * P:(t + 1) * P], gate_t[:, t * P:(t + 1) * P], b2[:, :],
                              start=True, stop=True)
                last.then_inc(sem("M_b2"), 1)

            def mix_front(m, u):
                mix_tokens(m)
                mix_logits(m, u)
                mix_gates(m, u)
                mix_biases(m)

            def hidden(m, u, e):
                for f in range(NF):
                    j = e * NF + f
                    pe.wait_ge(sem("M_relu"), m * EXP * NF + j + 1)
                    bank = (ps_q, ps_k)[j % 4 // 2][:, j % 2, :]
                    mm(bank, w1[:, e, f * P:(f + 1) * P], ym_t[u][:, :], start=True, stop=True)\
                        .then_inc(sem("M_h"), 1)

            def outputs(m, e):
                pe.wait_ge(sem("M_relu"), m * EXP * NF + e * NF + NF + 4)
                pe.wait_ge(sem("M_comb"), m * EXP + e + 1)
                for t in range(GT):
                    for f in range(NF):
                        last = mm(ps_o[:, e % 2, t * P:(t + 1) * P], h_sb[e % 2][:, f, t * P:(t + 1) * P],
                                  w2[:, e * NF + f, :], start=f == 0, stop=f == NF - 1)
                last.then_inc(sem("M_out"), 1)

            def key_tokens(g):
                pe.wait_ge(sem("KN_y"), g * 2 * GT + 2 * GT)
                pe.wait_ge(sem("K_hi"), g + 1)
                for t in range(GT):
                    last = tr(ps_m[:, 1, t * P:(t + 1) * P], y3[:, t, :])
                last.then_inc(sem("K_yt"), 1)

            def key_product(g, w, free, at):
                pe.wait_ge(sem(free), at)
                for t in range(GT):
                    last = mm(ps_m[:, 1, t * P:(t + 1) * P], z_t[:, t * P:(t + 1) * P], w_t[:, w, :],
                              start=True, stop=True)
                last.then_inc(sem("K_ps"), 1)

            def key_queries(g):
                key_product(g, W_Q1, "K_ytc", g + 1)

            def key_keys(g):
                key_product(g, W_K1, "K_read", g * 3 + 1)

            def key_values(g):
                key_product(g, W_V1, "K_read", g * 3 + 2)

            def key_heads(g):
                pe.wait_ge(sem("K_nrm"), g + 1)
                pe.wait_ge(sem("K_read"), g * 3 + 3)
                for t in range(GT):
                    last = tr(ps_m[:, 1, t * P:(t + 1) * P], nrm[:, t, :, :].rearrange("p d h -> p (d h)"))
                last.then_inc(sem("K_nt"), 1)

            def mixture(g, u, base, keys):
                m = base + g
                front = not isinstance(g, int) or g < NG - 1
                before = keys and not (isinstance(g, int) and g == 0)
                hidden(m, u, 0)
                hidden(m, u, 1)
                outputs(m, 0)
                hidden(m, u, 2)
                if front:
                    mix_tokens(m + 1)
                outputs(m, 1)
                hidden(m, u, 3)
                if before:
                    key_tokens(g - 1)
                if front:
                    mix_logits(m + 1, 1 - u)
                outputs(m, 2)
                hidden(m, u, 4)
                if before:
                    key_queries(g - 1)
                outputs(m, 3)
                hidden(m, u, 5)
                if before:
                    key_keys(g - 1)
                if front:
                    mix_gates(m + 1, 1 - u)
                outputs(m, 4)
                hidden(m, u, 6)
                if before:
                    key_values(g - 1)
                if front:
                    mix_biases(m + 1)
                outputs(m, 5)
                hidden(m, u, 7)
                outputs(m, 6)
                if before:
                    key_heads(g - 1)
                outputs(m, 7)

            def front_tokens(f):
                pe.wait_ge(sem("query_tok"), f + 1)
                pe.wait_ge(sem("fast_hi"), f + 1)
                for t in range(NT):
                    last = tr(ps_m[:, 0, t * P:(t + 1) * P], q_tok[:, t * P:(t + 1) * P])
                last.then_inc(sem("query_t"), 1)

            def front_product(f):
                pe.wait_ge(sem("query_tc"), f + 1)
                for t in range(NT):
                    last = mm(ps_m[:, 0, T + t * P:T + (t + 1) * P], q_chan[:, t * P:(t + 1) * P], block_w[:, 0, :],
                              start=True, stop=True)
                last.then_inc(sem("query_ps"), 1)

            def front_heads(f):
                pe.wait_ge(sem("query_nrm"), f + 1)
                for t in range(NT):
                    last = tr(ps_m[:, 0, t * P:(t + 1) * P], y[:, t, :])
                last.then_inc(sem("query_nt"), 1)

            def pair_scores(n, p, half, hp):
                pe.wait_ge(sem("fast_exp"), (n + B) * HP + hp + 1)
                if hp == 0:
                    pe.wait_ge(sem(f"fast_operands_in_{p}"), half * 96 + 96)
                bank = (ps_q, ps_k)[hp % 2]
                for u in range(2):
                    for t in range(NT):
                        last = mm(bank[:, u, t * T:(t + 1) * T], k_st[p][0:ROWS_P1, hp * 2 + u, t * P:(t + 1) * P],
                                  q_st[p][0:ROWS_P1, hp * 2 + u, :], start=True, stop=True)
                last.then_inc(sem("fast_scores"), 1)

            def fast_values(n, p, g):
                pe.wait_ge(sem("fast_exp"), (n + B) * HP + (g + 1) * HG // 2 + 2)
                pe.wait_ge(sem("fast_evac"), (n + B) * NGV + g + 1)
                if g == 0:
                    pe.wait_ge(sem("fast_v"), n + B + 1)
                for kt in range(NT):
                    for j in range(HG):
                        last = mm(ps_o[VW * j:VW * j + VW, g % 2, 0:T], v_st[p][:, kt, HG * g + j, :],
                                  e_buf[g % 2][:, j, kt * T:(kt + 1) * T], start=kt == 0, stop=kt == NT - 1,
                                  tile_position=(0, VW * j))
                last.then_inc(sem("fast_values"), 1)

            def back_tokens(n, b, it, t):
                if t == 0:
                    pe.wait_ge(sem("fast_evac"), (n + B) * NGV + NGV + 2)
                    if it == MAX_ITER - 1:
                        pe.wait_ge(sem("O_x"), b + 1)
                last_batch = isinstance(b, int) and b == B - 1
                if not (last_batch and t):
                    pe.wait_ge(sem("fast_o_read"), (n + B) * NT + t + 1)
                sums_t(n, t, BACK_BANK[t if last_batch else 0])

            def back_out(b):
                pe.wait_ge(sem("O_o"), b + 1)
                for t in range(NT):
                    last = tr(ps_m[:, 1, t * P:(t + 1) * P], o_tok[:, t, :, :].rearrange("p h d -> p (h d)"))
                last.then_inc(sem("O_ott"), 1)

            def back_project(b):
                pe.wait_ge(sem("O_otc"), b + 1)
                for t in range(NT):
                    last = mm(ps_m[:, 1, T + t * P:T + (t + 1) * P], o_t[:, t * P:(t + 1) * P], w_t[:, W_O1, :],
                              start=True, stop=True)
                last.then_inc(sem("O_proj"), 1)

            def change_sum(it, bank):
                pe.wait_ge(sem("d_total"), it + 1)
                mm(ps_m[:, bank, 0:1], ones[:, :], dtot[:, :], start=True, stop=True).then_inc(sem("d_sum"), 1)

            def fast_focus():
                front_tokens(0)
                front_product(0)
                front_heads(0)
                front_tokens(1)
                front_product(1)
                key_tokens(NG - 1)
                front_heads(1)
                key_queries(NG - 1)
                key_keys(NG - 1)
                key_values(NG - 1)
                key_heads(NG - 1)
                for it in range(MAX_ITER):
                    final = it == MAX_ITER - 1
                    if it:
                        pe.wait_ge(sem("window_in"), 32 * it)

                    def body(n, b, p, half):
                        first = isinstance(b, int) and b == 0
                        ahead = follow(n, b, 2)
                        for hp in range(HP):
                            pair_scores(n, p, half, hp)
                            if hp == 1:
                                if ahead:
                                    front_tokens(ahead[0])
                                if not first:
                                    fast_values(n - 1, 1 - p, NGV - 1)
                            elif hp == 2 and ahead:
                                front_product(ahead[0])
                            elif hp == 3:
                                if not first:
                                    back_tokens(n - 1, b - 1, it, 0)
                                fast_values(n, p, 0)
                            elif hp == 4 and not first:
                                back_tokens(n - 1, b - 1, it, 1)
                            elif hp == 5:
                                fast_values(n, p, 1)
                            elif hp == 6:
                                if ahead:
                                    front_heads(ahead[0])
                                if not first and final:
                                    back_out(b - 1)
                            elif hp == 7:
                                if not first and final:
                                    back_project(b - 1)
                                fast_values(n, p, 2)
                                if first and it == 0:
                                    pe.wait_ge(sem("K_hi"), NG + 1)

                    fast_steps(pe, it, body)
                    n = it * B + B - 1
                    fast_values(n, 1, NGV - 1)
                    for t in range(NT):
                        back_tokens(n, B - 1, it, t)
                    if final:
                        back_out(B - 1)
                        back_project(B - 1)
                    else:
                        change_sum(it, 1)

            def general_focus():
                key_tokens(NG - 1)
                key_queries(NG - 1)
                key_keys(NG - 1)
                key_values(NG - 1)
                key_heads(NG - 1)
                base = general_base(pe)
                for it in range(MAX_ITER):
                    if it:
                        pe.wait_ge(sem("window_in"), 32 * it)
                    with pe.Fori(0, B // 2) as i:
                        for p in range(2):
                            b = i * 2 + p
                            n = base + it * B + b
                            focus_front(it * B + b)
                            maxima_scores(n, p, False)
                            maxima_rows(n, False)
                            products(n, p, False)
                            back(n, p, False)
                            if it == MAX_ITER - 1:
                                project(b, "O", W_O1, b + 1)
                    if it < MAX_ITER - 1:
                        change_sum(it, 0)

            pe.wait_ge(sem("consts"), FIRST_CONSTS)
            pe.wait_ge(sem("loaded"), lots[0])
            for k in range(3):
                for j in range(4 * k, min(4 * k + 4, 9)):
                    last = tr(SQUARES[k][:, (j % 4) * P:(j % 4 + 1) * P], w_nat[:, j, :])
                last.then_inc(sem("setup_tensor"), 1)
            pe.sem_inc(sem("operands_free"), 2)
            pe.sem_inc(sem("values_done"), 2)
            pe.sem_inc(sem("M_out"), 2)
            pe.sem_inc(sem("fast_values"), 2)
            pe.wait_ge(sem("setup_scalar"), 3)
            tokens_t("T", norm1(0), y, MIX_BANK[2], NT)
            ffn_hidden(mix1(0), 2)
            ffn_out(mix1(0), 2)
            pe.wait_ge(sem("consts"), CONSTS)
            pe.wait_ge(sem("loaded"), lots[1])
            tr(ps_m[:, 1, 256:256 + EXP * NF], b1_nat[:, :], EXP * NF).then_inc(sem("setup_tensor"), 1)
            pe.wait_ge(sem("setup_vector"), 1)
            for j in range(3):
                last = tr(ps_k[:, 0, j * P:(j + 1) * P], e_buf[0][:, j, 0:P])
            last.then_inc(sem("setup_tensor"), 1)
            for f in range(2):
                pe.wait_ge(sem("F_gated"), mix1(f) + 1)
                tokens_t("T", norm1(f + 1), y, MIX_BANK[2], NT)
                ffn_hidden(mix1(f + 1), 2)
                if f:
                    pe.wait_ge(sem("G_vc"), f + 1)
                tokens_t("T", norm2(f), y, ps_m[:, 0, :], NT)
                queries_keys(f)
                ffn_out(mix1(f + 1), 2)
                values_front(f)
                squared_lengths(f)
                if f == 0:
                    pe.wait_ge(sem("setup_vector"), 2)
                    mm(ps_q[:, 0, 0:P], w_nat[:, 9, :], block_w[:, 1, :], start=True, stop=True)
                    mm(ps_q[:, 0, P:2 * P], w_nat[:, 10, :], block_w[:, 2, :], start=True, stop=True)\
                        .then_inc(sem("setup_tensor"), 1)
                    mm(ps_q[:, 1, 0:P], bv_rep[:, :], block_w[:, 2, :], start=True, stop=True)\
                        .then_inc(sem("setup_tensor"), 1)
            pe.wait_ge(sem("setup_scalar"), 5)
            pe.wait_ge(sem("F_gated"), mix1(2) + 1)
            causal_steps(pe, causal_round)
            causal_values(B - 1, 1, NGV - 1)
            pe.wait_ge(sem("F_gated"), mix2(B - 3) + 1)
            tokens_t("T", norm3(B - 2), y_b, MIX_BANK[1], NT)
            causal_back(B - 1, 0)
            causal_back(B - 1, 1)
            ffn_hidden(mix2(B - 2), 1)
            ffn_out(mix2(B - 2), 1)
            causal_out(B - 1)
            causal_project(B - 1)
            pe.wait_ge(sem("F_gated"), mix2(B - 2) + 1)
            tokens_t("T", norm3(B - 1), y_b, MIX_BANK[1], NT)
            ffn_hidden(mix2(B - 1), 1)
            ffn_out(mix2(B - 1), 1)
            pe.wait_ge(sem("setup_vector"), 4)
            mm(ps_m[:, 0, 0:1], ones[:, :], safe[:, 0:1], start=True, stop=True).then_inc(sem("setup_tensor"), 1)

            def general_causal():
                with pe.Fori(0, B // 2) as i:
                    for p in range(2):
                        n = i * 2 + p
                        ffn(n * 2 + MIXES, n * 3 + NORMS)
                        causal_front(n, n * 3 + 1 + NORMS)
                        maxima_scores(n, p, True)
                        maxima_rows(n, True)
                        products(n, p, True)
                        back(n, p, True)
                        project(n + B, "A", W_P0, n + B + 1)
                        ffn(n * 2 + 1 + MIXES, n * 3 + 2 + NORMS)

            redo_causal(pe, general_causal)
            pe.wait_ge(sem("loaded"), n_loads)
            mix_front(0, 0)
            mixture_groups(pe, lambda g, u: mixture(g, u, 0, True))
            any_path(pe, fast_focus, general_focus)
            mix_front(NG, 0)
            mixture_groups(pe, lambda g, u: mixture(g, u, NG, False))

        @block.vector
        def _(dve):
            tt, ts, stt, red = dve.tensor_tensor, dve.tensor_scalar, dve.scalar_tensor_tensor, dve.tensor_reduce

            class Steps:

                def __init__(self, name, base, per):
                    self.sem, self.base, self.per, self.k = sem(name), base, per, 0

                def __call__(self, ins):
                    ins.then_inc(self.sem, 1)
                    self.k += 1

                def wait(self):
                    dve.wait_ge(self.sem, self.base + self.k)

                def end(self):
                    assert self.k == self.per
                    self.wait()

            def hold():
                dve.sem_inc(sem("held"), 1)

            def ln_stats(pre, n, src, tiles, st, mv):
                for t in range(tiles):
                    dve.bn_stats(st[:, t, :], src(t)).then_inc(sem(pre + "_st"), 1)
                dve.wait_ge(sem(pre + "_st"), n * tiles + tiles)
                hold()
                for t in range(tiles):
                    dve.bn_aggr(mv[:, t, :], st[:, t, :]).then_inc(sem(pre + "_mom"), 1)

            def ln_apply(pre, n, src, dst, tiles, mv, rstd):
                dve.wait_ge(sem(pre + "_rstd"), n + 1)
                for t in range(tiles):
                    ts(dst(t), src(t), mv[:, t, 0:1], rstd[:, t:t + 1], ALU.subtract, ALU.mult)\
                        .then_inc(sem(pre + "_y"), 1)

            def layernorm(pre, n, src, dst, tiles):
                ln_stats(pre, n, src, tiles, st, mv)
                ln_apply(pre, n, src, dst, tiles, mv, rstd)

            def of_x(b):
                return lambda t: x[:, b, t * C:(t + 1) * C]

            def of(buf):
                return lambda t: buf[:, t, :]

            def mix_inputs(i):
                dve.wait_ge(sem("F_dy"), i + 1)
                stt(xr[:, :], dy[:, :], col(MU_R), y_t[:, 0:T], ALU.mult, ALU.add).then_inc(sem("F_mix"), 1)
                stt(xk[:, :], dy[:, :], col(MU_K), y_t[:, 0:T], ALU.mult, ALU.add).then_inc(sem("F_mix"), 1)

            def mix_gated(i, bank):
                dve.wait_ge(sem("F_v"), i + 1)
                dve.wait_ge(sem("F_rec"), i + 1)
                dve.wait_ge(sem("F_x"), i + 1)
                stt(gated[:, :], MIX_BANK[bank][:, 0:T], 0.5, rec[:, :], ALU.mult, ALU.mult).then_inc(sem("F_gated"), 1)

            def ffn(i, l, b):
                hold()
                layernorm("T", l, of_x(b), of(y), NT)
                mix_inputs(i)
                mix_gated(i, 0)
                dve.wait_ge(sem("F_x"), i + 1 + 1)

            def causal_front(n, l, p, b):
                hold()
                layernorm("T", l, of_x(b), of(y), NT)
                dve.wait_ge(sem("G_v"), n + B + 1)
                dve.tensor_copy(v_st[p][:, :, :, 0:HD],
                                ps_o[:, 0, 0:T].rearrange("p (t h d) -> p t h d", t=NT, h=H))\
                    .then_inc(sem("values_ready"), 1)

            def longest(f):
                dve.wait_ge(sem("qk_lengths"), f + 1)
                hold()
                red(qk_max[:, f, :], ps_o[0:H, 1, :].rearrange("p (s t) -> p s t", s=2), AX.X, ALU.max)\
                    .then_inc(sem("qk_longest"), 1)

            def row_maxima(n, hp):
                dve.wait_ge(sem("row_scores"), n * HP + hp + 1)
                if hp == 0 and (not isinstance(n, int) or n >= 1):
                    dve.wait_ge(sem("row_maxima"), n)
                hold()
                red(mx[:, hp * 2:hp * 2 + 2, :], ps_q[:, :, 0:3 * P].rearrange("p u (c k) -> p u c k", c=3),
                    AX.X, ALU.max).then_inc(sem("row_max"), 1)

            def all_maxima(n):
                dve.wait_ge(sem("row_max"), n * HP + HP + 1)
                hold()
                tt(rmax[:, 1, :], mx[:, :, 0], mx[:, :, 1], ALU.max)
                red(top[:, bass.ds(n, 1)], mx[:, :, :].rearrange("p h c -> p (h c)"), AX.X, ALU.max)
                dve.tensor_copy(rmax[:, 0, :], mx[:, :, 2]).then_inc(sem("row_maxima"), 1)

            def causal_sums(b, t):
                if t == 0 and within(b, 1, B):
                    dve.wait_ge(sem("A_ott"), b)
                if t == 0:
                    dve.wait_ge(sem("v_sums_c"), b + 1)
                dve.wait_ge(sem("fast_o_t"), b * NT + t + 1 + 2)
                o = ps_m[:, 1, :].rearrange("p (h w) -> p h w", w=VW)
                hold()
                ts(s_sum[:, t, :], o[:, :, HD], low_behind[:, t:t + 1], None, ALU.add)
                stt(o_tok[:, t, :, :], vs[:, t, :, :], LOW, o[:, :, 0:HD], ALU.mult, ALU.add)\
                    .then_inc(sem("fast_o_read"), 1)

            def causal_normalise(b):
                s = Steps("A_step", b * 6, 6)
                dve.wait_ge(sem("max_exps"), b + 1)
                dve.wait_ge(sem("fast_o_read"), b * NT + NT + 1)
                s(stt(s_u[:, :, :], emax[:, :, :], DEN_EPS, s_sum[:, :, :], ALU.mult, ALU.add))
                s.wait()
                hold()
                s(ts(s_du[:, :, :], s_u[:, :, :], P_EPS, None, ALU.mult))
                s(stt(s_den[:, :, :], s_u[:, :, :], P_EPS * T, s_sum[:, :, :], ALU.mult, ALU.add))
                s.wait()
                hold()
                s(tt(corr[:, :, :, :], s_du[:, :, :].unsqueeze(3).broadcast_to([P, NT, H, HD]),
                     vs[:, 2, :, :].unsqueeze(1).broadcast_to([P, NT, H, HD]), ALU.mult))
                s(dve.reciprocal(s_rec[:, :, :], s_den[:, :, :]))
                s.wait()
                s(tt(corr[:, :, :, :], corr[:, :, :, :], o_tok[:, :, :, :], ALU.add))
                s.end()
                tt(o_tok[:, :, :, :], corr[:, :, :, :], s_rec[:, :, :].unsqueeze(3).broadcast_to([P, NT, H, HD]),
                   ALU.mult).then_inc(sem("A_o"), 1)

            def causal_add(b):
                dve.wait_ge(sem("A_proj"), b + 1)
                hold()
                tt(x[:, b, :], x[:, b, :], ps_m[:, 1, T:2 * T], ALU.add).then_inc(sem("A_x"), 1)

            def front_norm(f):
                hold()
                ln_stats("T", norm1(f), of_x(f), NT, st, mv)

            def front_normed(f):
                dve.wait_ge(sem("T_yt"), norm2(f - 2) + 1)
                ln_apply("T", norm1(f), of_x(f), of(y), NT, mv, rstd)

            def middle_norm(f):
                dve.wait_ge(sem("F_x"), mix1(f) + 1 + 1)
                hold()
                ln_stats("T", norm2(f), of_x(f), NT, st, mv)

            def middle_normed(f, last):
                dve.wait_ge(sem("T_yt"), last + 1)
                ln_apply("T", norm2(f), of_x(f), of(y), NT, mv, rstd)

            def back_norm(b):
                dve.wait_ge(sem("A_x"), b + 1)
                hold()
                ln_stats("T", norm3(b), of_x(b), NT, st_k, mv_k)

            def back_normed(b):
                ln_apply("T", norm3(b), of_x(b), of(y_b), NT, mv_k, rstd_k)

            def causal_round(n, p, half):
                before, first, second, ahead = within(n, 1, B), within(n, 0, B - 4), within(n, 2, B), within(n, 0, B - 3)
                b = n - 1
                row_maxima(n, 0)
                if second:
                    back_normed(n - 2)
                row_maxima(n, 1)
                if first:
                    mix_inputs(mix1(n + 3))
                if before:
                    causal_sums(b, 0)
                if within(n, 1, B - 2):
                    longest(n + 1)
                row_maxima(n, 2)
                if before:
                    causal_sums(b, 1)
                if before:
                    causal_normalise(b)
                row_maxima(n, 3)
                if ahead:
                    middle_norm(n + 2)
                if second:
                    mix_inputs(mix2(n - 2))
                row_maxima(n, 4)
                if first:
                    mix_gated(mix1(n + 3), 0)
                if ahead:
                    middle_normed(n + 2, norm1(n + 3) if first else norm2(n + 1))
                row_maxima(n, 5)
                if before:
                    causal_add(b)
                row_maxima(n, 6)
                if within(n, 0, B - 5):
                    front_norm(n + 4)
                row_maxima(n, 7)
                all_maxima(n)
                if second:
                    mix_gated(mix2(n - 2), 1)
                if before:
                    back_norm(b)
                if within(n, 0, B - 5):
                    front_normed(n + 4)

            def maxima(n, causal):
                for h in range(H):
                    dve.wait_ge(sem("q_scores"), n * H + h + 1)
                    o = ps_q[:, h % 2, :]
                    if causal:
                        red(nmax[:, 1, h:h + 1], o[:, 0:2 * P], AX.X, ALU.max, negate=True)
                        last = red(nmax[:, 0, h:h + 1], o[:, 2 * P:3 * P], AX.X, ALU.max, negate=True)
                    else:
                        last = red(ml[:, :, 0, h], o.rearrange("p (t k) -> p t k", t=NT), AX.X, ALU.max, negate=True)
                    last.then_inc(sem("max_done"), 1)
                if causal:
                    dve.wait_ge(sem("max_done"), n * H + H + 2)
                    ts(ml[:, :, 0, :], nmax[:, :, :], -CLIP, CLIP, ALU.max, ALU.min).then_inc(sem("ml_m"), 1)

            def clamps(n):
                for hp in range(H // 2):
                    dve.wait_ge(sem("exp_done"), n * H + 2 * hp + 2 + 2)
                    dve.wait_ge(sem("floor"), n * (H // 2) + hp + 1)
                    j = 2 * hp % HG
                    e = e_buf[hp // 2 % 2][:, j:j + 2, :]
                    lo = ps_m[:, hp % 2, :].rearrange("p (h q) -> p h q", h=2)
                    stt(e[:, :, 0:P], e[:, :, 0:P], 1.0, lo[:, :, P:T], ALU.min, ALU.max)
                    stt(e[:, :, P:3 * P], e[:, :, P:3 * P], 1.0, lo[:, :, :], ALU.min, ALU.max)\
                        .then_inc(sem("clamp_done"), 1)

            def causal_back(n, b):
                dve.wait_ge(sem("o_t"), n + 1)
                dve.wait_ge(sem("v_sums"), n + B + 1)
                o = ps_m[:, :, :].rearrange("p t (h w) -> p t h w", w=VW)
                v1 = ps_o[:, 0, 0:P].rearrange("p (h d) -> p h d", h=H)
                vs = ps_o[:, 0, P:2 * P].rearrange("p (h d) -> p h d", h=H)
                low = ml[:, 0, 1, :]
                s = Steps("norm_step", n * 12, 12)
                s(dve.tensor_copy(s_sum[:, :, :], o[:, :, :, HD]))
                s.wait()
                s(stt(s_sum[:, 0, :], low, float(P), s_sum[:, 0, :], ALU.mult, ALU.add))
                s.wait()
                s(ts(s_u[:, :, :], s_sum[:, :, :], DEN_EPS, None, ALU.add))
                s.wait()
                s(ts(s_du[:, :, :], s_u[:, :, :], P_EPS, None, ALU.mult))
                s(stt(s_den[:, :, :], s_u[:, :, :], P_EPS * T, s_sum[:, :, :], ALU.mult, ALU.add))
                s.wait()
                s(dve.reciprocal(s_rec[:, :, :], s_den[:, :, :]))
                for t in range(NT):
                    s(tt(corr[:, t, :, :], s_du[:, t, :].unsqueeze(2).broadcast_to([P, H, HD]), vs, ALU.mult))
                s(tt(corr2[:, :, :], low.unsqueeze(2).broadcast_to([P, H, HD]), v1, ALU.mult))
                s.wait()
                s(tt(corr[:, 0, :, :], corr[:, 0, :, :], corr2[:, :, :], ALU.add))
                s.wait()
                s(tt(corr[:, :, :, :], corr[:, :, :, :], o[:, :, :, 0:HD], ALU.add))
                s.wait()
                s(tt(o_tok[:, :, :, :], corr[:, :, :, :], s_rec[:, :, :].unsqueeze(3).broadcast_to([P, NT, H, HD]),
                     ALU.mult))
                s.end()
                dve.nop().then_inc(sem("A_o"), 1)
                dve.wait_ge(sem("A_proj"), n + B + 1)
                tt(x[:, b, :], x[:, b, :], ps_m[:, 1, 0:T], ALU.add).then_inc(sem("A_x"), 1)
                dve.wait_ge(sem("A_x"), n + B + 1)

            def of_group(g):
                return lambda t: x[:, g * GB + t // NT, t % NT * C:(t % NT + 1) * C]

            def group(ap):
                return ap.rearrange("p b (t c) -> p (b t) c", c=C)

            def mix_stats(m, g):
                hold()
                ln_stats("M", m, of_group(g), GT, st, mv)

            def mix_norm(m, g):
                ln_apply("M", m, of_group(g), of(y), GT, mv, rstd)

            def mix_ranks(m):
                s = Steps("M_step", m * 10, 6)
                dve.wait_ge(sem("M_lg"), m + 1)
                s(tt(lg[:, :, :], ps_m[:, 0, 0:GT * EXP].rearrange("p (t e) -> p t e", t=GT),
                     br_row[:, :].unsqueeze(1).broadcast_to([P, GT, EXP]), ALU.add))
                s.wait()
                for t in range(GT):
                    mine = lg[:, t, :].unsqueeze(2).broadcast_to([P, EXP, EXP])
                    other = lg[:, t, :].unsqueeze(1).broadcast_to([P, EXP, EXP])
                    tt(gt_[:, t, :, :], other, mine, ALU.is_gt)
                    last = tt(eq_[:, t, :, :], other, mine, ALU.is_equal)
                s(last)
                s(red(lmax[:, :], lg[:, :, :], AX.X, ALU.max))
                s.wait()
                s(tt(eq_[:, :, :, :], eq_[:, :, :, :], tri[:, :, :].unsqueeze(1).broadcast_to([P, GT, EXP, EXP]), ALU.mult))
                s.wait()
                s(tt(gt_[:, :, :, :], gt_[:, :, :, :], eq_[:, :, :, :], ALU.add))
                s.wait()
                s(red(rank[:, :, :], gt_[:, :, :, :], AX.X, ALU.add))
                tt(eq_[:, :, 0, :], lg[:, :, :], lmax[:, :].unsqueeze(2).broadcast_to([P, GT, EXP]), ALU.subtract)\
                    .then_inc(sem("M_lmax"), 1)
                s.end()

            def mix_gates(m, u):
                s = Steps("M_step", m * 10 + 6, 4)
                s(ts(rank[:, :, :], rank[:, :, :], float(2), None, ALU.is_lt))
                s.wait()
                dve.wait_ge(sem("M_lexp"), m + 1)
                s(tt(lexp[:, :, :], lexp[:, :, :], rank[:, :, :], ALU.mult))
                s.wait()
                s(red(gsum[:, :], lexp[:, :, :], AX.X, ALU.add))
                s.wait()
                s(dve.reciprocal(gsum[:, :], gsum[:, :]))
                s.end()
                tt(gate[u][:, :, :], lexp[:, :, :], gsum[:, :].unsqueeze(2).broadcast_to([P, GT, EXP]), ALU.mult)\
                    .then_inc(sem("M_gate"), 1)

            def mix_biases(m, u):
                dve.wait_ge(sem("M_b2"), m + 1)
                dve.tensor_copy(acc[u][:, :, :], ps_m[:, 0, :].rearrange("p (t c) -> p t c", t=GT))\
                    .then_inc(sem("M_acc"), 1)

            def mix_front(m, g, u):
                mix_stats(m, g)
                mix_norm(m, g)
                mix_ranks(m)
                mix_gates(m, u)
                mix_biases(m, u)

            def combine(m, u, e):
                dve.wait_ge(sem("M_out"), m * EXP + e + 1 + 2)
                if e:
                    dve.wait_ge(sem("M_comb"), m * EXP + e + 2)
                else:
                    dve.wait_ge(sem("M_acc"), m + 1)
                    dve.wait_ge(sem("M_gate"), m + 1)
                for t in range(GT):
                    last = stt(acc[u][:, t, :], ps_o[:, e % 2, t * P:(t + 1) * P], gate[u][:, t, e:e + 1],
                               acc[u][:, t, :], ALU.mult, ALU.add)
                last.then_inc(sem("M_comb"), 1)

            def key_stats1(g):
                dve.wait_ge(sem("M_x"), g + 1)
                hold()
                ln_stats("KN", g * 2, of_group(g), GT, st_k, mv_k)

            def key_norm1(g):
                ln_apply("KN", g * 2, of_group(g), of(y2), GT, mv_k, rstd_k)

            def key_stats2(g):
                dve.wait_ge(sem("KN_y"), g * 2 * GT + GT)
                hold()
                ln_stats("KN", g * 2 + 1, of(y2), GT, st_k, mv_k)

            def key_norm2(g):
                ln_apply("KN", g * 2 + 1, of(y2), of(y3), GT, mv_k, rstd_k)

            def rows_g(r):
                return r.unsqueeze(1).broadcast_to([P, GT, C])

            def from_bank(bank):
                return bank.rearrange("p (t c) -> p t c", c=C)

            def key_queries(g):
                dve.wait_ge(sem("K_ps"), g * 3 + 1)
                stt(group(qcur[:, bass.ds(g * GB, GB), :]), from_bank(ps_m[:, 1, :]), SC, rows_g(rows[:, R_BQ, :]),
                    ALU.mult, ALU.add).then_inc(sem("K_read"), 1)

            def key_keys(g):
                dve.wait_ge(sem("K_ps"), g * 3 + 2)
                tt(cen[:, :, :, :].rearrange("p t h d -> p t (h d)"), from_bank(ps_m[:, 1, :]), rows_g(rows[:, R_LK, :]),
                   ALU.add).then_inc(sem("K_read"), 1)
                dve.wait_ge(sem("K_read"), g * 3 + 2)
                tt(sqr[:, :, :, :], cen[:, :, :, :], cen[:, :, :, :], ALU.mult).then_inc(sem("K_step"), 1)
                dve.wait_ge(sem("K_step"), g * 2 + 1)
                hold()
                red(hvar[:, :], heads(sqr, GT), AX.X, ALU.add).then_inc(sem("K_mom"), 1)

            def key_values(g):
                dve.wait_ge(sem("K_ps"), g * 3 + 3)
                tt(group(vp_all[:, bass.ds(g * GB, GB), :]), from_bank(ps_m[:, 1, :]), rows_g(v_bias[:, :]), ALU.add)\
                    .then_inc(sem("K_read"), 1)

            def heads(buf, tiles_):
                return buf[:, 0:tiles_, :, :].rearrange("p t h d -> p (t h) d")

            def normalise_heads(done, step, g, steps, tiles_, weights, scale=None, to=nrm):
                dve.wait_ge(sem(done), g + 1)
                w = tiles_ * H
                tt(heads(sqr, tiles_), heads(cen, tiles_), hrs[:, 0:w].unsqueeze(2).broadcast_to([P, w, HD]), ALU.mult)\
                    .then_inc(sem(step), 1)
                dve.wait_ge(sem(step), g * steps + steps)
                per = weights.rearrange("p (h d) -> p h d", h=H)
                for t in range(tiles_):
                    dst = to[:, t, :, :].rearrange("p d h -> p h d")
                    if scale is None:
                        last = tt(dst, sqr[:, t, :, :], per, ALU.mult)
                    else:
                        last = stt(dst, sqr[:, t, :, :], scale, per, ALU.mult, ALU.mult)
                return last

            def key_heads(g):
                normalise_heads("K_rstd", "K_step", g, 2, GT, rows[:, R_LND, :]).then_inc(sem("K_nrm"), 1)

            def mixture(g, u, base, keys):
                m = base + g
                front = not isinstance(g, int) or g < NG - 1
                before = keys and not (isinstance(g, int) and g == 0)
                if before:
                    key_stats1(g - 1)
                if front:
                    mix_stats(m + 1, g + 1)
                if before:
                    key_norm1(g - 1)
                if front:
                    mix_norm(m + 1, g + 1)
                if before:
                    key_stats2(g - 1)
                combine(m, u, 0)
                if before:
                    key_norm2(g - 1)
                combine(m, u, 1)
                if front:
                    mix_ranks(m + 1)
                combine(m, u, 2)
                if before:
                    key_queries(g - 1)
                if front:
                    mix_gates(m + 1, 1 - u)
                combine(m, u, 3)
                if before:
                    key_keys(g - 1)
                combine(m, u, 4)
                if before:
                    key_values(g - 1)
                if front:
                    mix_biases(m + 1, 1 - u)
                combine(m, u, 5)
                combine(m, u, 6)
                if before:
                    key_heads(g - 1)
                combine(m, u, 7)
                dve.wait_ge(sem("M_comb"), m * EXP + EXP + 2)
                xg = x[:, bass.ds(g * GB, GB), :]
                stt(xg, acc[u][:, :, :].rearrange("p (b t) c -> p b (t c)", b=GB), 0.5, xg, ALU.mult, ALU.add)\
                    .then_inc(sem("M_x"), 1)

            def tiles(ap):
                return ap.rearrange("p (t c) -> p t c", t=NT)

            def row2(j):
                return rows[:, j, :].unsqueeze(1).broadcast_to([P, NT, C])

            def query_deviations(f, src):
                tt(cen[:, 0:NT, :, :].rearrange("p t h d -> p t (h d)"), tiles(src), row2(R_LQ), ALU.add)\
                    .then_inc(sem("query_step"), 1)
                dve.wait_ge(sem("query_step"), f * 3 + 1)
                tt(sqr[:, 0:NT, :, :], cen[:, 0:NT, :, :], cen[:, 0:NT, :, :], ALU.mult).then_inc(sem("query_step"), 1)
                dve.wait_ge(sem("query_step"), f * 3 + 2)
                hold()
                red(hvar[:, 0:NT * H], heads(sqr, NT), AX.X, ALU.add).then_inc(sem("query_mom"), 1)

            def focus_front(f, p, b, it):
                hold()
                dve.tensor_copy(v_st[p][:, :, :, 0:HD],
                                vp_all[:, b, :].rearrange("p (t h d) -> p t h d", t=NT, h=H))\
                    .then_inc(sem("values_ready"), 1)
                dve.tensor_copy(o_prev[:, :], qcur[:, b, :]).then_inc(sem("query_tok"), 1)
                dve.wait_ge(sem("query_ps"), f + 1)
                query_deviations(f, ps_m[:, 1, 0:T])
                normalise_heads("query_rstd", "query_step", f, 3, NT, rows[:, R_LNC, :], temps[:, Q_SC, it:it + 1])\
                    .then_inc(sem("query_nrm"), 1)

            def evacuate(n):
                for g in range(H // HG):
                    dve.wait_ge(sem("values_done"), n * (H // HG) + g + 1 + 2)
                    dve.tensor_copy(o_sb[:, g, :], ps_o[:, g % 2, (g // 2) * T:(g // 2 + 1) * T])\
                        .then_inc(sem("o_evac"), 1)

            def focus_back(n, f, b, it):
                ot = o_tok[:, :, :, :].rearrange("p t h d -> p (t h d)")
                dve.wait_ge(sem("o_t"), n + 1)
                o = ps_m[:, :, :].rearrange("p t (h w) -> p t h w", w=VW)
                s = Steps("focus_norm", f * 2, 2)
                s(dve.reciprocal(s_rec[:, :, :], o[:, :, :, HD]))
                s.wait()
                s(tt(o_tok[:, :, :, :], o[:, :, :, 0:HD], s_rec[:, :, :].unsqueeze(3).broadcast_to([P, NT, H, HD]),
                     ALU.mult))
                s.end()
                if it:
                    for t in range(NT):
                        last = ts(o_tok[:, t, :, :], o_tok[:, t, :, :], in_win[:, t:t + 1], None, ALU.mult)
                    last.then_inc(sem("windowed"), 1)
                    dve.wait_ge(sem("windowed"), (it - 1) * B + b + 1)
                if it == 0:
                    hold()
                    red(dsum[:, bass.ds(b, 1)], ot, AX.X, ALU.add, apply_absolute_value=True).then_inc(sem("d_part"), 1)
                    dve.tensor_copy(heads_out[:, b, :], ot).then_inc(sem("d_part"), 1)
                    tt(qcur[:, b, :], qcur[:, b, :], ot, ALU.add).then_inc(sem("d_part"), 1)
                    dve.wait_ge(sem("d_part"), b * 3 + 3)
                elif it == 1:
                    tt(o_prev[:, :], ot, heads_out[:, b, :], ALU.subtract).then_inc(sem("d_diff"), 1)
                    tt(qcur[:, b, :], qcur[:, b, :], ot, ALU.add).then_inc(sem("d_diff"), 1)
                    dve.wait_ge(sem("d_diff"), b * 2 + 2)
                    hold()
                    red(dsum[:, bass.ds(b, 1)], o_prev[:, :], AX.X, ALU.add, apply_absolute_value=True)\
                        .then_inc(sem("d_part"), 2)
                    dve.tensor_copy(heads_out[:, b, :], ot).then_inc(sem("d_part"), 1)
                    dve.wait_ge(sem("d_part"), (B + b) * 3 + 3)
                else:
                    ts(o_prev[:, :], heads_out[:, b, :], c1(DONE), None, ALU.mult).then_inc(sem("d_diff"), 1)
                    dve.wait_ge(sem("d_diff"), B * 2 + b + 1)
                    stt(ot, ot, c1(KEEP), o_prev[:, :], ALU.mult, ALU.add).then_inc(sem("O_o"), 1)
                    dve.wait_ge(sem("O_proj"), b + 1)
                    tt(tiles(x[:, b, :]), tiles(x[:, b, :]), tiles(ps_m[:, 1, 0:T]), ALU.add).then_inc(sem("O_x"), 1)
                    dve.wait_ge(sem("O_x"), b * 2 + 1)
                    tt(tiles(x[:, b, :]), tiles(x[:, b, :]), row2(R_BO), ALU.add).then_inc(sem("O_x"), 1)
                    dve.wait_ge(sem("O_x"), b * 2 + 2)

            def front_tokens(f):
                dve.wait_ge(sem("query_t"), f + 1 + 1)
                dve.tensor_copy(q_chan, ps_m[:, 0, 0:T]).then_inc(sem("query_tc"), 1)

            def front_deviations(f):
                dve.wait_ge(sem("query_ps"), f + 1)
                query_deviations(f, ps_m[:, 0, T:2 * T])

            def front_heads(f, it):
                normalise_heads("query_rstd", "query_step", f, 3, NT, rows[:, R_LNC, :], temps[:, Q_SC, it:it + 1],
                                q_nrm)\
                    .then_inc(sem("query_nrm"), 1)

            def front_parts(f, p):
                dve.wait_ge(sem("query_nt"), f + 1)
                dve.wait_ge(sem("fast_parts_out"), f * 16 + 16)
                hold()
                dve.tensor_copy(qk32[:, p, :], ps_m[:, 0, 0:T])
                dve.tensor_copy(parts[:, p, 0, :], ps_m[:, 0, 0:T]).then_inc(sem("fast_hi"), 1)

            def evacuate_group(n, g):
                dve.wait_ge(sem("fast_values"), (n + B) * NGV + g + 1 + 2)
                if g == 0:
                    dve.wait_ge(sem("fast_o_t"), (n + B) * NT + 2)
                hold()
                dve.tensor_copy(o_sb[:, g, :], ps_o[:, g % 2, 0:T]).then_inc(sem("fast_evac"), 1)

            def normalise(n, it, t, last_batch=False):
                if t == 0:
                    dve.wait_ge(sem("fast_q_new"), n + B if it < MAX_ITER - 1 else (MAX_ITER - 1) * B + B)
                dve.wait_ge(sem("fast_o_t"), (n + B) * NT + t + 1 + 2)
                o = BACK_BANK[t if last_batch else 0].rearrange("p (h w) -> p h w", w=VW)
                hold()
                dve.reciprocal(s_rec[:, t, :], o[:, :, HD]).then_inc(sem("focus_norm"), 1)
                dve.wait_ge(sem("focus_norm"), n * NT + t + 1)
                if it:
                    ts(s_rec[:, t, :], s_rec[:, t, :], in_win[:, t:t + 1], None, ALU.mult)\
                        .then_inc(sem("windowed"), 1)
                    dve.wait_ge(sem("windowed"), (n - B) * NT + t + 1)
                tt(o_tok[:, t, :, :], o[:, :, 0:HD], s_rec[:, t, :].unsqueeze(2).broadcast_to([P, H, HD]), ALU.mult)\
                    .then_inc(sem("fast_o_read"), 1)

            def change(n, b, it):
                ot = o_tok[:, :, :, :].rearrange("p t h d -> p (t h d)")
                dve.wait_ge(sem("fast_o_read"), (n + B) * NT + NT + 1)
                hold()
                if it == 0:
                    red(dsum[:, bass.ds(b, 1)], ot, AX.X, ALU.add, apply_absolute_value=True)\
                        .then_inc(sem("d_part"), 1)
                elif it == 1:
                    tt(o_prev[:, :], ot, heads_out[:, b, :], ALU.subtract).then_inc(sem("d_diff"), 1)
                    dve.wait_ge(sem("d_diff"), b + 1)
                    hold()
                    red(dsum[:, bass.ds(b, 1)], o_prev[:, :], AX.X, ALU.add, apply_absolute_value=True)\
                        .then_inc(sem("d_part"), 1)
                else:
                    ts(o_prev[:, :], heads_out[:, b, :], c1(DONE), None, ALU.mult).then_inc(sem("d_diff"), 1)
                    dve.wait_ge(sem("d_diff"), B + b + 1)
                    stt(ot, ot, c1(KEEP), o_prev[:, :], ALU.mult, ALU.add).then_inc(sem("O_o"), 1)

            def back_out(b):
                dve.wait_ge(sem("O_ott"), b + 1)
                dve.tensor_copy(o_t[:, :], ps_m[:, 1, 0:T]).then_inc(sem("O_otc"), 1)

            def back_project(b):
                dve.wait_ge(sem("O_proj"), b + 1)
                dve.wait_ge(sem("fast_bias"), b + 1)
                tt(tiles(x[:, b, :]), tiles(x[:, b, :]), tiles(ps_m[:, 1, T:2 * T]), ALU.add).then_inc(sem("O_x"), 1)

            def fast_focus():
                dve.sem_inc(sem("fast_hi"), 1)
                dve.sem_inc(sem("O_x"), 1)
                front_tokens(0)
                key_stats1(NG - 1)
                front_deviations(0)
                key_norm1(NG - 1)
                front_heads(0, 0)
                key_stats2(NG - 1)
                dve.wait_ge(sem("K_out"), NG * 16 * GB)
                front_parts(0, 0)
                front_tokens(1)
                key_norm2(NG - 1)
                front_deviations(1)
                front_heads(1, 0)
                key_queries(NG - 1)
                front_parts(1, 1)
                key_keys(NG - 1)
                key_values(NG - 1)
                key_heads(NG - 1)
                for it in range(MAX_ITER):
                    final = it == MAX_ITER - 1

                    def body(n, b, p, half):
                        first = isinstance(b, int) and b == 0
                        ahead = follow(n, b, 2)
                        if ahead:
                            front_tokens(ahead[0])
                        if not first:
                            evacuate_group(n - 1, NGV - 1)
                        if ahead:
                            front_deviations(ahead[0])
                        if not first:
                            normalise(n - 1, it, 0)
                        evacuate_group(n, 0)
                        if not first:
                            normalise(n - 1, it, 1)
                        if ahead:
                            later = isinstance(b, int) and b + 2 >= B
                            front_heads(ahead[0], it + 1 if later else it)
                        if not first:
                            change(n - 1, b - 1, it)
                        evacuate_group(n, 1)
                        if not first and final:
                            back_out(b - 1)
                        if first and it == 0:
                            dve.wait_ge(sem("K_out"), (NG + 1) * 16 * GB)
                        if ahead:
                            front_parts(ahead[0], p)
                        if not first and final:
                            back_project(b - 1)
                        evacuate_group(n, 2)
                        if isinstance(b, int) and b == B - 2 and not final:
                            width_steps()

                    fast_steps(dve, it, body)
                    n = it * B + B - 1
                    evacuate_group(n, NGV - 1)
                    for t in range(NT):
                        normalise(n, it, t, True)
                    change(n, B - 1, it)
                    if final:
                        back_out(B - 1)
                        back_project(B - 1)
                        dve.wait_ge(sem("O_x"), B + 1)
                    else:
                        dve.wait_ge(sem("d_part"), n + 1)
                        control(it, 1)

            def general_focus():
                link(dve.memset(ml[:, :, 1, :], 0.0))
                key_stats1(NG - 1)
                key_norm1(NG - 1)
                key_stats2(NG - 1)
                key_norm2(NG - 1)
                key_queries(NG - 1)
                key_keys(NG - 1)
                key_values(NG - 1)
                key_heads(NG - 1)
                dve.wait_ge(sem("K_out"), (NG + 1) * 16 * GB)
                base = general_base(dve)
                for it in range(MAX_ITER):
                    with dve.Fori(0, B // 2) as i:
                        for p in range(2):
                            b = i * 2 + p
                            n = base + it * B + b
                            focus_front(it * B + b, p, b, it)
                            maxima(n, False)
                            evacuate(n)
                            focus_back(n, it * B + b, b, it)
                    if it < MAX_ITER - 1:
                        width_steps()
                        control(it, 0)

            step_at = [0]

            def link(ins):
                ins.then_inc(sem("control"), 1)
                step_at[0] += 1
                dve.wait_ge(sem("control"), step_at[0])

            def temperatures():
                link(dve.tensor_copy(temps[:, TEMP, 0:1], col(TMP)))
                for j in range(1, MAX_ITER):
                    link(ts(temps[:, TEMP, j:j + 1], temps[:, TEMP, j - 1:j], 0.005, None, ALU.add))
                link(ts(temps[:, T_POS, :], temps[:, TEMP, :], 0.0, None, ALU.is_gt))
                link(tt(temps[:, T_SAFE, :], temps[:, TEMP, :], temps[:, T_POS, :], ALU.mult))
                link(ts(temps[:, T_POS, :], temps[:, T_POS, :], -1.0, 1.0, ALU.mult, ALU.add))
                link(tt(temps[:, T_SAFE, :], temps[:, T_SAFE, :], temps[:, T_POS, :], ALU.add))
                dve.nop().then_inc(sem("setup_vector"), 1)
                dve.wait_ge(sem("setup_scalar"), 7)
                link(ts(temps[:, Q_SC, :], temps[:, Q_SC, :], INV_SQRT, None, ALU.mult))
                link(red(c1(T0), temps[:, Q_SC, :], AX.X, ALU.max))
                link(tt(o_prev[:, 0:C], rows[:, R_LNC, :], rows[:, R_LND, :], ALU.mult))
                link(red(c1(T1), o_prev[:, 0:C], AX.X, ALU.max, apply_absolute_value=True))
                link(ts(c1(BND), c1(T0), c1(T1), float(HD), ALU.mult, ALU.mult))
                link(ts(c1(BND), c1(BND), SAFE, None, ALU.is_le))
                link(dve.tensor_copy(path[:, :], c1(BND)))
                dve.nop().then_inc(sem("path_ready"), 1)

            def floor(dst, scale):
                link(ts(c1(T0), c1(CW), float(np.float32(scale)), None, ALU.mult))
                link(dve.tensor_copy(ctl_i[:, 0:1], c1(T0)))
                link(dve.tensor_copy(c1(dst), ctl_i[:, 0:1]))
                link(tt(c1(T1), c1(dst), c1(T0), ALU.is_gt))
                link(tt(c1(dst), c1(dst), c1(T1), ALU.subtract))

            def width_steps():
                floor(UP, UP_WIN)
                floor(DN, DOWN_WIN)
                link(tt(c1(UP), c1(UP), c1(CW), ALU.subtract))
                link(tt(c1(DN), c1(DN), c1(CW), ALU.subtract))
                link(ts(c1(T0), c1(CW), float(MIN_SIZE), None, ALU.is_gt))
                link(tt(c1(DN), c1(DN), c1(T0), ALU.mult))

            def control(it, bank):
                link(red(dtot[:, :], dsum[:, :], AX.X, ALU.add))
                dve.nop().then_inc(sem("d_total"), 1)
                dve.wait_ge(sem("d_sum"), it + 1)
                link(ts(c1(DIFF), ps_m[:, bank, 0:1], 1.0 / (B * T * C), None, ALU.mult))
                link(ts(c1(GUP), c1(DIFF), UP_DIFF, None, ALU.is_gt))
                link(ts(c1(GDN), c1(DIFF), DOWN_DIFF, None, ALU.is_lt))
                link(ts(c1(NW), c1(UP), c1(GUP), c1(CW), ALU.mult, ALU.add))
                link(ts(c1(NW), c1(DN), c1(GDN), c1(NW), ALU.mult, ALU.add))
                link(ts(c1(CW), c1(NW), float(MIN_SIZE), float(T), ALU.max, ALU.min))
                link(ts(win_row[:, :], pos_row[:, :], c1(CW), MASKED, ALU.is_ge, ALU.mult))
                dve.nop().then_inc(sem("window_ready"), 1)
                link(ts(in_win[:, :], pos_col[:, :], c1(CW), None, ALU.is_lt))
                if it:
                    link(ts(c1(LIM), c1(DIFF), col(FAC), col(THR), ALU.mult, ALU.add))
                    link(tt(c1(DONE), c1(DIFF), c1(LIM), ALU.is_lt))
                    link(ts(c1(KEEP), c1(DONE), -1.0, 1.0, ALU.mult, ALU.add))

            dve.sem_inc(sem("max_done"), 2)
            dve.sem_inc(sem("clamp_done"), 2)
            dve.sem_inc(sem("K_hi"), 1)
            dve.sem_inc(sem("M_comb"), 2)
            dve.sem_inc(sem("o_evac"), 2)
            dve.wait_ge(sem("consts"), FIRST_CONSTS)
            dve.wait_ge(sem("loaded"), lots[0])
            front_norm(0)
            ln_apply("T", norm1(0), of_x(0), of(y), NT, mv, rstd)
            mix_inputs(mix1(0))
            front_norm(1)
            dve.wait_ge(sem("T_yt"), norm1(0) + 1)
            ln_apply("T", norm1(1), of_x(1), of(y), NT, mv, rstd)
            mix_gated(mix1(0), 2)
            dve.wait_ge(sem("consts"), CONSTS)
            dve.wait_ge(sem("loaded"), lots[1])
            for j in range(3):
                link(tt(e_buf[0][:, j, 0:P].rearrange("p (h d) -> p h d", h=H), block_mask[:, :, :],
                        head_w[:, j, :].unsqueeze(1).broadcast_to([P, H, HD]), ALU.mult))
            dve.nop().then_inc(sem("setup_vector"), 1)
            for f in range(2):
                mix_inputs(mix1(f + 1))
                middle_norm(f)
                middle_normed(f, norm1(f + 1))
                if f == 0:
                    dve.wait_ge(sem("setup_tensor"), 5)
                    for j in range(3):
                        link(ts(block_w[:, j, :], ps_k[:, 0, j * P:(j + 1) * P], SC if j == 1 else 1.0, None, ALU.mult))
                    for row in (block_w[:, 0, :], block_w[:, 1, :], rows[:, R_LQ, :], rows[:, R_LK, :]):
                        per = row.rearrange("p (h d) -> p h d", h=H)
                        link(red(hvar[:, 0:H], per, AX.X, ALU.add))
                        link(stt(per, hvar[:, 0:H].unsqueeze(2).broadcast_to([P, H, HD]), -1.0 / HD, per, ALU.mult, ALU.add))
                    link(ts(rows[:, R_BQ, :], rows[:, R_BQ, :], SC, None, ALU.mult))
                    link(ts(bv_rep[:, :], ones[:, :], col(BV), None, ALU.mult))
                    dve.nop().then_inc(sem("setup_vector"), 1)
                front_norm(f + 2)
                front_normed(f + 2)
                mix_gated(mix1(f + 1), 2)
                longest(f)
                if f == 0:
                    dve.wait_ge(sem("setup_tensor"), 7)
                    link(tt(v_bias[:, :], ps_q[:, 1, 0:P], rows[:, R_LV, :], ALU.add))
                    link(dve.memset(c1(CW), float(max(min(T, 256), MIN_SIZE))))
                    temperatures()
            link(ts(low_behind[:, :], pos_col[:, :], -LOW, LOW * (T - 1), ALU.mult, ALU.add))
            dve.sem_inc(sem("row_max"), 1)
            dve.sem_inc(sem("fast_o_t"), 2)
            dve.sem_inc(sem("fast_o_read"), 1)
            causal_steps(dve, causal_round)
            back_normed(B - 2)
            mix_inputs(mix2(B - 2))
            causal_sums(B - 1, 0)
            causal_sums(B - 1, 1)
            causal_normalise(B - 1)
            mix_gated(mix2(B - 2), 1)
            causal_add(B - 1)
            back_norm(B - 1)
            back_normed(B - 1)
            mix_inputs(mix2(B - 1))
            mix_gated(mix2(B - 1), 1)
            link(red(safe[:, 1:2], top[:, :], AX.X, ALU.max))
            link(ts(safe[:, 0:1], safe[:, 1:2], MAX_SAFE, None, ALU.is_le))
            link(tt(corr2[:, :, :].rearrange("p h d -> p (h d)"), w_t[:, W_V0, :], w_t[:, W_V0, :], ALU.mult))
            link(red(safe[:, 2:3], corr2[:, :, :].rearrange("p h d -> p (h d)"), AX.X, ALU.add))
            link(ts(safe[:, 3:4], safe[:, 2:3], V_SAFE, None, ALU.is_le))
            link(tt(safe[:, 0:1], safe[:, 0:1], safe[:, 3:4], ALU.mult))
            link(tt(qk_bound[:, :], qk_max[:, :, 0], qk_max[:, :, 1], ALU.mult))
            link(red(safe[0:H, 1:2], qk_bound[:, :], AX.X, ALU.max))
            link(ts(safe[0:H, 2:3], safe[0:H, 1:2], CLIP_SAFE * CLIP_SAFE, None, ALU.is_le))
            link(tt(safe[0:H, 0:1], safe[0:H, 0:1], safe[0:H, 2:3], ALU.mult))
            dve.nop().then_inc(sem("setup_vector"), 1)
            dve.wait_ge(sem("setup_tensor"), 8)
            link(ts(c1(T0), ps_m[:, 0, 0:1], float(P) - 0.5, None, ALU.is_lt))
            link(dve.tensor_copy(redo[:, :], c1(T0)))
            dve.nop().then_inc(sem("setup_vector"), 1)
            dve.wait_ge(sem("F_x"), MIXES + 1)

            def general_causal():
                dve.wait_ge(sem("loaded"), n_loads + 16)
                with dve.Fori(0, B // 2) as i:
                    for p in range(2):
                        n = i * 2 + p
                        ffn(n * 2 + MIXES, n * 3 + NORMS, n)
                        causal_front(n, n * 3 + 1 + NORMS, p, n)
                        maxima(n, True)
                        clamps(n)
                        causal_back(n, n)
                        ffn(n * 2 + 1 + MIXES, n * 3 + 2 + NORMS, n)

            redo_causal(dve, general_causal)
            mix_front(0, 0, 0)
            mixture_groups(dve, lambda g, u: mixture(g, u, 0, True))
            links = step_at[0]

            def fast():
                step_at[0] = links
                fast_focus()

            def general():
                step_at[0] = links
                general_focus()

            any_path(dve, fast, general)
            mix_front(NG, 0, 0)
            mixture_groups(dve, lambda g, u: mixture(g, u, NG, False))



_INS = ['L0_attn_x', 'L0_attn_w_qkv', 'L0_attn_w_proj', 'L0_ffn_W_r', 'L0_ffn_W_k', 'L0_ffn_W_v', 'L0_ffn_mu_r',
        'L0_ffn_mu_k', 'L1_attn_Wq', 'L1_attn_bq', 'L1_attn_Wk', 'L1_attn_Wv', 'L1_attn_bv', 'L1_attn_Wo',
        'L1_attn_bo', 'L1_attn_lna_w', 'L1_attn_lnb_w', 'L1_attn_lnc_w', 'L1_attn_lnd_w', 'L1_attn_lq_w',
        'L1_attn_lq_b', 'L1_attn_lk_w', 'L1_attn_lk_b', 'L1_attn_lv_w', 'L1_attn_lv_b', 'L1_attn_threshold',
        'L1_attn_temp_base', 'L1_attn_factor', 'L1_ffn_Wr', 'L1_ffn_br', 'L1_ffn_W1', 'L1_ffn_b1', 'L1_ffn_W2',
        'L1_ffn_b2']


def kernel(**inputs):
    import concourse.bacc as _bacc
    from concourse.bass_utils import run_bass_kernel_spmd as _run

    nc = _bacc.Bacc("TRN2", target_bir_lowering=False, num_devices=1)
    arrays, args = {}, {}
    for name in _INS:
        v = np.ascontiguousarray(inputs[name])
        arrays[f"in_{name}_dram"] = v
        args[name] = nc.dram_tensor(f"in_{name}_dram", v.shape, mybir.dt.from_np(v.dtype), kind="ExternalInput").ap()
    out = nc.dram_tensor("out_0_dram", (B, T, C), F32, kind="ExternalOutput").ap()
    macaron_kernel(nc, args, out)
    r = _run(nc, [arrays], core_ids=[0])
    return r.results[0]["out_0_dram"]
```
